# Optimizing a Trainium2 kernel written in Bass

```python
import numpy as np
import jax
import jax.numpy as jnp

def _softmax(x, axis=-1):
    return jax.nn.softmax(x, axis=axis)

def _gelu(x):
    return jax.nn.gelu(x, approximate=True)

def _silu(x):
    return jax.nn.silu(x)

def _sigmoid(x):
    return jax.nn.sigmoid(x)

def _layernorm(x, axis=-1, eps=1e-05):
    m = jnp.mean(x, axis=axis, keepdims=True)
    v = jnp.var(x, axis=axis, keepdims=True)
    return (x - m) / jnp.sqrt(v + eps)

def _scatter_add(tgt, idx, src, axis=0):
    return tgt.at[idx].add(src)

def _segment_sum(src, seg, n):
    return jax.ops.segment_sum(src, seg, n)
kernel_name = 'mk_gnn_ffn_d4_gnn_r32_631617'

def setup_inputs(seed: int=0):
    np.random.seed(seed)
    _w = jnp.asarray

    def _rec_inputs():
        import jax
        import jax.numpy as jnp
        _gk = jax.random.key(seed)
        x = -8.776e-05 + 1 * jax.random.normal(jax.random.fold_in(_gk, 1), (3125, 256), jnp.float32)
        _s = jax.random.randint(jax.random.fold_in(_gk, 2), (25000,), 0, 3125, jnp.int32)
        _d = jax.random.randint(jax.random.fold_in(_gk, 3), (25000,), 0, 3125, jnp.int32)
        _loop = jnp.arange(3125, dtype=jnp.int32)
        src = jnp.concatenate([_s, _d, _loop])
        dst = jnp.concatenate([_d, _s, _loop])
        _o = jnp.argsort(dst, stable=True)
        src = src[_o]
        dst = dst[_o]
        edge_type_8 = jax.random.randint(jax.random.fold_in(_gk, 13), (53125,), 0, 8, jnp.int32)
        edge_weight = jax.random.uniform(jax.random.fold_in(_gk, 14), (53125,), jnp.float32, 0.0, 0.999998)
        node_type_4 = jax.random.randint(jax.random.fold_in(_gk, 15), (3125,), 0, 4, jnp.int32)
        return (x, src, dst, edge_type_8, edge_weight, node_type_4)
    x, src, dst, edge_type_8, edge_weight, node_type_4 = _rec_inputs()

    def _L0_gnn_setup():
        import jax, jax.numpy as jnp
        import numpy as np
        N_NODES = 625
        N_EDGES = 10000
        IN_DIM = 256
        OUT_DIM = 256
        N_HEADS = 4
        D_K = OUT_DIM // N_HEADS
        N_NTYPES = 4
        N_RELS = 8
        SQRT_DK = float(np.sqrt(D_K))

        def _typed_matmul(x, W, node_type):
            all_t = jnp.einsum('ni,tio->tno', x, W)
            return all_t[node_type, jnp.arange(x.shape[0])]
        key = jax.random.key(seed)
        ks = jax.random.split(key, 12)
        xav = lambda k, shape, fan: jax.random.normal(k, shape, jnp.float32) * (1.0 / np.sqrt(fan))
        return {'h': jax.random.normal(ks[0], (N_NODES, IN_DIM), jnp.float32), 'k_linears': xav(ks[1], (N_NTYPES, IN_DIM, OUT_DIM), IN_DIM), 'q_linears': xav(ks[2], (N_NTYPES, IN_DIM, OUT_DIM), IN_DIM), 'v_linears': xav(ks[3], (N_NTYPES, IN_DIM, OUT_DIM), IN_DIM), 'a_linears': xav(ks[4], (N_NTYPES, OUT_DIM, OUT_DIM), OUT_DIM), 'relation_att': xav(ks[5], (N_RELS, N_HEADS, D_K, D_K), D_K), 'relation_msg': xav(ks[6], (N_RELS, N_HEADS, D_K, D_K), D_K), 'relation_pri': jnp.ones((N_RELS, N_HEADS), jnp.float32), 'skip': jnp.ones((N_NTYPES,), jnp.float32), 'node_type': jax.random.randint(ks[7], (N_NODES,), 0, N_NTYPES), 'etype': jnp.sort(jax.random.randint(ks[8], (N_EDGES,), 0, N_RELS)), 'row_idx': jax.random.randint(ks[9], (N_EDGES,), 0, N_NODES), 'col_idx': jax.random.randint(ks[10], (N_EDGES,), 0, N_NODES)}
    _L0_gnn_all = _L0_gnn_setup()
    _L0_gnn_in = {k: v for k, v in _L0_gnn_all.items() if k in ('k_linears', 'q_linears', 'v_linears', 'a_linears', 'relation_att', 'relation_msg', 'relation_pri', 'skip')}
    del _L0_gnn_all

    def _L0_ffn_setup():
        import jax, jax.numpy as jnp
        import numpy as np
        NUM_EXPERTS = 8
        TOP_K = 2
        B, S, D = (8, 256, 256)

        def _moe(tokens, router_w, w1, b1, w2, b2):
            N = tokens.shape[0]
            E = router_w.shape[0]
            logits = tokens.astype(jnp.float32) @ router_w.astype(jnp.float32).T
            probs = jax.nn.softmax(logits, axis=-1)
            rw, re = jax.lax.top_k(probs, TOP_K)
            if TOP_K > 1:
                rw = rw / jnp.maximum(rw.sum(-1, keepdims=True), 1e-12)
            rw = rw.astype(tokens.dtype)
            combine = jnp.zeros((N, E), tokens.dtype).at[jnp.arange(N)[:, None], re].set(rw)
            out = tokens
            for e in range(E):
                h = jax.nn.gelu(tokens @ w1[e] + b1[e], approximate=False)
                y = h @ w2[e] + b2[e]
                out = out + combine[:, e:e + 1] * y
            return out
        key = jax.random.key(seed)
        ks = jax.random.split(key, 4)
        scale = 1.0 / np.sqrt(D).astype(np.float32)
        return {'input_embeddings': jax.random.normal(ks[0], (B, S, D), jnp.float32), 'router_w': jax.random.normal(ks[1], (NUM_EXPERTS, D), jnp.float32) * scale, 'w1': jax.random.normal(ks[2], (NUM_EXPERTS, D, D), jnp.float32) * scale, 'b1': jnp.zeros((NUM_EXPERTS, D), jnp.float32), 'w2': jax.random.normal(ks[3], (NUM_EXPERTS, D, D), jnp.float32) * scale, 'b2': jnp.zeros((NUM_EXPERTS, D), jnp.float32)}
    _L0_ffn_all = _L0_ffn_setup()
    _L0_ffn_in = {k: v for k, v in _L0_ffn_all.items() if k in ('router_w', 'w1', 'b1', 'w2', 'b2')}
    del _L0_ffn_all

    def _L1_gnn_setup():
        import jax, jax.numpy as jnp
        import numpy as np
        N_NODES = 50000
        key = jax.random.key(seed)
        k1, k2, k3 = jax.random.split(key, 3)
        x = jax.random.normal(k1, (N_NODES, 256), dtype=jnp.float32)
        W = jax.random.normal(k2, (256, 256), dtype=jnp.float32) * (1.0 / np.sqrt(256))
        edge_index = jax.random.randint(k3, (2, 50000), 0, N_NODES, dtype=jnp.int64)
        return {'x': x, 'W': W, 'edge_index': edge_index}
    _L1_gnn_all = _L1_gnn_setup()
    _L1_gnn_in = {k: v for k, v in _L1_gnn_all.items() if k in ('W',)}
    del _L1_gnn_all

    def _L1_ffn_setup():
        import jax, jax.numpy as jnp
        import numpy as np
        DIM = 256
        H = 8
        D = 64
        G = 64
        INNER = H * D
        SCALE = D ** (-0.5)
        key = jax.random.key(seed)
        ks = jax.random.split(key, 12)
        B, N = (4, 512)
        x = jax.random.normal(ks[0], (B, N, DIM), dtype=jnp.float32)
        s = lambda fan_in: 1.0 / np.sqrt(fan_in)
        W_fx = jax.random.normal(ks[1], (DIM, INNER), dtype=jnp.float32) * s(DIM)
        b_fx = jnp.zeros((INNER,), dtype=jnp.float32)
        W_x = jax.random.normal(ks[2], (DIM, INNER), dtype=jnp.float32) * s(DIM)
        b_x = jnp.zeros((INNER,), dtype=jnp.float32)
        A = jax.random.normal(ks[3], (G, D), dtype=jnp.float32)
        Q, _ = jnp.linalg.qr(A.T)
        W_slice = Q[:, :G].astype(jnp.float32)
        b_slice = jnp.zeros((G,), dtype=jnp.float32)
        W_q = jax.random.normal(ks[4], (D, D), dtype=jnp.float32) * s(D)
        W_k = jax.random.normal(ks[5], (D, D), dtype=jnp.float32) * s(D)
        W_v = jax.random.normal(ks[6], (D, D), dtype=jnp.float32) * s(D)
        W_out = jax.random.normal(ks[7], (INNER, DIM), dtype=jnp.float32) * s(INNER)
        b_out = jnp.zeros((DIM,), dtype=jnp.float32)
        temperature = jnp.ones((1, H, 1, 1), dtype=jnp.float32) * 0.5
        return {'x': x, 'W_fx': W_fx, 'b_fx': b_fx, 'W_x': W_x, 'b_x': b_x, 'W_slice': W_slice, 'b_slice': b_slice, 'W_q': W_q, 'W_k': W_k, 'W_v': W_v, 'W_out': W_out, 'b_out': b_out, 'temperature': temperature}
    _L1_ffn_all = _L1_ffn_setup()
    _L1_ffn_in = {k: v for k, v in _L1_ffn_all.items() if k in ('W_fx', 'b_fx', 'W_x', 'b_x', 'W_slice', 'b_slice', 'W_q', 'W_k', 'W_v', 'W_out', 'b_out', 'temperature')}
    del _L1_ffn_all

    def _L2_gnn_setup():
        import jax, jax.numpy as jnp
        import numpy as np
        EPS = 0.1
        key = jax.random.key(seed)
        k1, k2, k3, k4 = jax.random.split(key, 4)
        N, E, Din, Dout = (10000, 10000, 256, 256)
        x = jax.random.normal(k1, (N, Din), dtype=jnp.float32)
        edge_index = jax.random.randint(k2, (2, E), 0, N, dtype=jnp.int32)
        edge_weight = jax.random.uniform(k3, (E,), dtype=jnp.float32)
        limit = np.sqrt(6.0 / (Din + Dout)).astype(np.float32)
        W = jax.random.uniform(k4, (Dout, Din), dtype=jnp.float32, minval=-limit, maxval=limit)
        b = jnp.zeros((Dout,), dtype=jnp.float32)
        return {'x': x, 'edge_index': edge_index, 'edge_weight': edge_weight, 'num_nodes': N, 'W': W, 'b': b}
    _L2_gnn_all = _L2_gnn_setup()
    _L2_gnn_in = {k: v for k, v in _L2_gnn_all.items() if k in ('W', 'b')}
    del _L2_gnn_all

    def _L2_ffn_setup():
        import jax, jax.numpy as jnp
        import numpy as np
        B, N, D = (16, 128, 256)
        NUM_EXPERTS, TOP_K, HEADS = (4, 2, 4)
        N_EDGES = 32768
        LN_EPS = 1e-05

        def _layernorm(x, g, b):
            mu = x.mean(-1, keepdims=True)
            var = ((x - mu) ** 2).mean(-1, keepdims=True)
            return (x - mu) * jax.lax.rsqrt(var + LN_EPS) * g + b

        def _forward(x, edge_index, W_gat, att_src, att_dst, b_gat, ln_gamma, ln_beta, W1, b1, W2, b2):
            Bc, Nc, Dc = x.shape
            M = Bc * Nc
            x_flat = x.reshape(M, Dc)
            h = (x_flat @ W_gat).reshape(M, HEADS, NUM_EXPERTS)
            loops = jnp.arange(M, dtype=edge_index.dtype)
            src = jnp.concatenate([edge_index[0], loops])
            dst = jnp.concatenate([edge_index[1], loops])
            a_src = (h * att_src).sum(-1)
            a_dst = (h * att_dst).sum(-1)
            e = jax.nn.leaky_relu(a_src[src] + a_dst[dst], negative_slope=0.2)
            e_max = jax.ops.segment_max(e, dst, num_segments=M)
            ee = jnp.exp(e - e_max[dst])
            denom = jax.ops.segment_sum(ee, dst, num_segments=M)
            alpha = ee / (denom[dst] + 1e-16)
            msg = h[src] * alpha[:, :, None]
            agg = jax.ops.segment_sum(msg, dst, num_segments=M).reshape(M, HEADS * NUM_EXPERTS) + b_gat
            scores = _layernorm(agg, ln_gamma, ln_beta).reshape(M, HEADS, NUM_EXPERTS).mean(1)
            scores = scores.reshape(Bc, Nc, NUM_EXPERTS)
            topk_s, topk_i = jax.lax.top_k(scores, TOP_K)
            w = jax.nn.softmax(topk_s, axis=-1)
            out = jnp.zeros_like(x)
            for ei in range(NUM_EXPERTS):
                g = jnp.where(topk_i == ei, w, 0.0).sum(-1)
                hh = jax.nn.gelu(x @ W1[ei] + b1[ei], approximate=False)
                out = out + g[..., None] * (hh @ W2[ei] + b2[ei])
            return out
        key = jax.random.key(seed)
        ks = jax.random.split(key, 8)
        s = 0.05
        return {'x': jax.random.normal(ks[0], (B, N, D), jnp.float32), 'W_gat': jax.random.normal(ks[1], (D, HEADS * NUM_EXPERTS), jnp.float32) * s, 'att_src': jax.random.normal(ks[2], (HEADS, NUM_EXPERTS), jnp.float32) * s, 'att_dst': jax.random.normal(ks[3], (HEADS, NUM_EXPERTS), jnp.float32) * s, 'b_gat': jnp.zeros((HEADS * NUM_EXPERTS,), jnp.float32), 'ln_gamma': jnp.ones((HEADS * NUM_EXPERTS,), jnp.float32), 'ln_beta': jnp.zeros((HEADS * NUM_EXPERTS,), jnp.float32), 'W1': jax.random.normal(ks[4], (NUM_EXPERTS, D, 2 * D), jnp.float32) * s, 'b1': jnp.zeros((NUM_EXPERTS, 2 * D), jnp.float32), 'W2': jax.random.normal(ks[5], (NUM_EXPERTS, 2 * D, D), jnp.float32) * s, 'b2': jnp.zeros((NUM_EXPERTS, D), jnp.float32), 'edge_index': jax.random.randint(ks[6], (2, N_EDGES), 0, B * N, jnp.int32)}
    _L2_ffn_all = _L2_ffn_setup()
    _L2_ffn_in = {k: v for k, v in _L2_ffn_all.items() if k in ('W_gat', 'att_src', 'att_dst', 'b_gat', 'ln_gamma', 'ln_beta', 'W1', 'b1', 'W2', 'b2', 'edge_index')}
    del _L2_ffn_all

    def _L3_gnn_setup():
        import jax, jax.numpy as jnp
        import numpy as np
        N_NODES = 50000
        N_EDGES = 25000
        IN_FEATS = 256
        HID = 64
        HEADS = 4
        OUT = 64

        def _gat_layer(x, src, dst, W, a_s, a_d, b, num_nodes):
            H, F = a_s.shape
            h = (x @ W).reshape(num_nodes, H, F)
            al_s = jnp.einsum('nhf,hf->nh', h, a_s)
            al_d = jnp.einsum('nhf,hf->nh', h, a_d)
            e = jax.nn.leaky_relu(al_s[src] + al_d[dst], 0.2)
            emax = jax.ops.segment_max(e, dst, num_segments=num_nodes)
            emax = jnp.where(jnp.isfinite(emax), emax, 0.0)
            ee = jnp.exp(e - emax[dst])
            denom = jax.ops.segment_sum(ee, dst, num_segments=num_nodes)
            alpha = ee / (denom[dst] + 1e-16)
            out = jax.ops.segment_sum(alpha[:, :, None] * h[src], dst, num_segments=num_nodes)
            return out.reshape(num_nodes, H * F) + b
        key = jax.random.key(seed)
        ks = jax.random.split(key, 16)
        p = lambda k, shape: jax.random.normal(k, shape, dtype=jnp.float32) * 0.05
        return {'x': jax.random.normal(ks[0], (N_NODES, IN_FEATS), dtype=jnp.float32), 'edge_index': jax.random.randint(ks[1], (2, N_EDGES), 0, N_NODES), 'W0': p(ks[2], (IN_FEATS, HEADS * HID)), 'as0': p(ks[3], (HEADS, HID)), 'ad0': p(ks[4], (HEADS, HID)), 'b0': jnp.zeros((HEADS * HID,), jnp.float32), 'W1': p(ks[5], (HEADS * HID, HEADS * HID)), 'as1': p(ks[6], (HEADS, HID)), 'ad1': p(ks[7], (HEADS, HID)), 'b1': jnp.zeros((HEADS * HID,), jnp.float32), 'W2': p(ks[8], (HEADS * HID, HEADS * OUT)), 'as2': p(ks[9], (HEADS, OUT)), 'ad2': p(ks[10], (HEADS, OUT)), 'b2': jnp.zeros((HEADS * OUT,), jnp.float32)}
    _L3_gnn_all = _L3_gnn_setup()
    _L3_gnn_in = {k: v for k, v in _L3_gnn_all.items() if k in ('W0', 'as0', 'ad0', 'b0', 'W1', 'as1', 'ad1', 'b1', 'W2', 'as2', 'ad2', 'b2')}
    del _L3_gnn_all

    def _L3_ffn_setup():
        import jax, jax.numpy as jnp
        import numpy as np
        E = 8
        K = 2
        D = 256
        H = 512
        DOUT = 256
        EPS = 1e-05
        key = jax.random.key(seed)
        ks = jax.random.split(key, 9)
        s = 0.02
        return {'x': jax.random.normal(ks[0], (4, 256, D), jnp.float32), 'gamma': 1.0 + 0.05 * jax.random.normal(ks[1], (D,), jnp.float32), 'beta': 0.05 * jax.random.normal(ks[2], (D,), jnp.float32), 'Wr': 0.01 * jax.random.normal(ks[3], (D, E), jnp.float32), 'br': jnp.zeros((E,), jnp.float32), 'W1': s * jax.random.normal(ks[4], (E, D, H), jnp.float32), 'b1': s * jax.random.normal(ks[5], (E, H), jnp.float32), 'W2': s * jax.random.normal(ks[6], (E, H, DOUT), jnp.float32), 'b2': s * jax.random.normal(ks[7], (E, DOUT), jnp.float32)}
    _L3_ffn_all = _L3_ffn_setup()
    _L3_ffn_in = {k: v for k, v in _L3_ffn_all.items() if k in ('gamma', 'beta', 'Wr', 'br', 'W1', 'b1', 'W2', 'b2')}
    del _L3_ffn_all
    return {'x': x, 'src': src, 'dst': dst, 'edge_type_8': edge_type_8, 'edge_weight': edge_weight, 'node_type_4': node_type_4, 'L0_gnn_k_linears': _L0_gnn_in['k_linears'], 'L0_gnn_q_linears': _L0_gnn_in['q_linears'], 'L0_gnn_v_linears': _L0_gnn_in['v_linears'], 'L0_gnn_a_linears': _L0_gnn_in['a_linears'], 'L0_gnn_relation_att': _L0_gnn_in['relation_att'], 'L0_gnn_relation_msg': _L0_gnn_in['relation_msg'], 'L0_gnn_relation_pri': _L0_gnn_in['relation_pri'], 'L0_gnn_skip': _L0_gnn_in['skip'], 'L0_ffn_router_w': _L0_ffn_in['router_w'], 'L0_ffn_w1': _L0_ffn_in['w1'], 'L0_ffn_b1': _L0_ffn_in['b1'], 'L0_ffn_w2': _L0_ffn_in['w2'], 'L0_ffn_b2': _L0_ffn_in['b2'], 'L1_gnn_W': _L1_gnn_in['W'], 'L1_ffn_W_fx': _L1_ffn_in['W_fx'], 'L1_ffn_b_fx': _L1_ffn_in['b_fx'], 'L1_ffn_W_x': _L1_ffn_in['W_x'], 'L1_ffn_b_x': _L1_ffn_in['b_x'], 'L1_ffn_W_slice': _L1_ffn_in['W_slice'], 'L1_ffn_b_slice': _L1_ffn_in['b_slice'], 'L1_ffn_W_q': _L1_ffn_in['W_q'], 'L1_ffn_W_k': _L1_ffn_in['W_k'], 'L1_ffn_W_v': _L1_ffn_in['W_v'], 'L1_ffn_W_out': _L1_ffn_in['W_out'], 'L1_ffn_b_out': _L1_ffn_in['b_out'], 'L1_ffn_temperature': _L1_ffn_in['temperature'], 'L2_gnn_W': _L2_gnn_in['W'], 'L2_gnn_b': _L2_gnn_in['b'], 'L2_ffn_W_gat': _L2_ffn_in['W_gat'], 'L2_ffn_att_src': _L2_ffn_in['att_src'], 'L2_ffn_att_dst': _L2_ffn_in['att_dst'], 'L2_ffn_b_gat': _L2_ffn_in['b_gat'], 'L2_ffn_ln_gamma': _L2_ffn_in['ln_gamma'], 'L2_ffn_ln_beta': _L2_ffn_in['ln_beta'], 'L2_ffn_W1': _L2_ffn_in['W1'], 'L2_ffn_b1': _L2_ffn_in['b1'], 'L2_ffn_W2': _L2_ffn_in['W2'], 'L2_ffn_b2': _L2_ffn_in['b2'], 'L2_ffn_edge_index': _L2_ffn_in['edge_index'], 'L3_gnn_W0': _L3_gnn_in['W0'], 'L3_gnn_as0': _L3_gnn_in['as0'], 'L3_gnn_ad0': _L3_gnn_in['ad0'], 'L3_gnn_b0': _L3_gnn_in['b0'], 'L3_gnn_W1': _L3_gnn_in['W1'], 'L3_gnn_as1': _L3_gnn_in['as1'], 'L3_gnn_ad1': _L3_gnn_in['ad1'], 'L3_gnn_b1': _L3_gnn_in['b1'], 'L3_gnn_W2': _L3_gnn_in['W2'], 'L3_gnn_as2': _L3_gnn_in['as2'], 'L3_gnn_ad2': _L3_gnn_in['ad2'], 'L3_gnn_b2': _L3_gnn_in['b2'], 'L3_ffn_gamma': _L3_ffn_in['gamma'], 'L3_ffn_beta': _L3_ffn_in['beta'], 'L3_ffn_Wr': _L3_ffn_in['Wr'], 'L3_ffn_br': _L3_ffn_in['br'], 'L3_ffn_W1': _L3_ffn_in['W1'], 'L3_ffn_b1': _L3_ffn_in['b1'], 'L3_ffn_W2': _L3_ffn_in['W2'], 'L3_ffn_b2': _L3_ffn_in['b2']}

def reference(x, src, dst, edge_type_8, edge_weight, node_type_4, L0_gnn_k_linears, L0_gnn_q_linears, L0_gnn_v_linears, L0_gnn_a_linears, L0_gnn_relation_att, L0_gnn_relation_msg, L0_gnn_relation_pri, L0_gnn_skip, L0_ffn_router_w, L0_ffn_w1, L0_ffn_b1, L0_ffn_w2, L0_ffn_b2, L1_gnn_W, L1_ffn_W_fx, L1_ffn_b_fx, L1_ffn_W_x, L1_ffn_b_x, L1_ffn_W_slice, L1_ffn_b_slice, L1_ffn_W_q, L1_ffn_W_k, L1_ffn_W_v, L1_ffn_W_out, L1_ffn_b_out, L1_ffn_temperature, L2_gnn_W, L2_gnn_b, L2_ffn_W_gat, L2_ffn_att_src, L2_ffn_att_dst, L2_ffn_b_gat, L2_ffn_ln_gamma, L2_ffn_ln_beta, L2_ffn_W1, L2_ffn_b1, L2_ffn_W2, L2_ffn_b2, L2_ffn_edge_index, L3_gnn_W0, L3_gnn_as0, L3_gnn_ad0, L3_gnn_b0, L3_gnn_W1, L3_gnn_as1, L3_gnn_ad1, L3_gnn_b1, L3_gnn_W2, L3_gnn_as2, L3_gnn_ad2, L3_gnn_b2, L3_ffn_gamma, L3_ffn_beta, L3_ffn_Wr, L3_ffn_br, L3_ffn_W1, L3_ffn_b1, L3_ffn_W2, L3_ffn_b2):
    import jax
    import jax.numpy as jnp

    def _L0_gnn_ref(h, k_linears, q_linears, v_linears, a_linears, relation_att, relation_msg, relation_pri, skip, node_type, etype, row_idx, col_idx):
        import jax, jax.numpy as jnp
        import numpy as np
        N_NODES = 625
        N_EDGES = 10000
        IN_DIM = 256
        OUT_DIM = 256
        N_HEADS = 4
        D_K = OUT_DIM // N_HEADS
        N_NTYPES = 4
        N_RELS = 8
        SQRT_DK = float(np.sqrt(D_K))

        def _typed_matmul(x, W, node_type):
            all_t = jnp.einsum('ni,tio->tno', x, W)
            return all_t[node_type, jnp.arange(x.shape[0])]
        n = h.shape[0]
        k = _typed_matmul(h, k_linears, node_type).reshape(n, N_HEADS, D_K)
        q = _typed_matmul(h, q_linears, node_type).reshape(n, N_HEADS, D_K)
        v = _typed_matmul(h, v_linears, node_type).reshape(n, N_HEADS, D_K)
        q_att = jnp.einsum('nhd,rhde->rnhe', q, relation_att)
        v_msg = jnp.einsum('nhd,rhde->rnhe', v, relation_msg)
        aw_q_edge = q_att[etype, col_idx]
        msg_edge = v_msg[etype, row_idx]
        attn_score = jnp.sum(aw_q_edge * k[row_idx], axis=-1)
        score = attn_score * (relation_pri[etype] / SQRT_DK)
        m = jax.ops.segment_max(score, col_idx, num_segments=n)
        ex = jnp.exp(score - m[col_idx])
        denom = jax.ops.segment_sum(ex, col_idx, num_segments=n)
        alpha = ex / denom[col_idx]
        agg = jax.ops.segment_sum(alpha[..., None] * msg_edge, col_idx, num_segments=n)
        agg = agg.reshape(n, OUT_DIM)
        out = _typed_matmul(agg, a_linears, node_type)
        out = jax.nn.sigmoid(skip)[node_type][:, None] * out
        return out

    def _L0_ffn_ref(input_embeddings, router_w, w1, b1, w2, b2):
        import jax, jax.numpy as jnp
        import numpy as np
        NUM_EXPERTS = 8
        TOP_K = 2
        B, S, D = (8, 256, 256)

        def _moe(tokens, router_w, w1, b1, w2, b2):
            N = tokens.shape[0]
            E = router_w.shape[0]
            logits = tokens.astype(jnp.float32) @ router_w.astype(jnp.float32).T
            probs = jax.nn.softmax(logits, axis=-1)
            rw, re = jax.lax.top_k(probs, TOP_K)
            if TOP_K > 1:
                rw = rw / jnp.maximum(rw.sum(-1, keepdims=True), 1e-12)
            rw = rw.astype(tokens.dtype)
            combine = jnp.zeros((N, E), tokens.dtype).at[jnp.arange(N)[:, None], re].set(rw)
            out = tokens
            for e in range(E):
                h = jax.nn.gelu(tokens @ w1[e] + b1[e], approximate=False)
                y = h @ w2[e] + b2[e]
                out = out + combine[:, e:e + 1] * y
            return out
        b, s, d = input_embeddings.shape
        tokens = input_embeddings.reshape(b * s, d)
        return _moe(tokens, router_w, w1, b1, w2, b2).reshape(b, s, d)

    def _L1_gnn_ref(x, W, edge_index):
        import jax, jax.numpy as jnp
        import numpy as np
        N_NODES = 50000
        N = x.shape[0]
        src, dst = (edge_index[0], edge_index[1])
        h = x @ W
        deg = jax.ops.segment_sum(jnp.ones_like(dst, dtype=h.dtype), dst, num_segments=N)
        deg_inv_sqrt = jnp.where(deg > 0, jax.lax.rsqrt(jnp.maximum(deg, 1)), 0.0)
        norm = deg_inv_sqrt[src] * deg_inv_sqrt[dst]
        msgs = h[src] * norm[:, None]
        out = jax.ops.segment_sum(msgs, dst, num_segments=N)
        return out

    def _L1_ffn_ref(x, W_fx, b_fx, W_x, b_x, W_slice, b_slice, W_q, W_k, W_v, W_out, b_out, temperature):
        import jax, jax.numpy as jnp
        import numpy as np
        DIM = 256
        H = 8
        D = 64
        G = 64
        INNER = H * D
        SCALE = D ** (-0.5)
        B, N, _ = x.shape
        fx_mid = (x @ W_fx + b_fx).reshape(B, N, H, D).transpose(0, 2, 1, 3)
        x_mid = (x @ W_x + b_x).reshape(B, N, H, D).transpose(0, 2, 1, 3)
        temp = jnp.clip(temperature, 0.1, 5.0)
        slice_weights = jax.nn.softmax((x_mid @ W_slice + b_slice) / temp, axis=-1)
        slice_norm = slice_weights.sum(axis=2)
        slice_token = jnp.einsum('bhnc,bhng->bhgc', fx_mid, slice_weights)
        slice_token = slice_token / (slice_norm[..., None] + 1e-05)
        q = slice_token @ W_q
        k = slice_token @ W_k
        v = slice_token @ W_v
        attn = jax.nn.softmax(jnp.einsum('bhgc,bhkc->bhgk', q, k) * SCALE, axis=-1)
        out_slice = jnp.einsum('bhgk,bhkc->bhgc', attn, v)
        out_x = jnp.einsum('bhgc,bhng->bhnc', out_slice, slice_weights)
        out_x = out_x.transpose(0, 2, 1, 3).reshape(B, N, INNER)
        return out_x @ W_out + b_out

    def _L2_gnn_ref(x, edge_index, edge_weight, num_nodes, W, b):
        import jax, jax.numpy as jnp
        import numpy as np
        EPS = 0.1
        h = x @ W.T + b
        row, col = (edge_index[0], edge_index[1])
        alpha = jnp.tanh(jnp.sum(h[row] * h[col], axis=1))
        msg = h[col] * alpha[:, None]
        out = jax.ops.segment_sum(msg, row, num_segments=num_nodes)
        deg = jax.ops.segment_sum(jnp.ones_like(alpha), row, num_segments=num_nodes)
        deg = jnp.clip(deg, 1.0, None)
        out = out / deg[:, None]
        return EPS * h + (1.0 - EPS) * out

    def _L2_ffn_ref(x, W_gat, att_src, att_dst, b_gat, ln_gamma, ln_beta, W1, b1, W2, b2, edge_index):
        import jax, jax.numpy as jnp
        import numpy as np
        B, N, D = (16, 128, 256)
        NUM_EXPERTS, TOP_K, HEADS = (4, 2, 4)
        N_EDGES = 32768
        LN_EPS = 1e-05

        def _layernorm(x, g, b):
            mu = x.mean(-1, keepdims=True)
            var = ((x - mu) ** 2).mean(-1, keepdims=True)
            return (x - mu) * jax.lax.rsqrt(var + LN_EPS) * g + b

        def _forward(x, edge_index, W_gat, att_src, att_dst, b_gat, ln_gamma, ln_beta, W1, b1, W2, b2):
            Bc, Nc, Dc = x.shape
            M = Bc * Nc
            x_flat = x.reshape(M, Dc)
            h = (x_flat @ W_gat).reshape(M, HEADS, NUM_EXPERTS)
            loops = jnp.arange(M, dtype=edge_index.dtype)
            src = jnp.concatenate([edge_index[0], loops])
            dst = jnp.concatenate([edge_index[1], loops])
            a_src = (h * att_src).sum(-1)
            a_dst = (h * att_dst).sum(-1)
            e = jax.nn.leaky_relu(a_src[src] + a_dst[dst], negative_slope=0.2)
            e_max = jax.ops.segment_max(e, dst, num_segments=M)
            ee = jnp.exp(e - e_max[dst])
            denom = jax.ops.segment_sum(ee, dst, num_segments=M)
            alpha = ee / (denom[dst] + 1e-16)
            msg = h[src] * alpha[:, :, None]
            agg = jax.ops.segment_sum(msg, dst, num_segments=M).reshape(M, HEADS * NUM_EXPERTS) + b_gat
            scores = _layernorm(agg, ln_gamma, ln_beta).reshape(M, HEADS, NUM_EXPERTS).mean(1)
            scores = scores.reshape(Bc, Nc, NUM_EXPERTS)
            topk_s, topk_i = jax.lax.top_k(scores, TOP_K)
            w = jax.nn.softmax(topk_s, axis=-1)
            out = jnp.zeros_like(x)
            for ei in range(NUM_EXPERTS):
                g = jnp.where(topk_i == ei, w, 0.0).sum(-1)
                hh = jax.nn.gelu(x @ W1[ei] + b1[ei], approximate=False)
                out = out + g[..., None] * (hh @ W2[ei] + b2[ei])
            return out
        return _forward(x, edge_index, W_gat, att_src, att_dst, b_gat, ln_gamma, ln_beta, W1, b1, W2, b2)

    def _L3_gnn_ref(x, edge_index, W0, as0, ad0, b0, W1, as1, ad1, b1, W2, as2, ad2, b2):
        import jax, jax.numpy as jnp
        import numpy as np
        N_NODES = 50000
        N_EDGES = 25000
        IN_FEATS = 256
        HID = 64
        HEADS = 4
        OUT = 64

        def _gat_layer(x, src, dst, W, a_s, a_d, b, num_nodes):
            H, F = a_s.shape
            h = (x @ W).reshape(num_nodes, H, F)
            al_s = jnp.einsum('nhf,hf->nh', h, a_s)
            al_d = jnp.einsum('nhf,hf->nh', h, a_d)
            e = jax.nn.leaky_relu(al_s[src] + al_d[dst], 0.2)
            emax = jax.ops.segment_max(e, dst, num_segments=num_nodes)
            emax = jnp.where(jnp.isfinite(emax), emax, 0.0)
            ee = jnp.exp(e - emax[dst])
            denom = jax.ops.segment_sum(ee, dst, num_segments=num_nodes)
            alpha = ee / (denom[dst] + 1e-16)
            out = jax.ops.segment_sum(alpha[:, :, None] * h[src], dst, num_segments=num_nodes)
            return out.reshape(num_nodes, H * F) + b
        n = x.shape[0]
        loop = jnp.arange(n, dtype=edge_index.dtype)
        src = jnp.concatenate([edge_index[0], loop])
        dst = jnp.concatenate([edge_index[1], loop])
        h = _gat_layer(x, src, dst, W0, as0, ad0, b0, n)
        h = _gat_layer(h, src, dst, W1, as1, ad1, b1, n)
        h = _gat_layer(h, src, dst, W2, as2, ad2, b2, n)
        return h

    def _L3_ffn_ref(x, gamma, beta, Wr, br, W1, b1, W2, b2):
        import jax, jax.numpy as jnp
        import numpy as np
        E = 8
        K = 2
        D = 256
        H = 512
        DOUT = 256
        EPS = 1e-05
        mu = jnp.mean(x, axis=-1, keepdims=True)
        var = jnp.mean(jnp.square(x - mu), axis=-1, keepdims=True)
        xn = (x - mu) * jax.lax.rsqrt(var + EPS) * gamma + beta
        logits = jnp.einsum('bsd,de->bse', xn, Wr) + br
        top_vals, top_idx = jax.lax.top_k(logits, K)
        w = jax.nn.softmax(top_vals, axis=-1)
        w_full = jnp.einsum('bsk,bske->bse', w, jax.nn.one_hot(top_idx, E, dtype=w.dtype))
        y = jnp.zeros(x.shape[:-1] + (DOUT,), x.dtype)
        for e in range(E):
            h = jax.nn.gelu(jnp.einsum('bsd,dh->bsh', xn, W1[e]) + b1[e], approximate=False)
            y_e = jnp.einsum('bsh,hd->bsd', h, W2[e]) + b2[e]
            y = y + y_e * w_full[..., e, None]
        return y
    edge_index = jnp.stack([src, dst])
    x = x + _L0_gnn_ref(_layernorm(x, axis=-1), L0_gnn_k_linears, L0_gnn_q_linears, L0_gnn_v_linears, L0_gnn_a_linears, L0_gnn_relation_att, L0_gnn_relation_msg, L0_gnn_relation_pri, L0_gnn_skip, node_type_4, edge_type_8, src, dst)
    x = x + _L0_ffn_ref(_layernorm(x, axis=-1)[None], L0_ffn_router_w, L0_ffn_w1, L0_ffn_b1, L0_ffn_w2, L0_ffn_b2)[0]
    x = x + _L1_gnn_ref(_layernorm(x, axis=-1), L1_gnn_W, edge_index)
    x = x + _L1_ffn_ref(_layernorm(x, axis=-1)[None], L1_ffn_W_fx, L1_ffn_b_fx, L1_ffn_W_x, L1_ffn_b_x, L1_ffn_W_slice, L1_ffn_b_slice, L1_ffn_W_q, L1_ffn_W_k, L1_ffn_W_v, L1_ffn_W_out, L1_ffn_b_out, L1_ffn_temperature)[0]
    x = x + _L2_gnn_ref(_layernorm(x, axis=-1), edge_index, edge_weight, 3125, L2_gnn_W, L2_gnn_b)
    x = x + _L2_ffn_ref(_layernorm(x, axis=-1)[None], L2_ffn_W_gat, L2_ffn_att_src, L2_ffn_att_dst, L2_ffn_b_gat, L2_ffn_ln_gamma, L2_ffn_ln_beta, L2_ffn_W1, L2_ffn_b1, L2_ffn_W2, L2_ffn_b2, L2_ffn_edge_index)[0]
    x = x + _L3_gnn_ref(_layernorm(x, axis=-1), edge_index, L3_gnn_W0, L3_gnn_as0, L3_gnn_ad0, L3_gnn_b0, L3_gnn_W1, L3_gnn_as1, L3_gnn_ad1, L3_gnn_b1, L3_gnn_W2, L3_gnn_as2, L3_gnn_ad2, L3_gnn_b2)
    x = x + _L3_ffn_ref(_layernorm(x, axis=-1)[None], L3_ffn_gamma, L3_ffn_beta, L3_ffn_Wr, L3_ffn_br, L3_ffn_W1, L3_ffn_b1, L3_ffn_W2, L3_ffn_b2)[0]
    return x

_drawn_inputs = setup_inputs


def setup_inputs(seed=0):
    import zlib

    import numpy as np

    out = dict(_drawn_inputs(seed))
    spreads = {'L0_gnn_relation_pri': (1.0, 0.2),
     'L0_gnn_skip': (1.0, 0.2),
     'L0_ffn_b1': (0.0, 0.1),
     'L0_ffn_b2': (0.0, 0.1),
     'L1_ffn_b_fx': (0.0, 0.1),
     'L1_ffn_b_x': (0.0, 0.654),
     'L1_ffn_b_slice': (0.0, 0.8),
     'L1_ffn_b_out': (0.0, 0.1),
     'L1_ffn_temperature': (0.5, 0.6),
     'L2_gnn_b': (0.0, 0.1),
     'L2_ffn_b_gat': (0.0, 0.1),
     'L2_ffn_ln_gamma': (1.0, 0.2),
     'L2_ffn_ln_beta': (0.0, 0.358),
     'L2_ffn_b1': (0.0, 0.32),
     'L2_ffn_b2': (0.0, 0.1),
     'L3_gnn_b0': (0.0, 0.1),
     'L3_gnn_b1': (0.0, 0.1),
     'L3_gnn_b2': (0.0, 0.1),
     'L3_ffn_br': (0.0, 0.398)}
    factors = {'L1_ffn_W_x': 8.0,
     'L1_ffn_W_slice': 7.014,
     'L1_ffn_W_q': 8.0,
     'L1_ffn_W_k': 8.0,
     'L2_ffn_att_dst': 3.596,
     'L3_gnn_as0': 8.0,
     'L3_gnn_ad0': 36.933,
     'L3_gnn_as1': 8.0,
     'L3_gnn_ad1': 64.0,
     'L3_gnn_as2': 50.078,
     'L3_gnn_ad2': 64.0,
     'L3_ffn_gamma': 8.0,
     'L3_ffn_beta': 8.0,
     'L3_ffn_Wr': 2.727,
     'L3_ffn_b1': 23.402,
     'L3_ffn_b2': 8.0}
    for name, (base, spread) in spreads.items():
        noise = np.random.default_rng([zlib.crc32(name.encode()), seed]).standard_normal(out[name].shape)
        drawn = base * np.exp(spread * noise) if base else spread * noise
        out[name] = jnp.asarray(drawn.astype(out[name].dtype))
    for name, factor in factors.items():
        out[name] = (out[name] * factor).astype(out[name].dtype)
    return out
```

```python
from contextlib import ExitStack

import concourse.bass as bass
from concourse import mybir

ALU = mybir.AluOpType
ACT = mybir.ActivationFunctionType
F32 = mybir.dt.float32
I32 = mybir.dt.int32
U32 = mybir.dt.uint32
U16 = mybir.dt.uint16
AX_X = mybir.AxisListType.X

P = 128
D = 256
N = 3125
T = (N + P - 1) // P
NP = T * P
NC = D // P
LAST = N - (T - 1) * P
U = 5
G = T // U
EPS = 1e-5
BIG = 1e30

ds = bass.ds


class Stage:

    def __init__(self, nc, name):
        self.nc, self.name = nc, name

    def __enter__(self):
        self.ctx = ExitStack()
        self.sems = []
        self.n = 0
        return self

    def sb(self, name, shape, dt=F32):
        return self.ctx.enter_context(self.nc.sbuf_tensor(f"{self.name}_{name}", shape, dt))

    def ps(self, name, shape, dt=F32):
        return self.ctx.enter_context(self.nc.psum_tensor(f"{self.name}_{name}", shape, dt))

    def sem(self, name):
        s = self.nc.alloc_semaphore(name=f"{self.name}_{name}")
        self.sems.append(s)
        return s

    def block(self):
        return self.nc.Block()

    def __exit__(self, *exc):
        self.ctx.close()
        self.nc.all_engine_barrier()
        self.nc.clear_and_free_semaphores(self.sems)
        self.nc.all_engine_barrier()
        return False


class Chain:

    def __init__(self, eng, sem):
        self.eng, self.sem, self.n, self.base = eng, sem, 0, 0

    def link(self, ins):
        self.n += 1
        ins.then_inc(self.sem, 1)
        self.eng.wait_ge(self.sem, self.base + self.n)

    def loop(self, i, per):
        self.start, self.per = self.base + self.n, per
        self.base, self.n = self.start + i * per, 0

    def end(self, trips):
        assert self.n == self.per, (self.n, self.per)
        self.base, self.n = self.start + trips * self.per, 0


def col(ap):
    return ap.rearrange("(p a) -> p a", a=1)


def row(ap):
    return ap.rearrange("(a n) -> a n", a=1)


def setup(nc, R, x):
    with Stage(nc, "setup") as st:
        loaded = st.sem("x_loaded")
        zeroed = st.sem("tail_zeroed")
        made = st.sem("constants_made")
        with st.block() as block:
            @block.sync
            def _(sp):
                sp.dma_start(R.x[:, 0:T - 1, :], x[0:(T - 1) * P, :].rearrange("(t p) d -> p t d", p=P)
                             ).then_inc(loaded, 16)
                sp.wait_ge(zeroed, 1)
                sp.dma_start(R.x[0:LAST, T - 1, :], x[(T - 1) * P:N, :]).then_inc(loaded, 16)
                sp.wait_ge(loaded, 32)

            @block.gpsimd
            def _(pool):
                nc.gpsimd.memset(R.x[:, T - 1, :], 0.0).then_inc(zeroed, 1)
                nc.gpsimd.memset(R.ident[:], 0.0).then_inc(made, 1)
                nc.gpsimd.memset(R.ones[:], 1.0).then_inc(made, 1)
                nc.gpsimd.memset(R.lower[:], 1.0).then_inc(made, 1)
                nc.gpsimd.memset(R.valid[:], 1.0).then_inc(made, 1)
                pool.wait_ge(made, 4)
                nc.gpsimd.affine_select(out=R.ident[:], in_=R.ident[:], compare_op=ALU.not_equal, fill=1.0,
                                        base=0, pattern=[[-1, P]], channel_multiplier=1).then_inc(made, 1)
                nc.gpsimd.affine_select(out=R.lower[:], in_=R.lower[:], compare_op=ALU.is_gt, fill=0.0,
                                        base=0, pattern=[[-1, P]], channel_multiplier=1).then_inc(made, 1)
                nc.gpsimd.affine_select(out=R.valid[:], in_=R.valid[:], compare_op=ALU.is_gt, fill=0.0,
                                        base=N, pattern=[[-P, T]], channel_multiplier=-1).then_inc(made, 1)
                pool.wait_ge(made, 7)


def store(nc, R, out):
    with Stage(nc, "store") as st:
        stored = st.sem("out_stored")
        with st.block() as block:
            @block.sync
            def _(sp):
                sp.dma_start(out[0:(T - 1) * P, :].rearrange("(t p) d -> p t d", p=P), R.x[:, 0:T - 1, :]
                             ).then_inc(stored, 16)
                sp.dma_start(out[(T - 1) * P:N, :], R.x[0:LAST, T - 1, :]).then_inc(stored, 16)
                sp.wait_ge(stored, 32)


def layernorm_T(nc, R, name, src, gamma=None, beta=None, norm=True):
    with Stage(nc, name) as st:
        mean = st.sb("mean", [P, T])
        root = st.sb("root", [P, T])
        rstd = st.sb("rstd", [P, T])
        sq = st.sb("sq", [P, T, D]) if norm else None
        xs = st.sb("xs", [P, U, D])
        gb = st.sb("gb", [P, 2, D])
        pt = st.ps("pt", [P, U, 512])
        chain_s = st.sem("dve_chain")
        gb_loaded = st.sem("gb_loaded")
        centred = st.sem("centred")
        squared = st.sem("squared")
        var_ready = st.sem("var_ready")
        root_ready = st.sem("root_ready")
        xn_ready = st.sem("xn_ready")
        staged = st.sem("tile_staged")
        turned = st.sem("tile_transposed")
        copied = st.sem("tile_copied")
        rounds = norm + (gamma is not None)
        with st.block() as block:
            if gamma is not None:
                @block.sync
                def _(sp):
                    sp.dma_start(gb[:, 0, :], row(gamma).to_broadcast([P, D])).then_inc(gb_loaded, 16)
                    sp.dma_start(gb[:, 1, :], row(beta).to_broadcast([P, D])).then_inc(gb_loaded, 16)

            if norm:
                @block.vector
                def _(dve):
                    ch = Chain(dve, chain_s)
                    for k in range(rounds):
                        a = src if k == 0 else R.xn
                        ch.link(nc.vector.tensor_reduce(mean[:], a[:], AX_X, ALU.add))
                        ch.link(nc.vector.tensor_scalar(mean[:], mean[:], 1.0 / D, None, ALU.mult))
                        nc.vector.tensor_tensor(R.xn[:], a[:], mean[:, :].unsqueeze(2).to_broadcast([P, T, D]),
                                                ALU.subtract).then_inc(centred, 1)
                        dve.wait_ge(squared, k + 1)
                        ch.link(nc.vector.tensor_reduce(root[:], sq[:], AX_X, ALU.add))
                        nc.vector.tensor_scalar(root[:], root[:], 1.0 / D, EPS, ALU.mult, ALU.add
                                                ).then_inc(var_ready, 1)
                        dve.wait_ge(root_ready, k + 1)
                        ch.link(nc.vector.reciprocal(rstd[:], root[:]))
                        ins = nc.vector.tensor_tensor(R.xn[:], R.xn[:],
                                                      rstd[:, :].unsqueeze(2).to_broadcast([P, T, D]), ALU.mult)
                        if k < rounds - 1:
                            ch.link(ins)
                    if gamma is not None:
                        dve.wait_ge(gb_loaded, 32)
                        ch.link(ins)
                        ch.link(nc.vector.tensor_tensor(R.xn[:], R.xn[:],
                                                        gb[:, 0:1, :].to_broadcast([P, T, D]), ALU.mult))
                        ins = nc.vector.tensor_tensor(R.xn[:], R.xn[:], gb[:, 1:2, :].to_broadcast([P, T, D]),
                                                      ALU.add)
                    ins.then_inc(xn_ready, 1)

            @block.gpsimd
            def _(pool):
                if norm:
                    pool.wait_ge(xn_ready, 1)
                a = R.xn if norm else src
                with pool.Fori(0, G) as g:
                    for u in range(U):
                        pool.wait_ge(turned, g * U + u + 1)
                        nc.gpsimd.tensor_copy(xs[:, u, :], a[:, ds(g * U + u, 1), :].rearrange("p a d -> p (a d)")
                                              ).then_inc(staged, 1)

            @block.tensor
            def _(pe):
                pe.sem_inc(turned, U)
                with pe.Fori(0, G) as g:
                    for u in range(U):
                        pe.wait_ge(staged, g * U + u + 1)
                        pe.wait_ge(copied, g * U + u + 1)
                        for c in range(NC):
                            ins = nc.tensor.transpose(pt[:, u, c * P:(c + 1) * P], xs[:, u, c * P:(c + 1) * P],
                                                      R.ident[:])
                        ins.then_inc(turned, 1)

            @block.scalar
            def _(act):
                for k in range(rounds):
                    act.wait_ge(centred, k + 1)
                    nc.scalar.activation(sq[:], R.xn[:], ACT.Square).then_inc(squared, 1)
                    act.wait_ge(var_ready, k + 1)
                    nc.scalar.activation(root[:], root[:], ACT.Sqrt).then_inc(root_ready, 1)
                act.sem_inc(copied, U)
                with act.Fori(0, G) as g:
                    for u in range(U):
                        act.wait_ge(turned, g * U + u + 1 + U)
                        nc.scalar.activation(R.xt[:, :, ds((g * U + u) * P, P)],
                                             pt[:, u, 0:NC * P].rearrange("p (c n) -> p c n", c=NC),
                                             ACT.Copy).then_inc(copied, 1)


def project(nc, R, name, C, load, dst, bias=False, W=None):
    with Stage(nc, name) as st:
        if W is None:
            W = st.sb("W", [P, NC, C])
        b = st.sb("b", [1, C])
        xs = st.sb("xs", [P, U, NC, P])
        pt = st.ps("pt", [P, U, 512])
        loaded = st.sem("weights_loaded")
        staged = st.sem("tile_staged")
        multiplied = st.sem("tile_multiplied")
        copied = st.sem("tile_copied")
        n = []
        with st.block() as block:
            if load is None:
                n.append(0)
            else:
                @block.sync
                def _(sp):
                    n.append(load(sp, W, b, loaded))

            @block.gpsimd
            def _(pool):
                with pool.Fori(0, G) as g:
                    for u in range(U):
                        pool.wait_ge(multiplied, g * U + u + 1)
                        nc.gpsimd.tensor_copy(xs[:, u], R.xt[:, :, ds((g * U + u) * P, P)]).then_inc(staged, 1)

            @block.tensor
            def _(pe):
                pe.sem_inc(multiplied, U)
                if n[0]:
                    pe.wait_ge(loaded, n[0])
                with pe.Fori(0, G) as g:
                    for u in range(U):
                        pe.wait_ge(staged, g * U + u + 1)
                        pe.wait_ge(copied, g * U + u + 1)
                        for c in range(NC):
                            ins = nc.tensor.matmul(pt[:, u, 0:C], xs[:, u, c], W[:, c, :], start=(c == 0),
                                                   stop=(c == NC - 1 and not bias))
                        if bias:
                            ins = nc.tensor.matmul(pt[:, u, 0:C], R.ones[0:1, :], b[:, :], start=False, stop=True)
                        ins.then_inc(multiplied, 1)

            @block.scalar
            def _(act):
                act.sem_inc(copied, U)
                with act.Fori(0, G) as g:
                    for u in range(U):
                        act.wait_ge(multiplied, g * U + u + 1 + U)
                        for buf, lo, hi in dst:
                            ins = nc.scalar.activation(buf[:, ds(g * U + u, 1), 0:hi - lo]
                                                       .rearrange("p a c -> p (a c)"), pt[:, u, lo:hi], ACT.Copy)
                        ins.then_inc(copied, 1)


def top2_gates(nc, R, name, E, softmax_first):
    with Stage(nc, name) as st:
        m = st.sb("max", [P, T])
        e = st.sb("exp", [P, T, E])
        v = st.sb("values", [P, T, E])
        total = st.sb("total", [P, T])
        rank = st.sb("rank", [P, T, E])
        gt = st.sb("greater", [P, T, E, E])
        eq = st.sb("equal", [P, T, E, E])
        before = st.sb("before", [P, E, E])
        chain_s = st.sem("dve_chain")
        shifted = st.sem("scores_shifted")
        exp_ready = st.sem("exp_ready")
        ones_set = st.sem("before_set")
        before_ready = st.sem("before_ready")
        scores = R.scores[:, :, 0:E]
        gates = R.gates[:, :, 0:E]

        def wide(ap):
            return ap.unsqueeze(2).to_broadcast([P, T, E])
        with st.block() as block:
            @block.gpsimd
            def _(pool):
                nc.gpsimd.memset(before[:], 1.0).then_inc(ones_set, 1)
                pool.wait_ge(ones_set, 1)
                nc.gpsimd.affine_select(out=before[:], in_=before[:], compare_op=ALU.is_gt, fill=0.0, base=0,
                                        pattern=[[1, E], [-1, E]], channel_multiplier=0).then_inc(before_ready, 1)

            @block.vector
            def _(dve):
                ch = Chain(dve, chain_s)
                ch.link(nc.vector.tensor_reduce(m[:], scores, AX_X, ALU.max))
                nc.vector.tensor_tensor(e[:], scores, wide(m[:, :]), ALU.subtract).then_inc(shifted, 1)
                dve.wait_ge(exp_ready, 1)
                if softmax_first:
                    ch.link(nc.vector.tensor_reduce(total[:], e[:], AX_X, ALU.add))
                    ch.link(nc.vector.reciprocal(total[:], total[:]))
                    ch.link(nc.vector.tensor_tensor(e[:], e[:], wide(total[:, :]), ALU.mult))
                    ch.link(nc.vector.tensor_copy(v[:], e[:]))
                else:
                    ch.link(nc.vector.tensor_copy(v[:], scores))
                for k in range(E):
                    mine = v[:, :, k:k + 1].to_broadcast([P, T, E])
                    nc.vector.tensor_tensor(gt[:, :, k, :], v[:], mine, ALU.is_gt)
                    ins = nc.vector.tensor_tensor(eq[:, :, k, :], v[:], mine, ALU.is_equal)
                ch.link(ins)
                dve.wait_ge(before_ready, 1)
                for k in range(E):
                    ins = nc.vector.tensor_tensor(eq[:, :, k, :], eq[:, :, k, :],
                                                  before[:, k:k + 1, :].to_broadcast([P, T, E]), ALU.mult)
                ch.link(ins)
                ch.link(nc.vector.tensor_tensor(gt[:], gt[:], eq[:], ALU.add))
                ch.link(nc.vector.tensor_reduce(rank[:], gt[:], AX_X, ALU.add))
                ch.link(nc.vector.tensor_scalar(rank[:], rank[:], 2.0, None, ALU.is_lt))
                ch.link(nc.vector.tensor_tensor(e[:], e[:], rank[:], ALU.mult))
                ch.link(nc.vector.tensor_reduce(total[:], e[:], AX_X, ALU.add))
                if softmax_first:
                    ch.link(nc.vector.tensor_scalar(total[:], total[:], 1e-12, None, ALU.max))
                ch.link(nc.vector.reciprocal(total[:], total[:]))
                ch.link(nc.vector.tensor_tensor(gates, e[:], wide(total[:, :]), ALU.mult))

            @block.scalar
            def _(act):
                act.wait_ge(shifted, 1)
                nc.scalar.activation(e[:], e[:], ACT.Exp).then_inc(exp_ready, 1)


def experts(nc, R, name, E, H, w1, b1, w2, b2, add_xn):
    HC = H // P
    with Stage(nc, name) as st:
        w1s = st.sb("w1", [P, E, NC, H])
        w2s = st.sb("w2", [P, E, HC, D])
        b1s = st.sb("b1", [P, E, HC])
        b2s = st.sb("b2", [1, E, D])
        hT = st.sb("hT", [P, 2, HC, P])
        ph = st.ps("ph", [P, 2, 512])
        py = st.ps("py", [P, 2, 512])
        loaded = st.sem("weights_loaded")
        h_ready = st.sem("hidden_ready")
        gelu_ready = st.sem("gelu_ready")
        y_ready = st.sem("y_ready")
        y_added = st.sem("y_added")
        chain_s = st.sem("dve_chain")
        with st.block() as block:
            @block.sync
            def _(sp):
                for e in range(E):
                    sp.dma_start(w1s[:, e], w1[e].rearrange("(c p) h -> p c h", p=P)).then_inc(loaded, 16)
                    sp.dma_start(w2s[:, e], w2[e].rearrange("(c p) d -> p c d", p=P)).then_inc(loaded, 16)
                sp.dma_start(b1s[:].rearrange("p e c -> p (e c)"), b1.rearrange("e (c p) -> p (e c)", p=P),
                             allow_slow_non_contiguous=True).then_inc(loaded, 16)
                sp.dma_start(b2s[:], b2.rearrange("(a e) d -> a e d", a=1)).then_inc(loaded, 16)

            @block.tensor
            def _(pe):
                pe.wait_ge(loaded, 16 * (2 * E + 2))
                pe.sem_inc(y_ready, 2)
                with pe.Fori(0, T) as i:
                    def hidden(e):
                        pe.wait_ge(gelu_ready, i * E + e + 1)
                        for h in range(HC):
                            for c in range(NC):
                                ins = nc.tensor.matmul(ph[:, e % 2, h * P:(h + 1) * P],
                                                       w1s[:, e, c, h * P:(h + 1) * P],
                                                       R.xt[:, c, ds(i * P, P)], start=(c == 0),
                                                       stop=(c == NC - 1))
                        ins.then_inc(h_ready, 1)

                    hidden(0)
                    for e in range(E):
                        if e + 1 < E:
                            hidden(e + 1)
                        pe.wait_ge(gelu_ready, i * E + e + 3)
                        pe.wait_ge(y_added, i * E + e + 1)
                        for h in range(HC):
                            nc.tensor.matmul(py[:, e % 2, 0:D], hT[:, e % 2, h, :], w2s[:, e, h, :],
                                             start=(h == 0), stop=False)
                        nc.tensor.matmul(py[:, e % 2, 0:D], R.ones[0:1, :], b2s[0:1, e, :], start=False,
                                         stop=True).then_inc(y_ready, 1)

            @block.scalar
            def _(act):
                act.wait_ge(loaded, 16 * (2 * E + 2))
                act.sem_inc(gelu_ready, 2)
                with act.Fori(0, T) as i:
                    for e in range(E):
                        act.wait_ge(h_ready, i * E + e + 1)
                        act.wait_ge(y_ready, i * E + e + 1)
                        for h in range(HC):
                            ins = nc.scalar.activation(hT[:, e % 2, h, :], ph[:, e % 2, h * P:(h + 1) * P],
                                                       ACT.Gelu, bias=b1s[:, e, h:h + 1])
                        ins.then_inc(gelu_ready, 1)

            @block.vector
            def _(dve):
                ch = Chain(dve, chain_s)
                if add_xn:
                    ch.link(nc.vector.tensor_tensor(R.x[:], R.x[:], R.xn[:], ALU.add))
                dve.sem_inc(y_added, 2)
                with dve.Fori(0, T) as i:
                    xi = R.x[:, ds(i, 1), :].rearrange("p a d -> p (a d)")
                    for e in range(E):
                        dve.wait_ge(y_ready, i * E + e + 3)
                        if e:
                            dve.wait_ge(y_added, i * E + e + 2)
                        nc.vector.scalar_tensor_tensor(out=xi, in0=py[:, e % 2, 0:D],
                                                       scalar=R.gates[:, ds(i, 1), e], in1=xi,
                                                       op0=ALU.mult, op1=ALU.add).then_inc(y_added, 1)


def load_plain(w, bias=None):
    def load(sp, W, b, sem):
        sp.dma_start(W[:], w.rearrange("(c p) n -> p c n", p=P)).then_inc(sem, 16)
        if bias is None:
            return 16
        sp.dma_start(b[:], row(bias)).then_inc(sem, 16)
        return 32
    return load


def l0_ffn(nc, R, A):
    layernorm_T(nc, R, "l0f_ln", R.x)

    def load(sp, W, b, sem):
        for c in range(NC):
            sp.dma_start(W[:, c, :], A["L0_ffn_router_w"].rearrange("e (c p) -> p c e", p=P)[:, c, :],
                         allow_slow_non_contiguous=True).then_inc(sem, 16)
        return 16 * NC
    project(nc, R, "l0f_router", 8, load, [(R.scores, 0, 8)])
    top2_gates(nc, R, "l0f_gates", 8, True)
    experts(nc, R, "l0f_experts", 8, D, A["L0_ffn_w1"], A["L0_ffn_b1"], A["L0_ffn_w2"], A["L0_ffn_b2"], True)


def l3_ffn(nc, R, A):
    layernorm_T(nc, R, "l3f_ln", R.x, gamma=A["L3_ffn_gamma"], beta=A["L3_ffn_beta"])
    project(nc, R, "l3f_router", 8, load_plain(A["L3_ffn_Wr"], A["L3_ffn_br"]), [(R.scores, 0, 8)], bias=True)
    top2_gates(nc, R, "l3f_gates", 8, False)
    experts(nc, R, "l3f_experts", 8, 2 * D, A["L3_ffn_W1"], A["L3_ffn_b1"], A["L3_ffn_W2"], A["L3_ffn_b2"], False)


def count_edges(nc, R, name, src, dst, E, table):
    W = 4
    EC = -(-E // P)
    EC += -EC % (2 * W)
    full, rest = E // EC, E % EC
    GR = EC // W
    SPARE = NP * NP
    with Stage(nc, name) as st:
        zeros = st.sb("zeros", [P, NP])
        ends = st.sb("ends", [P, 2, EC], I32)
        key = st.sb("key", [P, EC])
        earlier = st.sb("earlier", [P, W, W * P])
        spare_i = st.sb("spare_i", [P, W], I32)
        spare = st.sb("spare", [P, W])
        kb = st.sb("key_wide", [P, 2, W, P])
        same = st.sb("same", [P, 2 * W, W * P])
        ones = st.sb("ones", [P, W * P])
        total = st.sb("total", [P, 2, W])
        before = st.sb("before", [P, 2, W])
        where = st.sb("where", [P, 2, W])
        idx = st.sb("idx", [P, 2, W], I32)
        old = st.sb("old", [P, 2, W])
        pk = st.ps("pk", [P, 2, W * P])
        zeroed = st.sem("zeros_set")
        cleared = st.sem("table_cleared")
        padded = st.sem("padding_set")
        loaded = st.sem("edges_loaded")
        const = st.sem("masks_made")
        chain_s = st.sem("dve_chain")
        widened = st.sem("key_widened")
        turned = st.sem("key_rows_ready")
        idx_ready = st.sem("idx_ready")
        gathered = st.sem("old_gathered")
        added = st.sem("count_added")
        admitted = st.sem("pool_admitted")
        written = st.sem("group_written")
        scattered = st.sem("count_scattered")
        rows = table[0:NP * NP, :].rearrange("(t p n) a -> t p (n a)", p=P, n=NP)
        with st.block() as block:
            @block.sync
            def _(sp):
                sp.wait_ge(padded, 1)
                for k, ap in enumerate((src, dst)):
                    sp.dma_start(ends[0:full, k, :], ap[0:full * EC].rearrange("(p k) -> p k", k=EC)
                                 ).then_inc(loaded, 16)
                    if rest:
                        sp.dma_start(ends[full:full + 1, k, 0:rest], row(ap[full * EC:E])).then_inc(loaded, 16)
                sp.wait_ge(zeroed, 1)
                with sp.Fori(0, T) as t:
                    sp.dma_start(rows[ds(t, 1)].rearrange("a p n -> p (a n)"), zeros[:]).then_inc(cleared, 16)
                sp.dma_start(table[SPARE:SPARE + W * P, :].rearrange("(p k) a -> p (k a)", k=W), zeros[:, 0:W]
                             ).then_inc(cleared, 16)
                sp.wait_ge(cleared, 16 * (T + 1))
                sp.wait_ge(loaded, 16 * (4 if rest else 2))

            @block.gpsimd
            def _(pool):
                nc.gpsimd.memset(ends[:], NP - 1).then_inc(padded, 1)
                nc.gpsimd.memset(zeros[:], 0.0).then_inc(zeroed, 1)
                nc.gpsimd.memset(earlier[:], 1.0).then_inc(const, 1)
                nc.gpsimd.memset(ones[:], 1.0).then_inc(const, 1)
                nc.gpsimd.iota(spare_i[:], pattern=[[P, W]], base=SPARE, channel_multiplier=1).then_inc(const, 1)
                pool.wait_ge(const, 3)
                nc.gpsimd.affine_select(out=earlier[:], in_=earlier[:], compare_op=ALU.is_gt, fill=0.0, base=0,
                                        pattern=[[P, W], [-1, W * P]], channel_multiplier=1).then_inc(const, 1)
                pool.wait_ge(cleared, 16 * (T + 1))
                with pool.Fori(0, GR // 2) as g:
                    for b in range(2):
                        n = g * 2 + b
                        pool.wait_ge(idx_ready, n + 1)
                        pool.sem_inc(admitted, 1)
                        for a in range(W):
                            nc.gpsimd.indirect_dma_start(
                                out=old[:, b, a:a + 1], out_offset=None, in_=table[:, :],
                                in_offset=bass.IndirectOffsetOnAxis(ap=idx[:, b, a:a + 1], axis=0)
                            ).then_inc(gathered, 16)
                        pool.wait_ge(added, n + 1)
                        pool.sem_inc(admitted, 1)
                        for a in range(W):
                            nc.gpsimd.indirect_dma_start(
                                out=table[:, :], in_=old[:, b, a:a + 1], in_offset=None,
                                out_offset=bass.IndirectOffsetOnAxis(ap=idx[:, b, a:a + 1], axis=0)
                            ).then_inc(scattered, 16)
                        pool.wait_ge(scattered, (n + 1) * 16 * W)
                        pool.sem_inc(written, 1)

            @block.tensor
            def _(pe):
                with pe.Fori(0, GR // 2) as g:
                    for b in range(2):
                        pe.wait_ge(widened, g * 2 + b + 1)
                        for a in range(W):
                            ins = nc.tensor.transpose(pk[:, b, a * P:(a + 1) * P], kb[:, b, a, :], R.ident[:])
                        ins.then_inc(turned, 1)

            @block.vector
            def _(dve):
                ch = Chain(dve, chain_s)
                dve.wait_ge(const, 4)
                dve.sem_inc(written, 2)
                ch.link(nc.vector.tensor_copy(spare[:], spare_i[:]))
                dve.wait_ge(loaded, 16 * (4 if rest else 2))
                ch.link(nc.vector.tensor_copy(key[:], ends[:, 1, :]))
                ch.link(nc.vector.tensor_scalar(key[:], key[:], float(NP), None, ALU.mult))
                ch.link(nc.vector.tensor_tensor(key[:], key[:], ends[:, 0, :], ALU.add))
                with dve.Fori(0, GR // 2) as g:
                    ch.loop(g, 2 * 5)
                    for b in range(2):
                        n = g * 2 + b
                        kg = key[:, ds(n * W, W)]
                        nc.vector.tensor_copy(kb[:, b], kg.unsqueeze(2).to_broadcast([P, W, P])
                                              ).then_inc(widened, 1)
                        dve.wait_ge(turned, n + 1)
                        for a in range(W):
                            ka = key[:, ds(n * W + a, 1)]
                            nc.vector.scalar_tensor_tensor(out=same[:, a], in0=pk[:, b, :], scalar=ka,
                                                           in1=earlier[:, a, :], op0=ALU.is_equal, op1=ALU.mult,
                                                           accum_out=before[:, b, a:a + 1])
                            ins = nc.vector.scalar_tensor_tensor(out=same[:, W + a], in0=pk[:, b, :], scalar=ka,
                                                                 in1=ones[:], op0=ALU.is_equal, op1=ALU.mult,
                                                                 accum_out=total[:, b, a:a + 1])
                        ch.link(ins)
                        ch.link(nc.vector.tensor_scalar(before[:, b], before[:, b], 0.5, None, ALU.is_lt))
                        ch.link(nc.vector.tensor_tensor(where[:, b], kg, spare[:], ALU.subtract))
                        ch.link(nc.vector.tensor_tensor(where[:, b], where[:, b], before[:, b], ALU.mult))
                        ch.link(nc.vector.tensor_tensor(where[:, b], where[:, b], spare[:], ALU.add))
                        dve.wait_ge(written, n + 1)
                        nc.vector.tensor_copy(idx[:, b], where[:, b]).then_inc(idx_ready, 1)
                        dve.wait_ge(gathered, (n + 1) * 16 * W)
                        nc.vector.tensor_tensor(old[:, b], old[:, b], total[:, b], ALU.add).then_inc(added, 1)
                ch.end(GR // 2)


JG = [(j, min(j + 4, T)) for j in range(0, T, 4)]
NJ = len(JG)


def turn_group(nc, pe, R, src, q, bank):
    lo, hi = JG[q]
    for j in range(lo, hi):
        ins = nc.tensor.transpose(bank[:, (j - lo) * P:(j - lo + 1) * P], src[:, j * P:(j + 1) * P], R.ident[:])
    return ins


def multiply_group(nc, pe, turned, V, lo_c, hi_c, q, out):
    lo, hi = JG[q]
    for j in range(lo, hi):
        ins = nc.tensor.matmul(out, turned[:, (j - lo) * P:(j - lo + 1) * P], V[:, j, lo_c:hi_c],
                               start=(j == 0), stop=(j == T - 1))
    return ins


def table_rows(table):
    return table[0:NP * NP, :].rearrange("(t p n) a -> t p (n a)", p=P, n=NP)


def load_table(sp, rows, cnt, loaded, freed):
    def one(it, slot, first=False):
        if not first:
            sp.wait_ge(freed, it + 1)
        src = rows[0] if first else rows[ds(it, 1)].rearrange("a p n -> p (a n)")
        sp.dma_start(cnt[:, slot], src).then_inc(loaded[slot], 16)
    one(0, 0, True)
    with sp.Fori(0, T // 2) as g:
        one(g * 2 + 1, 1)
        one(g * 2 + 2, 0)


def gcn(nc, R, name, table):
    rows = table_rows(table)
    with Stage(nc, name + "_deg") as st:
        cnt = st.sb("cnt", [P, 2, NP])
        deg = st.sb("deg", [P, T])
        root = st.sb("root", [P, T])
        loaded = [st.sem("rows_loaded0"), st.sem("rows_loaded1")]
        freed = st.sem("rows_used")
        root_ready = st.sem("root_ready")
        deg_ready = st.sem("deg_ready")
        chain_s = st.sem("dve_chain")
        with st.block() as block:
            @block.sync
            def _(sp):
                load_table(sp, rows, cnt, loaded, freed)

            @block.vector
            def _(dve):
                ch = Chain(dve, chain_s)

                def degree(it, k, slot):
                    dve.wait_ge(loaded[slot], k * 16 + 16)
                    nc.vector.tensor_reduce(deg[:, ds(it, 1)], cnt[:, slot], AX_X, ALU.add).then_inc(freed, 1)

                dve.sem_inc(freed, 2)
                degree(0, 0, 0)
                with dve.Fori(0, T // 2) as g:
                    degree(g * 2 + 1, g, 1)
                    degree(g * 2 + 2, g + 1, 0)
                dve.wait_ge(freed, T + 2)
                nc.vector.tensor_scalar(root[:], deg[:], 1.0, None, ALU.max).then_inc(deg_ready, 1)
                dve.wait_ge(root_ready, 1)
                ch.link(nc.vector.reciprocal(root[:], root[:]))
                ch.link(nc.vector.tensor_scalar(deg[:], deg[:], 0.0, None, ALU.is_gt))
                ch.link(nc.vector.tensor_tensor(R.dis[:], root[:], deg[:], ALU.mult))
                ch.link(nc.vector.tensor_tensor(R.xn[:], R.xn[:], R.dis[:, :].unsqueeze(2).to_broadcast([P, T, D]),
                                                ALU.mult))

            @block.scalar
            def _(act):
                act.wait_ge(deg_ready, 1)
                nc.scalar.activation(root[:], root[:], ACT.Sqrt).then_inc(root_ready, 1)

    with Stage(nc, name) as st:
        cnt = st.sb("cnt", [P, 2, NP])
        turned = st.sb("turned", [P, 2, 512])
        pt = st.ps("pt", [P, 2, 512])
        po = st.ps("po", [P, 2, 512])
        loaded = [st.sem("rows_loaded0"), st.sem("rows_loaded1")]
        freed = st.sem("rows_turned")
        bank_ready = st.sem("bank_ready")
        copied = st.sem("bank_copied")
        used = st.sem("turned_used")
        out_ready = st.sem("out_ready")
        out_used = st.sem("out_used")
        with st.block() as block:
            @block.sync
            def _(sp):
                load_table(sp, rows, cnt, loaded, freed)

            @block.tensor
            def _(pe):
                pe.sem_inc(freed, 2)
                pe.sem_inc(used, 2)

                def turn(it, b, q):
                    n = it * NJ + q
                    pe.wait_ge(copied, n + 1)
                    turn_group(nc, pe, R, cnt[:, b], q, pt[:, (b + q) % 2]).then_inc(bank_ready, 1)

                def tile(it, k, b):
                    pe.wait_ge(loaded[b], k * 16 + 16)
                    pe.wait_ge(out_used, it + 1)
                    turn(it, b, 0)
                    for q in range(NJ):
                        if q + 1 < NJ:
                            turn(it, b, q + 1)
                        if q + 1 == NJ:
                            pe.wait_ge(bank_ready, it * NJ + NJ)
                            pe.sem_inc(freed, 1)
                        pe.wait_ge(copied, it * NJ + q + 3)
                        ins = multiply_group(nc, pe, turned[:, (b + q) % 2], R.xn, 0, D, q, po[:, b, 0:D])
                        ins.then_inc(used, 1)
                    pe.wait_ge(used, it * NJ + NJ + 2)
                    pe.sem_inc(out_ready, 1)

                tile(0, 0, 0)
                with pe.Fori(0, T // 2) as g:
                    tile(g * 2 + 1, g, 1)
                    tile(g * 2 + 2, g + 1, 0)

            @block.scalar
            def _(act):
                act.sem_inc(copied, 2)

                def tile(it, b):
                    for q in range(NJ):
                        w = (JG[q][1] - JG[q][0]) * P
                        act.wait_ge(bank_ready, it * NJ + q + 1)
                        act.wait_ge(used, it * NJ + q + 1)
                        nc.scalar.activation(turned[:, (b + q) % 2, 0:w], pt[:, (b + q) % 2, 0:w], ACT.Copy
                                             ).then_inc(copied, 1)
                tile(0, 0)
                with act.Fori(0, T // 2) as g:
                    tile(g * 2 + 1, 1)
                    tile(g * 2 + 2, 0)

            @block.vector
            def _(dve):
                dve.sem_inc(out_used, 2)

                def tile(it, b):
                    xi = R.x[:, ds(it, 1), :].rearrange("p a d -> p (a d)")
                    dve.wait_ge(out_ready, it + 1)
                    nc.vector.scalar_tensor_tensor(out=xi, in0=po[:, b, 0:D], scalar=R.dis[:, ds(it, 1)], in1=xi,
                                                   op0=ALU.mult, op1=ALU.add).then_inc(out_used, 1)
                tile(0, 0)
                with dve.Fori(0, T // 2) as g:
                    tile(g * 2 + 1, 1)
                    tile(g * 2 + 2, 0)


HEADS = 4
SLOPE = 0.2


def gat_weights(nc, R, name, W, att_src, att_dst, F):
    HF = HEADS * F
    with Stage(nc, name) as st:
        a = st.sb("a", [P, 2, HF])
        prod = st.sb("prod", [P, 2, NC, HEADS, F])
        wa = st.sb("wa", [P, 2, NC, HEADS])
        loaded = st.sem("weights_loaded")
        chain_s = st.sem("dve_chain")
        with st.block() as block:
            @block.sync
            def _(sp):
                sp.dma_start(R.we[:, :, 0:HF], W.rearrange("(c p) n -> p c n", p=P)).then_inc(loaded, 16)
                for k, v in enumerate((att_src, att_dst)):
                    sp.dma_start(a[:, k, :], row(v.rearrange("h f -> (h f)")).to_broadcast([P, HF])
                                 ).then_inc(loaded, 16)

            @block.vector
            def _(dve):
                ch = Chain(dve, chain_s)
                dve.wait_ge(loaded, 48)
                for k in range(2):
                    for c in range(NC):
                        ins = nc.vector.tensor_tensor(prod[:, k, c].rearrange("p h f -> p (h f)"),
                                                      R.we[:, c, 0:HF], a[:, k, :], ALU.mult)
                ch.link(ins)
                for k in range(2):
                    ins = nc.vector.tensor_reduce(wa[:, k], prod[:, k], AX_X, ALU.add)
                ch.link(ins)
                nc.vector.tensor_copy(R.we[:, :, HF:HF + HEADS], wa[:, 1])
                for c in range(NC):
                    ins = nc.vector.tensor_copy(R.was[:, c], wa[:, 0, c, :].unsqueeze(2).to_broadcast([P, HEADS, P]))
                ch.link(ins)


def source_rows(nc, R, name, as_row):
    with Stage(nc, name) as st:
        pt = st.ps("pt", [P, U, 512])
        multiplied = st.sem("tile_multiplied")
        copied = st.sem("tile_copied")
        with st.block() as block:
            @block.tensor
            def _(pe):
                with pe.Fori(0, G) as g:
                    for u in range(U):
                        pe.wait_ge(copied, g * U + u + 1)
                        for h in range(HEADS):
                            for c in range(NC):
                                ins = nc.tensor.matmul(pt[:, u, h * P:(h + 1) * P], R.was[:, c, h, :],
                                                       R.xt[:, c, ds((g * U + u) * P, P)], start=(c == 0),
                                                       stop=(c == NC - 1))
                        ins.then_inc(multiplied, 1)

            @block.scalar
            def _(act):
                act.sem_inc(copied, U)
                with act.Fori(0, G) as g:
                    for u in range(U):
                        act.wait_ge(multiplied, g * U + u + 1)
                        nc.scalar.activation(as_row[:, :, ds((g * U + u) * P, P)],
                                             pt[:, u, :].rearrange("p (h n) -> p h n", h=HEADS),
                                             ACT.Copy).then_inc(copied, 1)


def gat_attend(nc, R, name, table, as_row, bias, F, finish, self_loops, dram=None):
    rows = table_rows(table)
    HF = HEADS * F
    with Stage(nc, name) as st:
        cnt = st.sb("cnt", [P, 2, NP])
        neg = st.sb("neg", [P, NP])
        more = st.sb("more", [P, HEADS - NC, NP])
        Y = [R.xt[:, h] for h in range(NC)] + [more[:, h] for h in range(HEADS - NC)]
        adc = st.sb("a_dst", [P, 2, HEADS])
        top = st.sb("top", [P, 2, HEADS])
        negm = st.sb("negm", [P, 2, HEADS])
        den = st.sb("den", [P, 2, HEADS])
        bb = st.sb("bias", [P, HF])
        ot = st.sb("out", [P, 2, HEADS, F])
        turned = st.sb("turned", [P, 2, 512])
        pt = st.ps("pt", [P, 2, 512])
        po = st.ps("po", [P, 2, 512])
        loaded = [st.sem("rows_loaded0"), st.sem("rows_loaded1")]
        stored = [st.sem("out_stored0"), st.sem("out_stored1")]
        bias_loaded = st.sem("bias_loaded")
        freed = st.sem("rows_used")
        adc_ready = st.sem("a_dst_ready")
        shifted = st.sem("scores_shifted")
        masked = st.sem("masked_ready")
        exp_ready = st.sem("exp_ready")
        p_ready = st.sem("p_ready")
        p_turned = st.sem("p_turned")
        bank_ready = st.sem("bank_ready")
        copied = st.sem("bank_copied")
        used = st.sem("turned_used")
        out_ready = st.sem("out_ready")
        out_used = st.sem("out_used")
        out_done = st.sem("out_done")
        po_read = st.sem("output_bank_read")
        admitted = st.sem("dve_admitted")
        chain_s = st.sem("dve_chain")
        with st.block() as block:
            @block.sync
            def _(sp):
                sp.dma_start(bb[:], row(bias).to_broadcast([P, HF])).then_inc(bias_loaded, 16)

                def one(it, slot, first=False):
                    if not first:
                        sp.wait_ge(freed, it + 1)
                    src = rows[0] if first else rows[ds(it, 1)].rearrange("a p n -> p (a n)")
                    sp.dma_start(cnt[:, slot], src).then_inc(loaded[slot], 16)

                one(0, 0, True)
                with sp.Fori(0, T // 2) as g:
                    one(g * 2 + 1, 1)
                    one(g * 2 + 2, 0)

            if dram is not None:
                @block.gpsimd
                def _(pool):
                    with pool.Fori(0, T // 2) as g:
                        for b in range(2):
                            it = g * 2 + b
                            pool.wait_ge(out_done, it + 1)
                            pool.dma_start(dram[ds(it * P, P), :], ot[:, b].rearrange("p h f -> p (h f)")
                                           ).then_inc(stored[b], 16)
                            pool.wait_ge(stored[b], g * 16 + 16)
                            pool.sem_inc(out_used, 1)
                    pool.wait_ge(out_done, T)
                    pool.dma_start(dram[(T - 1) * P:T * P, :], ot[:, 0].rearrange("p h f -> p (h f)")
                                   ).then_inc(stored[0], 16)
                    pool.wait_ge(stored[0], (T // 2 + 1) * 16)

            @block.vector
            def _(dve):
                ch = Chain(dve, chain_s)
                dve.sem_inc(freed, 2)
                dve.sem_inc(p_turned, HEADS)

                def begin(it, k, b):
                    dve.wait_ge(loaded[b], k * 16 + 16)
                    if self_loops:
                        dgl = cnt[:, b, ds(it * P, P)]
                        ch.link(nc.vector.tensor_tensor(dgl, dgl, R.ident[:], ALU.add))
                    nc.vector.tensor_scalar(neg[:], cnt[:, b], 0.5, -BIG, ALU.is_lt, ALU.mult)
                    ch.link(nc.vector.tensor_copy(adc[:, b], R.ad[:, ds(it, 1), :].rearrange("p a h -> p (a h)")))
                    dve.sem_inc(adc_ready, 1)

                def mask(it, b, h):
                    u = it * HEADS + h
                    dve.wait_ge(shifted, u + 1)
                    dve.sem_inc(admitted, 1)
                    ch.link(nc.vector.tensor_tensor_reduce(Y[h], Y[h], neg[:], 1.0, -3e38,
                                                           ALU.add, ALU.max, top[:, b, h:h + 1]))
                    t = top[:, b, h:h + 1]
                    ch.link(nc.vector.scalar_tensor_tensor(out=t, in0=t, scalar=SLOPE, in1=t, op0=ALU.mult,
                                                           op1=ALU.max))
                    ch.link(nc.vector.tensor_scalar(negm[:, b, h:h + 1], t, -1.0, None, ALU.mult))
                    nc.vector.scalar_tensor_tensor(out=Y[h], in0=Y[h], scalar=SLOPE, in1=Y[h], op0=ALU.mult,
                                                   op1=ALU.max).then_inc(masked, 1)

                def weigh(it, b, h):
                    u = it * HEADS + h
                    dve.wait_ge(exp_ready, u + 1)
                    ins = nc.vector.tensor_tensor_reduce(Y[h], Y[h], cnt[:, b], 1.0, 0.0, ALU.mult,
                                                         ALU.add, den[:, b, h:h + 1])
                    ins.then_inc(p_ready, 1)
                    if h == HEADS - 1:
                        dve.wait_ge(p_ready, u + 1)
                        dve.sem_inc(freed, 1)

                def end(it, b):
                    dve.wait_ge(p_ready, it * HEADS + HEADS)
                    ch.link(nc.vector.tensor_scalar(den[:, b], den[:, b], 1e-16, None, ALU.add))
                    ch.link(nc.vector.reciprocal(den[:, b], den[:, b]))
                    dve.wait_ge(out_ready, it + 1)
                    dve.wait_ge(out_used, it + 1)
                    ch.link(nc.vector.tensor_tensor(ot[:, b], po[:, b, 0:HF].rearrange("p (h f) -> p h f", h=HEADS),
                                                    den[:, b].unsqueeze(2).to_broadcast([P, HEADS, F]), ALU.mult))
                    dve.sem_inc(po_read, 1)
                    of = ot[:, b].rearrange("p h f -> p (h f)")
                    ch.link(nc.vector.tensor_tensor(of, of, bb[:], ALU.add))
                    if finish == "x":
                        xi = R.x[:, ds(it, 1), :].rearrange("p a d -> p (a d)")
                        ch.link(nc.vector.tensor_tensor(xi, xi, of, ALU.add))
                    elif finish == "scores":
                        ch.link(nc.vector.tensor_copy(R.scores[:, ds(it, 1), 0:HF].rearrange("p a c -> p (a c)"),
                                                      of))
                    dve.sem_inc(out_done, 1)
                    if dram is None:
                        dve.sem_inc(out_used, 1)

                def tile(it, k, b, last=None):
                    begin(it, k, b)
                    for h in range(HEADS):
                        mask(it, b, h)
                        if h:
                            weigh(it, b, h - 1)
                        if h == 1 and last is not None:
                            end(last, 1 - b)
                    weigh(it, b, HEADS - 1)

                dve.sem_inc(out_used, 2)
                dve.sem_inc(po_read, 2)
                dve.wait_ge(bias_loaded, 16)
                per = self_loops + 1 + 3 * HEADS + 4 + (finish in ("x", "scores"))
                tile(0, 0, 0)
                with dve.Fori(0, T // 2) as g:
                    ch.loop(g, 2 * per)
                    tile(g * 2 + 1, g, 1, g * 2)
                    tile(g * 2 + 2, g + 1, 0, g * 2 + 1)
                ch.end(T // 2)
                end(T - 1, 0)

            @block.scalar
            def _(act):
                act.sem_inc(copied, 2)

                def shift(it, b, h):
                    if h == 0:
                        act.wait_ge(adc_ready, it + 1)
                    act.wait_ge(p_turned, it * HEADS + h + 1)
                    nc.scalar.activation(Y[h], as_row[:, h], ACT.Identity, bias=adc[:, b, h:h + 1]
                                         ).then_inc(shifted, 1)

                def exp(it, b, h):
                    act.wait_ge(masked, it * HEADS + h + 1)
                    nc.scalar.activation(Y[h], Y[h], ACT.Exp, bias=negm[:, b, h:h + 1]).then_inc(exp_ready, 1)

                def copies(it, h):
                    for q in range(NJ):
                        n = (it * HEADS + h) * NJ + q
                        w = (JG[q][1] - JG[q][0]) * P
                        act.wait_ge(bank_ready, n + 1)
                        act.wait_ge(used, n + 1)
                        nc.scalar.activation(turned[:, (h + q) % 2, 0:w], pt[:, (h + q) % 2, 0:w], ACT.Copy
                                             ).then_inc(copied, 1)

                def tile(it, b):
                    shift(it, b, 0)
                    shift(it, b, 1)
                    for h in range(HEADS):
                        exp(it, b, h)
                        if h + 2 < HEADS:
                            shift(it, b, h + 2)
                        if h:
                            copies(it, h - 1)
                    copies(it, HEADS - 1)

                tile(0, 0)
                with act.Fori(0, T // 2) as g:
                    tile(g * 2 + 1, 1)
                    tile(g * 2 + 2, 0)

            @block.tensor
            def _(pe):
                pe.sem_inc(used, 2)

                def turn(it, h, q):
                    n = (it * HEADS + h) * NJ + q
                    pe.wait_ge(copied, n + 1)
                    turn_group(nc, pe, R, Y[h], q, pt[:, (h + q) % 2]).then_inc(bank_ready, 1)

                def tile(it, b):
                    pe.wait_ge(po_read, it + 1)
                    for h in range(HEADS):
                        pe.wait_ge(p_ready, it * HEADS + h + 1)
                        turn(it, h, 0)
                        for q in range(NJ):
                            if q + 1 < NJ:
                                turn(it, h, q + 1)
                            else:
                                pe.wait_ge(bank_ready, (it * HEADS + h + 1) * NJ)
                                pe.sem_inc(p_turned, 1)
                            pe.wait_ge(copied, (it * HEADS + h) * NJ + q + 3)
                            multiply_group(nc, pe, turned[:, (h + q) % 2], R.xn, h * F, (h + 1) * F, q,
                                           po[:, b, h * F:(h + 1) * F]).then_inc(used, 1)
                    pe.wait_ge(used, (it + 1) * HEADS * NJ + 2)
                    pe.sem_inc(out_ready, 1)

                tile(0, 0)
                with pe.Fori(0, T // 2) as g:
                    tile(g * 2 + 1, 1)
                    tile(g * 2 + 2, 0)


def gat(nc, R, name, table, W, att_src, att_dst, bias, F, finish, self_loops=False, dram=None):
    HF = HEADS * F
    gat_weights(nc, R, name + "_w", W, att_src, att_dst, F)
    project(nc, R, name + "_h", HF + HEADS, None, [(R.xn, 0, HF), (R.ad, HF, HF + HEADS)], W=R.we[:, :, 0:HF + HEADS])
    with nc.sbuf_tensor(name + "_as_row", [P, HEADS, NP], F32) as as_row:
        source_rows(nc, R, name + "_src", as_row)
        gat_attend(nc, R, name, table, as_row, bias, F, finish, self_loops, dram)


def l1_gnn(nc, R, A, edges):
    layernorm_T(nc, R, "l1g_ln", R.x)
    project(nc, R, "l1g_h", D, load_plain(A["L1_gnn_W"]), [(R.xn, 0, D)])
    gcn(nc, R, "l1g", edges)


def reload(nc, R, name, dram):
    with Stage(nc, name) as st:
        loaded = st.sem("rows_loaded")
        with st.block() as block:
            @block.sync
            def _(sp):
                sp.dma_start(R.xn[:], dram[:, :].rearrange("(t p) d -> p t d", p=P)).then_inc(loaded, 16)
                sp.wait_ge(loaded, 16)
    layernorm_T(nc, R, name + "_T", R.xn, norm=False)


def l3_gnn(nc, R, A, edges):
    hidden = nc.dram_tensor("gat_hidden", [2, NP, D], F32).ap()
    layernorm_T(nc, R, "l3g_ln", R.x)
    for k in range(3):
        gat(nc, R, f"l3g{k}", edges, A[f"L3_gnn_W{k}"], A[f"L3_gnn_as{k}"], A[f"L3_gnn_ad{k}"], A[f"L3_gnn_b{k}"],
            D // HEADS, "x" if k == 2 else "dram", self_loops=True, dram=None if k == 2 else hidden[k])
        if k < 2:
            reload(nc, R, f"l3g{k}_next", hidden[k])


def transpose_weight(nc, R, name, W):
    with Stage(nc, name) as st:
        ws = st.sb("ws", [P, NC, D])
        pt = st.ps("pt", [P, NC, 512])
        loaded = st.sem("weight_loaded")
        turned = st.sem("weight_turned")
        copied = st.sem("weight_copied")
        with st.block() as block:
            @block.sync
            def _(sp):
                sp.dma_start(ws[:], W.rearrange("(c p) n -> p c n", p=P)).then_inc(loaded, 16)

            @block.tensor
            def _(pe):
                pe.wait_ge(loaded, 16)
                for c in range(NC):
                    for o in range(NC):
                        ins = nc.tensor.transpose(pt[:, c, o * P:(o + 1) * P], ws[:, o, c * P:(c + 1) * P],
                                                  R.ident[:])
                ins.then_inc(turned, 1)

            @block.vector
            def _(dve):
                dve.wait_ge(turned, 1)
                nc.vector.tensor_copy(R.we[:, :, 0:D], pt[:, :, 0:D]).then_inc(copied, 1)
                dve.wait_ge(copied, 1)


def similarity_gnn(nc, R, name, table):
    cols = table[0:NP * NP, :].rearrange("(t p n) a -> p t (n a)", p=P, n=NP)
    with Stage(nc, name) as st:
        cnt = st.sb("cnt", [P, 2, T, P])
        th = st.sb("tanh", [P, 2, 512])
        mw = st.sb("weights", [P, 2, 512])
        deg = st.sb("deg", [P, 2, 1])
        ot = st.sb("out", [P, 2, D])
        pt = st.ps("ps", [P, 2, 512])
        po = st.ps("po", [P, 2, 512])
        loaded = [st.sem("cols_loaded0"), st.sem("cols_loaded1")]
        freed = st.sem("cols_used")
        dots = st.sem("dots_ready")
        tanhed = st.sem("tanh_ready")
        weighed = st.sem("weights_ready")
        th_free = st.sem("tanh_slot_free")
        used = st.sem("weights_used")
        out_ready = st.sem("out_ready")
        out_used = st.sem("out_used")
        chain_s = st.sem("dve_chain")
        with st.block() as block:
            @block.sync
            def _(sp):
                def one(jt, slot, first=False):
                    if not first:
                        sp.wait_ge(freed, jt + 1)
                    sp.dma_start(cnt[:, slot], cols[:, :, 0:P] if first else cols[:, :, ds(jt * P, P)]
                                 ).then_inc(loaded[slot], 16)
                one(0, 0, True)
                with sp.Fori(0, T // 2) as g:
                    one(g * 2 + 1, 1)
                    one(g * 2 + 2, 0)

            @block.tensor
            def _(pe):
                pe.sem_inc(freed, 2)
                pe.sem_inc(used, 2)

                def dot(jt, b, q):
                    n = jt * NJ + q
                    pe.wait_ge(tanhed, n + 1)
                    lo, hi = JG[q]
                    for i in range(lo, hi):
                        for c in range(NC):
                            ins = nc.tensor.matmul(pt[:, (b + q) % 2, (i - lo) * P:(i - lo + 1) * P],
                                                   R.xt[:, c, i * P:(i + 1) * P], R.xt[:, c, ds(jt * P, P)],
                                                   start=(c == 0), stop=(c == NC - 1))
                    ins.then_inc(dots, 1)

                def tile(jt, k, b):
                    dot(jt, b, 0)
                    pe.wait_ge(out_used, jt + 1)
                    for q in range(NJ):
                        if q + 1 < NJ:
                            dot(jt, b, q + 1)
                        pe.wait_ge(weighed, jt * NJ + q + 1)
                        multiply_group(nc, pe, mw[:, (b + q) % 2], R.xn, 0, D, q, po[:, b, 0:D]).then_inc(used, 1)
                    for i in range(T):
                        ins = nc.tensor.matmul(po[:, b, D:D + 1], cnt[:, b, i, :], R.ones[:, 0:1], start=(i == 0),
                                               stop=(i == T - 1))
                    ins.then_inc(out_ready, 1)
                    pe.wait_ge(out_ready, jt + 1)
                    pe.sem_inc(freed, 1)

                tile(0, 0, 0)
                with pe.Fori(0, T // 2) as g:
                    tile(g * 2 + 1, g, 1)
                    tile(g * 2 + 2, g + 1, 0)

            @block.scalar
            def _(act):
                act.sem_inc(tanhed, 2)

                def tile(jt, b):
                    for q in range(NJ):
                        w = (JG[q][1] - JG[q][0]) * P
                        n = jt * NJ + q
                        act.wait_ge(dots, n + 1)
                        act.wait_ge(th_free, n + 1)
                        nc.scalar.activation(th[:, (b + q) % 2, 0:w], pt[:, (b + q) % 2, 0:w], ACT.Tanh
                                             ).then_inc(tanhed, 1)
                tile(0, 0)
                with act.Fori(0, T // 2) as g:
                    tile(g * 2 + 1, 1)
                    tile(g * 2 + 2, 0)

            @block.vector
            def _(dve):
                ch = Chain(dve, chain_s)
                dve.sem_inc(out_used, 2)
                dve.sem_inc(th_free, 2)

                def tile(jt, k, b):
                    dve.wait_ge(loaded[b], k * 16 + 16)
                    for q in range(NJ):
                        lo, hi = JG[q]
                        n = jt * NJ + q
                        w = (hi - lo) * P
                        dve.wait_ge(tanhed, n + 3)
                        dve.wait_ge(used, n + 1)
                        nc.vector.tensor_tensor(mw[:, (b + q) % 2, 0:w], th[:, (b + q) % 2, 0:w],
                                                cnt[:, b, lo:hi, :].rearrange("p t n -> p (t n)"), ALU.mult
                                                ).then_inc(weighed, 1)
                        dve.wait_ge(weighed, n + 1)
                        dve.sem_inc(th_free, 1)
                    xi = R.x[:, ds(jt, 1), :].rearrange("p a d -> p (a d)")
                    hi_ = R.xn[:, ds(jt, 1), :].rearrange("p a d -> p (a d)")
                    dve.wait_ge(out_ready, jt + 1)
                    ch.link(nc.vector.tensor_scalar(deg[:, b], po[:, b, D:D + 1], 1.0, None, ALU.max))
                    ch.link(nc.vector.reciprocal(deg[:, b], deg[:, b]))
                    ch.link(nc.vector.tensor_scalar(ot[:, b], po[:, b, 0:D], deg[:, b], 0.9, ALU.mult, ALU.mult))
                    dve.sem_inc(out_used, 1)
                    ch.link(nc.vector.scalar_tensor_tensor(out=ot[:, b], in0=hi_, scalar=0.1, in1=ot[:, b],
                                                           op0=ALU.mult, op1=ALU.add))
                    ch.link(nc.vector.tensor_tensor(xi, xi, ot[:, b], ALU.add))

                tile(0, 0, 0)
                with dve.Fori(0, T // 2) as g:
                    ch.loop(g, 10)
                    tile(g * 2 + 1, g, 1)
                    tile(g * 2 + 2, g + 1, 0)
                ch.end(T // 2)


def l2_gnn(nc, R, A, edges):
    layernorm_T(nc, R, "l2g_ln", R.x)
    transpose_weight(nc, R, "l2g_w", A["L2_gnn_W"])

    def load(sp, W, b, sem):
        sp.dma_start(b[:], row(A["L2_gnn_b"])).then_inc(sem, 16)
        return 16
    project(nc, R, "l2g_h", D, load, [(R.xn, 0, D)], bias=True, W=R.we[:, :, 0:D])
    layernorm_T(nc, R, "l2g_hT", R.xn, norm=False)
    similarity_gnn(nc, R, "l2g", edges)


def router_scores(nc, R, name, gamma, beta, E):
    C = HEADS * E
    with Stage(nc, name) as st:
        c = st.sb("centred", [P, T, C])
        sq = st.sb("squared", [P, T, C])
        mean = st.sb("mean", [P, T])
        gb = st.sb("gb", [P, 2, C])
        loaded = st.sem("gb_loaded")
        var_ready = st.sem("var_ready")
        root_ready = st.sem("root_ready")
        chain_s = st.sem("dve_chain")
        with st.block() as block:
            @block.sync
            def _(sp):
                sp.dma_start(gb[:, 0, :], row(gamma).to_broadcast([P, C])).then_inc(loaded, 16)
                sp.dma_start(gb[:, 1, :], row(beta).to_broadcast([P, C])).then_inc(loaded, 16)

            @block.scalar
            def _(act):
                act.wait_ge(var_ready, 1)
                nc.scalar.activation(mean[:], mean[:], ACT.Sqrt).then_inc(root_ready, 1)

            @block.vector
            def _(dve):
                ch = Chain(dve, chain_s)
                a = R.scores[:, :, 0:C]

                def wide(ap):
                    return ap.unsqueeze(2).to_broadcast([P, T, C])
                ch.link(nc.vector.tensor_reduce(mean[:], a, AX_X, ALU.add))
                ch.link(nc.vector.tensor_scalar(mean[:], mean[:], 1.0 / C, None, ALU.mult))
                ch.link(nc.vector.tensor_tensor(c[:], a, wide(mean[:, :]), ALU.subtract))
                ch.link(nc.vector.tensor_tensor(sq[:], c[:], c[:], ALU.mult))
                ch.link(nc.vector.tensor_reduce(mean[:], sq[:], AX_X, ALU.add))
                nc.vector.tensor_scalar(mean[:], mean[:], 1.0 / C, EPS, ALU.mult, ALU.add).then_inc(var_ready, 1)
                dve.wait_ge(root_ready, 1)
                dve.wait_ge(loaded, 32)
                ch.link(nc.vector.reciprocal(mean[:], mean[:]))
                ch.link(nc.vector.tensor_tensor(c[:], c[:], wide(mean[:, :]), ALU.mult))
                ch.link(nc.vector.tensor_tensor(c[:], c[:], gb[:, 0:1, :].to_broadcast([P, T, C]), ALU.mult))
                ch.link(nc.vector.tensor_tensor(c[:], c[:], gb[:, 1:2, :].to_broadcast([P, T, C]), ALU.add))
                s0 = R.scores[:, :, 0:E]
                ch.link(nc.vector.tensor_tensor(s0, c[:, :, 0:E], c[:, :, E:2 * E], ALU.add))
                for h in range(2, HEADS):
                    ch.link(nc.vector.tensor_tensor(s0, s0, c[:, :, h * E:(h + 1) * E], ALU.add))
                ch.link(nc.vector.tensor_scalar(s0, s0, 1.0 / HEADS, None, ALU.mult))


def l2_ffn(nc, R, A, routes):
    E = 4
    ends = A["L2_ffn_edge_index"]
    count_edges(nc, R, "cnt2", ends[0], ends[1], ends.shape[1], routes)
    layernorm_T(nc, R, "l2f_ln", R.x)
    gat(nc, R, "l2f", routes, A["L2_ffn_W_gat"], A["L2_ffn_att_src"], A["L2_ffn_att_dst"], A["L2_ffn_b_gat"], E,
        "scores", self_loops=True)
    router_scores(nc, R, "l2f_scores", A["L2_ffn_ln_gamma"], A["L2_ffn_ln_beta"], E)
    top2_gates(nc, R, "l2f_gates", E, False)
    layernorm_T(nc, R, "l2f_ln2", R.x)
    experts(nc, R, "l2f_experts", E, 2 * D, A["L2_ffn_W1"], A["L2_ffn_b1"], A["L2_ffn_W2"], A["L2_ffn_b2"], False)


SH = 8
SG = 64
SD = 64
INNER = SH * SD
PAIRS = SH // 2


def slice_weights(nc, R, name, A, S):
    with Stage(nc, name) as st:
        wx = st.sb("wx", [P, NC, INNER])
        wxT = st.sb("wxT", [P, PAIRS, D])
        bd = st.sb("bd_slice", [P, P])
        bx = st.sb("bx", [P, PAIRS])
        bs = st.sb("b_slice", [1, SG])
        rt = st.sb("temp", [P, SH])
        pt = st.ps("pt", [P, PAIRS, 512])
        pw = st.ps("pw", [P, NC, 512])
        pb = st.ps("pb", [P, 512])
        zeroed = st.sem("bd_zeroed")
        loaded = st.sem("weights_loaded")
        turned = st.sem("wx_turned")
        copied = st.sem("wx_copied")
        multiplied = st.sem("multiplied")
        chain_s = st.sem("dve_chain")
        with st.block() as block:
            @block.gpsimd
            def _(pool):
                nc.gpsimd.memset(bd[:], 0.0).then_inc(zeroed, 1)

            @block.sync
            def _(sp):
                sp.dma_start(wx[:], A["L1_ffn_W_x"].rearrange("(c p) n -> p c n", p=P)).then_inc(loaded, 16)
                sp.dma_start(bx[:], A["L1_ffn_b_x"].rearrange("(k p) -> p k", p=P), allow_slow_non_contiguous=True
                             ).then_inc(loaded, 16)
                sp.dma_start(bs[:], row(A["L1_ffn_b_slice"])).then_inc(loaded, 16)
                sp.dma_start(rt[:], A["L1_ffn_temperature"].rearrange("a h b c -> a (h b c)").to_broadcast([P, SH])
                             ).then_inc(loaded, 16)
                sp.wait_ge(zeroed, 1)
                for k in range(2):
                    sp.dma_start(bd[k * SD:(k + 1) * SD, k * SG:(k + 1) * SG], A["L1_ffn_W_slice"]
                                 ).then_inc(loaded, 16)

            @block.tensor
            def _(pe):
                pe.wait_ge(loaded, 96)
                for k in range(PAIRS):
                    for c in range(NC):
                        ins = nc.tensor.transpose(pt[:, k, c * P:(c + 1) * P], wx[:, c, k * P:(k + 1) * P],
                                                  R.ident[:])
                ins.then_inc(turned, 1)
                pe.wait_ge(copied, 1)
                for k in range(PAIRS):
                    for c in range(NC):
                        nc.tensor.matmul(pw[:, c, k * P:(k + 1) * P], wxT[:, k, c * P:(c + 1) * P], bd[:],
                                         start=True, stop=True)
                    ins = nc.tensor.matmul(pb[0:1, k * P:(k + 1) * P], bx[:, k:k + 1], bd[:], start=True, stop=True)
                ins.then_inc(multiplied, 1)

            @block.vector
            def _(dve):
                ch = Chain(dve, chain_s)
                dve.wait_ge(turned, 1)
                nc.vector.tensor_copy(wxT[:], pt[:, :, 0:D]).then_inc(copied, 1)
                dve.wait_ge(loaded, 96)
                ch.link(nc.vector.tensor_scalar(rt[:], rt[:], 0.1, 5.0, ALU.max, ALU.min))
                ch.link(nc.vector.reciprocal(rt[:], rt[:]))
                dve.wait_ge(multiplied, 1)
                for c in range(NC):
                    ins = nc.vector.tensor_tensor(S.wc[:, c, :].rearrange("p (h g) -> p h g", h=SH),
                                                  pw[:, c, :].rearrange("p (h g) -> p h g", h=SH),
                                                  rt[:, :].unsqueeze(2).to_broadcast([P, SH, SG]), ALU.mult)
                cb = S.cb[:, :].rearrange("p (h g) -> p h g", h=SH)
                ch.link(nc.vector.tensor_tensor(cb, pb[0:1, :].rearrange("p (h g) -> p h g", h=SH),
                                                bs[:, :].unsqueeze(1).to_broadcast([1, SH, SG]), ALU.add))
                ch.link(nc.vector.tensor_tensor(cb, cb, rt[0:1, :].unsqueeze(2).to_broadcast([1, SH, SG]), ALU.mult))


def slice_tokens(nc, R, name, A, S):
    with Stage(nc, name) as st:
        wf = st.sb("wf", [P, NC, INNER])
        bf = st.sb("bf", [1, INNER])
        xs = st.sb("xs", [P, 2, NC, P])
        zero = st.sb("zero", [P, P])
        top = st.sb("top", [P, 2, SH])
        total = st.sb("total", [P, 2, SH])
        sw = st.sb("sw", [P, 2, SH, SG])
        fx = st.sb("fx", [P, 2, PAIRS, P + 1])
        pl = st.ps("pl", [P, 512])
        pf = st.ps("pf", [P, 2, 512])
        pt = st.ps("pt", [P, 2, 512])
        pa = st.ps("pa", [P, 2, 512])
        loaded = st.sem("weights_loaded")
        const = st.sem("constants_set")
        staged = st.sem("tile_staged")
        logits = st.sem("logits_ready")
        logits_read = st.sem("logits_read")
        fx_ready = st.sem("fx_ready")
        fx_copied = st.sem("fx_copied")
        shifted = st.sem("shifted")
        exp_ready = st.sem("exp_ready")
        sw_ready = st.sem("slice_weights_ready")
        sw_turned = st.sem("slice_weights_turned")
        swT_copied = st.sem("turned_copied")
        summed = st.sem("tile_summed")
        done = st.sem("sums_done")
        chain_s = st.sem("dve_chain")
        with st.block() as block:
            @block.sync
            def _(sp):
                sp.dma_start(wf[:], A["L1_ffn_W_fx"].rearrange("(c p) n -> p c n", p=P)).then_inc(loaded, 16)
                sp.dma_start(bf[:], row(A["L1_ffn_b_fx"])).then_inc(loaded, 16)

            @block.gpsimd
            def _(pool):
                nc.gpsimd.memset(zero[:], 0.0).then_inc(const, 1)
                nc.gpsimd.memset(fx[:], 1.0).then_inc(const, 1)

                def tile(it, b):
                    pool.wait_ge(fx_ready, it + 1)
                    nc.gpsimd.tensor_copy(xs[:, b], R.xt[:, :, ds(it * P, P)]).then_inc(staged, 1)
                tile(0, 0)
                with pool.Fori(0, T // 2) as g:
                    tile(g * 2 + 1, 1)
                    tile(g * 2 + 2, 0)

            @block.tensor
            def _(pe):
                pe.sem_inc(fx_ready, 2)
                pe.sem_inc(summed, 2)
                pe.wait_ge(loaded, 32)
                pe.wait_ge(const, 2)
                for k in range(2):
                    nc.tensor.matmul(pa[:, k, 0:2 * (P + 1)], zero[:],
                                     fx[:, 0, 0:2, :].rearrange("p k c -> p (k c)"), start=True, stop=False,
                                     skip_group_check=True)

                def project_tile(it, b):
                    pe.wait_ge(staged, it + 1)
                    pe.wait_ge(logits_read, it + 1)
                    for c in range(NC):
                        nc.tensor.matmul(pl[:], xs[:, b, c], S.wc[:, c, :], start=(c == 0), stop=False)
                    nc.tensor.matmul(pl[:], R.ones[0:1, :], S.cb[:], start=False, stop=True).then_inc(logits, 1)
                    pe.wait_ge(fx_copied, it + 1)
                    for c in range(NC):
                        nc.tensor.matmul(pf[:, b], xs[:, b, c], wf[:, c, :], start=(c == 0), stop=False)
                    nc.tensor.matmul(pf[:, b], R.ones[0:1, :], bf[:], start=False, stop=True).then_inc(fx_ready, 1)

                def sum_tile(it, b):
                    pe.wait_ge(sw_ready, it + 1)
                    pe.wait_ge(swT_copied, it + 1)
                    for k in range(PAIRS):
                        ins = nc.tensor.transpose(pt[:, b, k * P:(k + 1) * P],
                                                  sw[:, b, 2 * k:2 * k + 2, :].rearrange("p h g -> p (h g)"),
                                                  R.ident[:])
                    ins.then_inc(sw_turned, 1)
                    pe.wait_ge(fx_copied, it + 3)
                    for k in range(PAIRS):
                        o = (k % 2) * (P + 1)
                        ins = nc.tensor.matmul(pa[:, k // 2, o:o + P + 1],
                                               sw[:, b, 2 * k:2 * k + 2, :].rearrange("p h g -> p (h g)"),
                                               fx[:, b, k, :], start=False, stop=False, skip_group_check=True)
                    ins.then_inc(summed, 1)

                def tile(it, b):
                    project_tile(it, b)
                    sum_tile(it, b)

                tile(0, 0)
                with pe.Fori(0, T // 2) as g:
                    tile(g * 2 + 1, 1)
                    tile(g * 2 + 2, 0)
                for k in range(2):
                    ins = nc.tensor.matmul(pa[:, k, 0:2 * (P + 1)], zero[:],
                                           fx[:, 0, 0:2, :].rearrange("p k c -> p (k c)"), start=False, stop=True,
                                           skip_group_check=True)
                ins.then_inc(done, 1)

            @block.scalar
            def _(act):
                act.sem_inc(fx_copied, 2)
                act.sem_inc(swT_copied, 2)
                act.wait_ge(const, 2)

                def tile(it, b):
                    act.wait_ge(fx_ready, it + 3)
                    act.wait_ge(summed, it + 1)
                    nc.scalar.activation(fx[:, b, :, 0:P], pf[:, b].rearrange("p (k c) -> p k c", k=PAIRS), ACT.Copy
                                         ).then_inc(fx_copied, 1)
                    act.wait_ge(shifted, it + 1)
                    nc.scalar.activation(sw[:, b], sw[:, b], ACT.Exp).then_inc(exp_ready, 1)
                    act.wait_ge(sw_turned, it + 1)
                    nc.scalar.activation(S.swT[:, :, ds(it * P, P)], pt[:, b].rearrange("p (k n) -> p k n", k=PAIRS),
                                         ACT.Copy).then_inc(swT_copied, 1)
                tile(0, 0)
                with act.Fori(0, T // 2) as g:
                    tile(g * 2 + 1, 1)
                    tile(g * 2 + 2, 0)

            @block.vector
            def _(dve):
                ch = Chain(dve, chain_s)
                dve.sem_inc(logits_read, 1)

                def tile(it, b):
                    lg = pl[:].rearrange("p (h g) -> p h g", h=SH)
                    dve.wait_ge(logits, it + 1)
                    ch.link(nc.vector.tensor_reduce(top[:, b], lg, AX_X, ALU.max))
                    dve.wait_ge(summed, it + 1)
                    nc.vector.tensor_tensor(sw[:, b], lg, top[:, b].unsqueeze(2).to_broadcast([P, SH, SG]),
                                            ALU.subtract).then_inc(shifted, 1)
                    dve.wait_ge(shifted, it + 1)
                    dve.sem_inc(logits_read, 1)
                    dve.wait_ge(exp_ready, it + 1)
                    ch.link(nc.vector.tensor_reduce(total[:, b], sw[:, b], AX_X, ALU.add))
                    ch.link(nc.vector.reciprocal(total[:, b], total[:, b]))
                    ch.link(nc.vector.tensor_scalar(total[:, b], total[:, b], R.valid[:, ds(it, 1)], None, ALU.mult))
                    nc.vector.tensor_tensor(sw[:, b], sw[:, b], total[:, b].unsqueeze(2).to_broadcast([P, SH, SG]),
                                            ALU.mult).then_inc(sw_ready, 1)
                tile(0, 0)
                with dve.Fori(0, T // 2) as g:
                    ch.loop(g, 8)
                    tile(g * 2 + 1, 1)
                    tile(g * 2 + 2, 0)
                ch.end(T // 2)
                dve.wait_ge(done, 1)
                for k in range(PAIRS):
                    o = (k % 2) * (P + 1)
                    ins = nc.vector.tensor_copy(S.tok[:, k, :], pa[:, k // 2, o:o + P + 1])
                ch.link(ins)


def slice_attention(nc, R, name, A, S):
    SCALE = float(SD) ** -0.5
    with Stage(nc, name) as st:
        bd = st.sb("bd", [P, P])
        off = st.sb("off", [P, P])
        w3 = st.sb("w_qkv", [P, 3, P])
        wo = st.sb("wo", [P, PAIRS, D])
        nrm = st.sb("norm", [P, PAIRS])
        tb = st.sb("tokens", [P, PAIRS, P])
        tT = st.sb("tokens_T", [P, PAIRS, P])
        qT = st.sb("qT", [P, PAIRS, P])
        kT = st.sb("kT", [P, PAIRS, P])
        v = st.sb("v", [P, PAIRS, P])
        at = st.sb("attn", [P, PAIRS, P])
        top = st.sb("top", [P, PAIRS])
        aT = st.sb("attn_T", [P, PAIRS, P])
        oT = st.sb("out_T", [P, PAIRS, P])
        ps = st.ps("ps", [P, 6, 512])
        pz = st.ps("pz", [P, 2, 512])
        zeroed = st.sem("zeroed")
        loaded = st.sem("weights_loaded")
        made = st.sem("mask_made")
        pe_done = st.sem("pe_step_done")
        dve_done = st.sem("dve_step_done")
        exp_ready = st.sem("exp_ready")
        chain_s = st.sem("dve_chain")

        def four(bank):
            return ps[:, bank, :].rearrange("p (k c) -> p k c", k=PAIRS)

        with st.block() as block:
            @block.gpsimd
            def _(pool):
                nc.gpsimd.memset(w3[:], 0.0).then_inc(zeroed, 1)
                nc.gpsimd.memset(bd[:], 1.0).then_inc(made, 1)
                pool.wait_ge(made, 1)
                nc.gpsimd.affine_select(out=bd[:, SG:P], in_=bd[:, SG:P], compare_op=ALU.is_ge, fill=0.0, base=-SG,
                                        pattern=[[0, SG]], channel_multiplier=1).then_inc(made, 1)
                nc.gpsimd.affine_select(out=bd[:, 0:SG], in_=bd[:, 0:SG], compare_op=ALU.is_gt, fill=0.0, base=SG,
                                        pattern=[[0, SG]], channel_multiplier=-1).then_inc(made, 1)

            @block.sync
            def _(sp):
                sp.dma_start(wo[:], A["L1_ffn_W_out"].rearrange("(k p) d -> p k d", p=P)).then_inc(loaded, 16)
                sp.wait_ge(zeroed, 1)
                for i, w in enumerate(("L1_ffn_W_q", "L1_ffn_W_k", "L1_ffn_W_v")):
                    for h in range(2):
                        sp.dma_start(w3[h * SD:(h + 1) * SD, i, h * SD:(h + 1) * SD], A[w]).then_inc(loaded, 16)

            @block.tensor
            def _(pe):
                pe.wait_ge(dve_done, 1)
                for k in range(PAIRS):
                    ins = nc.tensor.transpose(ps[:, 0, k * P:(k + 1) * P], tb[:, k], R.ident[:])
                ins.then_inc(pe_done, 1)
                pe.wait_ge(loaded, 16 * 7)
                pe.wait_ge(dve_done, 2)
                for k in range(PAIRS):
                    nc.tensor.matmul(ps[:, 1, k * P:(k + 1) * P], w3[:, 0], tT[:, k], start=True, stop=True)
                    nc.tensor.matmul(ps[:, 2, k * P:(k + 1) * P], w3[:, 1], tT[:, k], start=True, stop=True)
                    ins = nc.tensor.matmul(ps[:, 3, k * P:(k + 1) * P], tT[:, k], w3[:, 2], start=True, stop=True)
                ins.then_inc(pe_done, 1)
                pe.wait_ge(dve_done, 3)
                for k in range(PAIRS):
                    ins = nc.tensor.matmul(ps[:, 4, k * P:(k + 1) * P], qT[:, k], kT[:, k], start=True, stop=True)
                ins.then_inc(pe_done, 1)
                pe.wait_ge(dve_done, 4)
                for k in range(PAIRS):
                    ins = nc.tensor.transpose(ps[:, 5, k * P:(k + 1) * P], at[:, k], R.ident[:])
                ins.then_inc(pe_done, 1)
                pe.wait_ge(dve_done, 5)
                for k in range(PAIRS):
                    ins = nc.tensor.matmul(ps[:, 0, k * P:(k + 1) * P], v[:, k], aT[:, k], start=True, stop=True)
                ins.then_inc(pe_done, 1)
                pe.wait_ge(dve_done, 6)
                for k in range(PAIRS):
                    ins = nc.tensor.matmul(pz[:, k // 2, (k % 2) * D:(k % 2 + 1) * D], oT[:, k], wo[:, k], start=True,
                                           stop=True)
                ins.then_inc(pe_done, 1)

            @block.scalar
            def _(act):
                act.wait_ge(made, 4)
                nc.scalar.activation(at[:], at[:], ACT.Exp).then_inc(exp_ready, 1)

            @block.vector
            def _(dve):
                ch = Chain(dve, chain_s)
                dve.wait_ge(made, 3)
                ch.link(nc.vector.tensor_scalar(off[:], bd[:], -1.0, BIG, ALU.add, ALU.mult))
                ch.link(nc.vector.tensor_scalar(nrm[:], S.tok[:, :, P], 1e-5, None, ALU.add))
                ch.link(nc.vector.reciprocal(nrm[:], nrm[:]))
                ch.link(nc.vector.tensor_tensor(tb[:], S.tok[:, :, 0:P], nrm[:, :].unsqueeze(2).to_broadcast([P, PAIRS, P]),
                                                ALU.mult))
                nc.vector.tensor_tensor(tb[:], tb[:], bd[:, :].unsqueeze(1).to_broadcast([P, PAIRS, P]), ALU.mult
                                        ).then_inc(dve_done, 1)
                dve.wait_ge(pe_done, 1)
                nc.vector.tensor_copy(tT[:], four(0)).then_inc(dve_done, 1)
                dve.wait_ge(pe_done, 2)
                nc.vector.tensor_copy(qT[:], four(1))
                nc.vector.tensor_copy(kT[:], four(2))
                nc.vector.tensor_copy(v[:], four(3)).then_inc(dve_done, 1)
                dve.wait_ge(pe_done, 3)
                ch.link(nc.vector.tensor_scalar(at[:], four(4), SCALE, None, ALU.mult))
                ch.link(nc.vector.tensor_tensor(at[:], at[:], off[:, :].unsqueeze(1).to_broadcast([P, PAIRS, P]),
                                                ALU.add))
                ch.link(nc.vector.tensor_reduce(top[:], at[:], AX_X, ALU.max))
                nc.vector.tensor_tensor(at[:], at[:], top[:, :].unsqueeze(2).to_broadcast([P, PAIRS, P]), ALU.subtract
                                        ).then_inc(made, 1)
                dve.wait_ge(exp_ready, 1)
                ch.link(nc.vector.tensor_reduce(top[:], at[:], AX_X, ALU.add))
                ch.link(nc.vector.reciprocal(top[:], top[:]))
                nc.vector.tensor_tensor(at[:], at[:], top[:, :].unsqueeze(2).to_broadcast([P, PAIRS, P]), ALU.mult
                                        ).then_inc(dve_done, 1)
                dve.wait_ge(pe_done, 4)
                nc.vector.tensor_copy(aT[:], four(5)).then_inc(dve_done, 1)
                dve.wait_ge(pe_done, 5)
                nc.vector.tensor_copy(oT[:], four(0)).then_inc(dve_done, 1)
                dve.wait_ge(pe_done, 6)
                nc.vector.tensor_copy(S.z[:].rearrange("p (a k) d -> p a k d", a=2),
                                      pz[:, :, :].rearrange("p a (k d) -> p a k d", k=2)).then_inc(dve_done, 1)
                dve.wait_ge(dve_done, 7)


def slice_spread(nc, R, name, A, S):
    with Stage(nc, name) as st:
        bo = st.sb("bo", [1, D])
        ss = st.sb("sw_staged", [P, U, PAIRS, P])
        po = st.ps("po", [P, U, 512])
        loaded = st.sem("bias_loaded")
        staged = st.sem("tile_staged")
        out_ready = st.sem("out_ready")
        added = st.sem("tile_added")
        with st.block() as block:
            @block.sync
            def _(sp):
                sp.dma_start(bo[:], row(A["L1_ffn_b_out"])).then_inc(loaded, 16)

            @block.scalar
            def _(act):
                with act.Fori(0, G) as g:
                    for u in range(U):
                        act.wait_ge(out_ready, g * U + u + 1)
                        nc.scalar.activation(ss[:, u], S.swT[:, :, ds((g * U + u) * P, P)], ACT.Copy
                                             ).then_inc(staged, 1)

            @block.tensor
            def _(pe):
                pe.sem_inc(out_ready, U)
                pe.wait_ge(loaded, 16)
                with pe.Fori(0, G) as g:
                    for u in range(U):
                        pe.wait_ge(staged, g * U + u + 1)
                        pe.wait_ge(added, g * U + u + 1)
                        for k in range(PAIRS):
                            nc.tensor.matmul(po[:, u, 0:D], ss[:, u, k], S.z[:, k], start=(k == 0), stop=False)
                        nc.tensor.matmul(po[:, u, 0:D], R.ones[0:1, :], bo[:], start=False, stop=True
                                         ).then_inc(out_ready, 1)

            @block.vector
            def _(dve):
                dve.sem_inc(added, U)
                with dve.Fori(0, G) as g:
                    for u in range(U):
                        xi = R.x[:, ds(g * U + u, 1), :].rearrange("p a d -> p (a d)")
                        dve.wait_ge(out_ready, g * U + u + 1 + U)
                        nc.vector.tensor_tensor(xi, xi, po[:, u, 0:D], ALU.add).then_inc(added, 1)


def l1_ffn(nc, R, A):
    class S:
        pass
    layernorm_T(nc, R, "l1f_ln", R.x)
    with ExitStack() as ctx:
        def sb(name, shape):
            return ctx.enter_context(nc.sbuf_tensor("l1f_" + name, shape, F32))
        S.wc = sb("wc", [P, NC, INNER])
        S.cb = sb("cb", [1, INNER])
        S.swT = sb("swT", [P, PAIRS, NP])
        S.tok = sb("tok", [P, PAIRS, P + 1])
        S.z = sb("z", [P, PAIRS, D])
        slice_weights(nc, R, "l1f_w", A, S)
        slice_tokens(nc, R, "l1f_tok", A, S)
        slice_attention(nc, R, "l1f_att", A, S)
        slice_spread(nc, R, "l1f_out", A, S)


NT = 4
RELS = 8
DK = D // HEADS
STREAMS = 4
ROW = D + 2 * HEADS


def node_types(nc, R, name, node_type, skip, S):
    with Stage(nc, name) as st:
        nt = st.sb("nt", [P, T], I32)
        sk = st.sb("skip", [P, NT])
        zeroed = st.sem("nt_zeroed")
        loaded = st.sem("loaded")
        sig_ready = st.sem("sigmoid_ready")
        chain_s = st.sem("dve_chain")
        with st.block() as block:
            @block.gpsimd
            def _(pool):
                nc.gpsimd.memset(nt[:], 0).then_inc(zeroed, 1)

            @block.sync
            def _(sp):
                sp.dma_start(sk[:], row(skip).to_broadcast([P, NT])).then_inc(loaded, 16)
                sp.wait_ge(zeroed, 1)
                sp.dma_start(nt[:, 0:T - 1], node_type[0:(T - 1) * P].rearrange("(t p) -> p t", p=P),
                             allow_slow_non_contiguous=True).then_inc(loaded, 16)
                sp.dma_start(nt[0:LAST, T - 1:T], col(node_type[(T - 1) * P:N])).then_inc(loaded, 16)

            @block.scalar
            def _(act):
                act.wait_ge(loaded, 48)
                nc.scalar.activation(sk[:], sk[:], ACT.Sigmoid).then_inc(sig_ready, 1)

            @block.vector
            def _(dve):
                ch = Chain(dve, chain_s)
                dve.wait_ge(loaded, 48)
                for k in range(NT):
                    ins = nc.vector.tensor_scalar(S.oh[:, :, k], nt[:], float(k), None, ALU.is_equal)
                ch.link(ins)
                dve.wait_ge(sig_ready, 1)
                ch.link(nc.vector.tensor_tensor(S.ohg[:], S.oh[:], sk[:, :].unsqueeze(1).to_broadcast([P, T, NT]),
                                                ALU.mult))


def typed_project(nc, R, name, W, oh, dst, add):
    with Stage(nc, name) as st:
        ws = st.sb("W", [P, NC, NT, D])
        xs = st.sb("xs", [P, 2, NC, P])
        pt = st.ps("pt", [P, 2, NT // 2, 512])
        loaded = st.sem("weights_loaded")
        staged = st.sem("tile_staged")
        multiplied = st.sem("tile_multiplied")
        chosen = st.sem("tile_chosen")
        chain_s = st.sem("dve_chain")
        with st.block() as block:
            @block.sync
            def _(sp):
                for c in range(NC):
                    sp.dma_start(ws[:, c], W[:, c * P:(c + 1) * P, :].rearrange("t p n -> p t n")
                                 ).then_inc(loaded, 16)

            @block.scalar
            def _(act):
                def tile(it, b):
                    act.wait_ge(multiplied, it + 1)
                    nc.scalar.activation(xs[:, b], R.xt[:, :, ds(it * P, P)], ACT.Copy).then_inc(staged, 1)
                tile(0, 0)
                with act.Fori(0, T // 2) as g:
                    tile(g * 2 + 1, 1)
                    tile(g * 2 + 2, 0)

            @block.tensor
            def _(pe):
                pe.sem_inc(multiplied, 2)
                pe.wait_ge(loaded, 16 * NC)

                def tile(it, b):
                    pe.wait_ge(staged, it + 1)
                    pe.wait_ge(chosen, it + 1)
                    for k in range(NT // 2):
                        for c in range(NC):
                            ins = nc.tensor.matmul(pt[:, b, k], xs[:, b, c],
                                                   ws[:, c, 2 * k:2 * k + 2, :].rearrange("p t n -> p (t n)"),
                                                   start=(c == 0), stop=(c == NC - 1))
                    ins.then_inc(multiplied, 1)
                tile(0, 0)
                with pe.Fori(0, T // 2) as g:
                    tile(g * 2 + 1, 1)
                    tile(g * 2 + 2, 0)

            @block.vector
            def _(dve):
                ch = Chain(dve, chain_s)
                dve.sem_inc(chosen, 2)

                def tile(it, b):
                    o = dst[:, ds(it, 1), :].rearrange("p a d -> p (a d)")
                    dve.wait_ge(multiplied, it + 3)
                    for k in range(NT):
                        y = pt[:, b, k // 2, (k % 2) * D:(k % 2 + 1) * D]
                        f = oh[:, ds(it, 1), k]
                        if k == 0 and not add:
                            ch.link(nc.vector.tensor_scalar(o, y, f, None, ALU.mult))
                        else:
                            ch.link(nc.vector.scalar_tensor_tensor(out=o, in0=y, scalar=f, in1=o, op0=ALU.mult,
                                                                   op1=ALU.add))
                    dve.sem_inc(chosen, 1)
                tile(0, 0)
                with dve.Fori(0, T // 2) as g:
                    ch.loop(g, 2 * NT)
                    tile(g * 2 + 1, 1)
                    tile(g * 2 + 2, 0)
                ch.end(T // 2)


def relation_table(nc, R, name, rel, pri, extra, dram):
    C = D + (D if extra is not None else 0)
    with Stage(nc, name) as st:
        bd = st.sb("bd", [P, NC, RELS, P])
        pr = st.sb("pri", [P, RELS * HEADS])
        xs = st.sb("xs", [P, 2, NC, P])
        ot = st.sb("rows", [P, 2, RELS, C])
        pt = st.ps("pt", [P, 2 * NC * 2, 512])
        zeroed = st.sem("bd_zeroed")
        loaded = st.sem("weights_loaded")
        scaled = st.sem("weights_scaled")
        staged = st.sem("tile_staged")
        multiplied = st.sem("tile_multiplied")
        copied = st.sem("tile_copied")
        extra_copied = st.sem("extra_copied")
        slot_free = st.sem("rows_slot_free")
        admitted = st.sem("store_admitted")
        stored = [st.sem("rows_stored0"), st.sem("rows_stored1")]
        chain_s = st.sem("dve_chain")
        rows = dram[:, :].rearrange("(n r) c -> n (r c)", r=RELS)
        with st.block() as block:
            @block.gpsimd
            def _(pool):
                nc.gpsimd.memset(bd[:], 0.0).then_inc(zeroed, 1)

                def tile(it, b):
                    pool.wait_ge(multiplied, it + 1)
                    nc.gpsimd.tensor_copy(xs[:, b], R.xt[:, :, ds(it * P, P)]).then_inc(staged, 1)
                tile(0, 0)
                with pool.Fori(0, T // 2) as g:
                    tile(g * 2 + 1, 1)
                    tile(g * 2 + 2, 0)

            @block.sync
            def _(sp):
                sp.dma_start(pr[:], row(pri.rearrange("r h -> (r h)")).to_broadcast([P, RELS * HEADS])
                             ).then_inc(loaded, 16)
                sp.wait_ge(zeroed, 1)
                for h in range(HEADS):
                    lo = (h % 2) * DK
                    sp.dma_start(bd[lo:lo + DK, h // 2, :, lo:lo + DK], rel[:, h].rearrange("r d e -> d r e")
                                 ).then_inc(loaded, 16)

                def tile(it, k, b):
                    sp.wait_ge(copied, it + 3)
                    if extra is not None:
                        sp.sem_inc(admitted, 1)
                        sp.wait_ge(extra_copied, it + 1)
                    sp.sem_inc(admitted, 1)
                    sp.dma_start(rows[ds(it * P, P), :], ot[:, b].rearrange("p r c -> p (r c)")
                                 ).then_inc(stored[b], 16)
                    sp.wait_ge(stored[b], k * 16 + 16)
                    sp.sem_inc(slot_free, 1)
                tile(0, 0, 0)
                with sp.Fori(0, T // 2) as g:
                    tile(g * 2 + 1, g, 1)
                    tile(g * 2 + 2, g + 1, 0)

            @block.tensor
            def _(pe):
                pe.sem_inc(multiplied, 2)
                pe.wait_ge(scaled, 1)

                def tile(it, b):
                    pe.wait_ge(staged, it + 1)
                    pe.wait_ge(copied, it + 1)
                    for c in range(NC):
                        for k in range(2):
                            ins = nc.tensor.matmul(pt[:, b * 4 + c * 2 + k, :], xs[:, b, c],
                                                   bd[:, c, 4 * k:4 * k + 4, :].rearrange("p r n -> p (r n)"),
                                                   start=True, stop=True)
                    ins.then_inc(multiplied, 1)
                tile(0, 0)
                with pe.Fori(0, T // 2) as g:
                    tile(g * 2 + 1, 1)
                    tile(g * 2 + 2, 0)

            @block.scalar
            def _(act):
                act.sem_inc(copied, 2)
                act.sem_inc(slot_free, 2)

                def tile(it, b):
                    act.wait_ge(multiplied, it + 3)
                    act.wait_ge(slot_free, it + 1)
                    for c in range(NC):
                        for k in range(2):
                            ins = nc.scalar.activation(ot[:, b, 4 * k:4 * k + 4, c * P:(c + 1) * P],
                                                       pt[:, b * 4 + c * 2 + k, :].rearrange("p (r n) -> p r n", r=4),
                                                       ACT.Copy)
                    ins.then_inc(copied, 1)
                tile(0, 0)
                with act.Fori(0, T // 2) as g:
                    tile(g * 2 + 1, 1)
                    tile(g * 2 + 2, 0)

            @block.vector
            def _(dve):
                ch = Chain(dve, chain_s)
                dve.wait_ge(loaded, 16 * (1 + HEADS))
                if extra is None:
                    ch.link(nc.vector.tensor_scalar(pr[:], pr[:], float(DK) ** -0.5, None, ALU.mult))
                    prv = pr[:, :].rearrange("p (r h) -> p r h", h=HEADS)
                    for h in range(HEADS):
                        lo = (h % 2) * DK
                        blk = bd[lo:lo + DK, h // 2, :, lo:lo + DK]
                        ins = nc.vector.tensor_tensor(blk, blk, prv[lo:lo + DK, :, h].unsqueeze(2)
                                                      .to_broadcast([DK, RELS, DK]), ALU.mult)
                    ch.link(ins)
                dve.sem_inc(scaled, 1)
                if extra is not None:
                    def tile(it, b):
                        dve.wait_ge(slot_free, it + 1)
                        nc.vector.tensor_copy(ot[:, b, :, D:C], extra[:, ds(it, 1), :].to_broadcast([P, RELS, D])
                                              ).then_inc(extra_copied, 1)
                    tile(0, 0)
                    with dve.Fori(0, T // 2) as g:
                        tile(g * 2 + 1, 1)
                        tile(g * 2 + 2, 0)


def clear_sums(nc, R, name, sums):
    with Stage(nc, name) as st:
        init = st.sb("init", [P, ROW])
        made = st.sem("init_made")
        stored = st.sem("init_stored")
        with st.block() as block:
            @block.gpsimd
            def _(pool):
                nc.gpsimd.memset(init[:, 0:D + HEADS], 0.0).then_inc(made, 1)
                nc.gpsimd.memset(init[:, D + HEADS:ROW], -BIG).then_inc(made, 1)

            @block.sync
            def _(sp):
                sp.wait_ge(made, 2)
                with sp.Fori(0, T + 1) as t:
                    for k in range(STREAMS):
                        sp.dma_start(sums[k][ds(t * P, P), :], init[:]).then_inc(stored, 16)
                sp.wait_ge(stored, 16 * STREAMS * (T + 1))


def edge_sums(nc, R, name, src, dst, etype, E, qtab, vktab, sums):
    EC = -(-E // P)
    EC += -EC % STREAMS
    full, rest = E // EC, E % EC
    S = STREAMS
    with Stage(nc, name) as st:
        ends = st.sb("ends", [P, 3, EC], I32)
        key = st.sb("key", [P, EC])
        tmp = st.sb("tmp", [P, EC])
        idx_all = st.sb("idx_all", [P, EC, 3], I32)
        spare_i = st.sb("spare_i", [P, 1], I32)
        spare = st.sb("spare", [P, 1])
        idx = st.sb("idx", [P, S, 3], I32)
        widx = st.sb("write_idx", [P, S], I32)
        kb = st.sb("key_wide", [P, S, P])
        eq = st.sb("same", [P, S, P])
        neg = st.sb("neg", [P, S, P])
        low = st.sb("same_earlier", [P, S, P])
        before = st.sb("before", [P, S])
        q = st.sb("q", [P, S, D])
        vk = st.sb("vk", [P, S, 2 * D])
        old = st.sb("old", [P, S, ROW])
        new = st.sb("new", [P, S, ROW])
        prod = st.sb("prod", [P, S, D])
        score = st.sb("score", [P, S, HEADS])
        sw = st.sb("score_wide", [P, S, HEADS, P])
        msk = st.sb("masked", [P, S, HEADS, P])
        top = st.sb("top", [P, S, HEADS])
        ex = st.sb("exponents", [P, S, 2 * HEADS])
        w = st.sb("weighted", [P, S, ROW])
        pk = st.ps("pk", [P, S, 512])
        pr = st.ps("pr", [P, S, 512])
        padded = st.sem("padding_set")
        loaded = st.sem("edges_loaded")
        const = st.sem("spare_made")
        chain_s = st.sem("dve_chain")
        kb_ready = st.sem("key_wide_ready")
        idx_ready = st.sem("idx_ready")
        key_rows = st.sem("key_rows_ready")
        sw_ready = st.sem("score_wide_ready")
        score_rows = st.sem("score_rows_ready")
        ex_ready = st.sem("exponents_ready")
        w_ready = st.sem("weights_ready")
        weighted = st.sem("weighted_ready")
        summed = st.sem("column_summed")
        new_ready = st.sem("new_ready")
        written = st.sem("sum_written")
        admitted = st.sem("pool_admitted")
        rows_gathered = [st.sem(f"rows_gathered{k}") for k in range(S)]
        old_gathered = [st.sem(f"old_gathered{k}") for k in range(S)]
        scattered = [st.sem(f"sum_scattered{k}") for k in range(S)]
        with st.block() as block:
            @block.sync
            def _(sp):
                sp.wait_ge(padded, 3)
                for k, ap in enumerate((src, dst, etype)):
                    sp.dma_start(ends[0:full, k, :], ap[0:full * EC].rearrange("(p k) -> p k", k=EC)
                                 ).then_inc(loaded, 16)
                    sp.dma_start(ends[full:full + 1, k, 0:rest], row(ap[full * EC:E])).then_inc(loaded, 16)

            @block.gpsimd
            def _(pool):
                nc.gpsimd.memset(ends[:, 0], NP - 1).then_inc(padded, 1)
                nc.gpsimd.memset(ends[:, 1], NP - 1).then_inc(padded, 1)
                nc.gpsimd.memset(ends[:, 2], 0).then_inc(padded, 1)
                nc.gpsimd.iota(spare_i[:], pattern=[[0, 1]], base=NP, channel_multiplier=1).then_inc(const, 1)
                with pool.Fori(0, EC // S) as g:
                    for k in range(S):
                        pool.wait_ge(idx_ready, g * S + k + 1)
                        pool.sem_inc(admitted, 1)
                        for slot, (buf, tab, sem) in enumerate(((q, qtab, rows_gathered), (vk, vktab, rows_gathered),
                                                                (old, sums[k], old_gathered))):
                            nc.gpsimd.indirect_dma_start(
                                out=buf[:, k], out_offset=None, in_=tab[:, :],
                                in_offset=bass.IndirectOffsetOnAxis(ap=idx[:, k, slot:slot + 1], axis=0)
                            ).then_inc(sem[k], 16)
                    for k in range(S):
                        pool.wait_ge(new_ready, g * S + k + 1)
                        pool.sem_inc(admitted, 1)
                        nc.gpsimd.indirect_dma_start(
                            out=sums[k][:, :], in_=new[:, k], in_offset=None,
                            out_offset=bass.IndirectOffsetOnAxis(ap=widx[:, k:k + 1], axis=0)
                        ).then_inc(scattered[k], 16)
                    for k in range(S):
                        pool.wait_ge(scattered[k], g * 16 + 16)
                        pool.sem_inc(written, 1)

            @block.tensor
            def _(pe):
                with pe.Fori(0, EC // S) as g:
                    for k in range(S):
                        pe.wait_ge(kb_ready, g * S + k + 1)
                        nc.tensor.transpose(pk[:, k, 0:P], kb[:, k], R.ident[:]).then_inc(key_rows, 1)
                    for k in range(S):
                        pe.wait_ge(sw_ready, g * S + k + 1)
                        for h in range(HEADS):
                            ins = nc.tensor.transpose(pr[:, k, h * P:(h + 1) * P], sw[:, k, h], R.ident[:])
                        ins.then_inc(score_rows, 1)
                    for k in range(S):
                        pe.wait_ge(weighted, g * S + k + 1)
                        nc.tensor.matmul(pk[:, k, P:P + D + HEADS], eq[:, k], w[:, k, 0:D + HEADS], start=True,
                                         stop=True).then_inc(summed, 1)

            @block.scalar
            def _(act):
                with act.Fori(0, EC // S) as g:
                    for k in range(S):
                        act.wait_ge(ex_ready, g * S + k + 1)
                        nc.scalar.activation(w[:, k, D:ROW], ex[:, k], ACT.Exp).then_inc(w_ready, 1)

            @block.vector
            def _(dve):
                ch = Chain(dve, chain_s)
                dve.sem_inc(written, S)
                dve.wait_ge(loaded, 96)
                dve.wait_ge(const, 1)
                ch.link(nc.vector.tensor_copy(spare[:], spare_i[:]))
                ch.link(nc.vector.tensor_copy(key[:], ends[:, 1]))
                for slot, e in ((0, 1), (1, 0)):
                    ch.link(nc.vector.tensor_scalar(tmp[:], ends[:, e], float(RELS), None, ALU.mult))
                    ch.link(nc.vector.tensor_tensor(tmp[:], tmp[:], ends[:, 2], ALU.add))
                    ch.link(nc.vector.tensor_copy(idx_all[:, :, slot], tmp[:]))
                ch.link(nc.vector.tensor_copy(idx_all[:, :, 2], ends[:, 1]))

                def heads(ap):
                    return ap.rearrange("p (h f) -> p h f", h=HEADS)

                with dve.Fori(0, EC // S) as g:
                    ch.loop(g, 10 * S)
                    for k in range(S):
                        n = g * S + k
                        nc.vector.tensor_copy(kb[:, k], key[:, ds(n, 1)].to_broadcast([P, P])).then_inc(kb_ready, 1)
                        nc.vector.tensor_copy(idx[:, k], idx_all[:, ds(n, 1), :].rearrange("p a c -> p (a c)")
                                              ).then_inc(idx_ready, 1)
                    for k in range(S):
                        n = g * S + k
                        kn = key[:, ds(n, 1)]
                        dve.wait_ge(key_rows, n + 1)
                        nc.vector.scalar_tensor_tensor(out=low[:, k], in0=pk[:, k, 0:P], scalar=kn, in1=R.lower[:],
                                                       op0=ALU.is_equal, op1=ALU.mult, accum_out=before[:, k:k + 1])
                        ch.link(nc.vector.tensor_scalar(eq[:, k], pk[:, k, 0:P], kn, None, ALU.is_equal))
                        nc.vector.tensor_scalar(neg[:, k], eq[:, k], -1.0, BIG, ALU.add, ALU.mult)
                        ch.link(nc.vector.tensor_scalar(before[:, k:k + 1], before[:, k:k + 1], 0.5, None, ALU.is_lt))
                        ch.link(nc.vector.scalar_tensor_tensor(out=before[:, k:k + 1], in0=kn, scalar=spare[:],
                                                               in1=before[:, k:k + 1], op0=ALU.subtract,
                                                               op1=ALU.mult))
                        dve.wait_ge(written, n + 1)
                        nc.vector.tensor_scalar(widx[:, k:k + 1], before[:, k:k + 1], spare[:], None, ALU.add)
                        dve.wait_ge(rows_gathered[k], g * 32 + 32)
                        ch.link(nc.vector.tensor_tensor(prod[:, k], q[:, k], vk[:, k, D:2 * D], ALU.mult))
                        ch.link(nc.vector.tensor_reduce(score[:, k], heads(prod[:, k]), AX_X, ALU.add))
                        nc.vector.tensor_copy(sw[:, k], score[:, k].unsqueeze(2).to_broadcast([P, HEADS, P])
                                              ).then_inc(sw_ready, 1)
                    for k in range(S):
                        n = g * S + k
                        dve.wait_ge(score_rows, n + 1)
                        ch.link(nc.vector.tensor_tensor(msk[:, k], pr[:, k].rearrange("p (h n) -> p h n", h=HEADS),
                                                        neg[:, k:k + 1, :].to_broadcast([P, HEADS, P]), ALU.add))
                        ch.link(nc.vector.tensor_reduce(top[:, k], msk[:, k], AX_X, ALU.max))
                        dve.wait_ge(old_gathered[k], g * 16 + 16)
                        mo, mn = old[:, k, D + HEADS:ROW], new[:, k, D + HEADS:ROW]
                        ch.link(nc.vector.tensor_tensor(mn, top[:, k], mo, ALU.max))
                        nc.vector.tensor_tensor(ex[:, k, 0:HEADS], score[:, k], mn, ALU.subtract)
                        nc.vector.tensor_tensor(ex[:, k, HEADS:2 * HEADS], mo, mn, ALU.subtract
                                                ).then_inc(ex_ready, 1)
                    for k in range(S):
                        n = g * S + k
                        dve.wait_ge(w_ready, n + 1)
                        nc.vector.tensor_tensor(heads(w[:, k, 0:D]), heads(vk[:, k, 0:D]),
                                                w[:, k, D:D + HEADS].unsqueeze(2).to_broadcast([P, HEADS, DK]),
                                                ALU.mult).then_inc(weighted, 1)
                        fac = w[:, k, D + HEADS:ROW]
                        nc.vector.tensor_tensor(heads(old[:, k, 0:D]), heads(old[:, k, 0:D]),
                                                fac.unsqueeze(2).to_broadcast([P, HEADS, DK]), ALU.mult)
                        ch.link(nc.vector.tensor_tensor(old[:, k, D:D + HEADS], old[:, k, D:D + HEADS], fac,
                                                        ALU.mult))
                        dve.wait_ge(summed, n + 1)
                        ch.link(nc.vector.tensor_tensor(new[:, k, 0:D + HEADS], old[:, k, 0:D + HEADS],
                                                        pk[:, k, P:P + D + HEADS], ALU.add))
                        dve.sem_inc(new_ready, 1)
                ch.end(EC // S)


def merge_sums(nc, R, name, sums):
    S = STREAMS
    with Stage(nc, name) as st:
        a = st.sb("sums", [P, T, S, ROW])
        m = st.sb("max", [P, T, HEADS])
        ex = st.sb("factor", [P, T, S, HEADS])
        loaded = st.sem("sums_loaded")
        chain_s = st.sem("dve_chain")
        ready = st.sem("exponents_ready")
        exp_ready = st.sem("factors_ready")
        with st.block() as block:
            @block.sync
            def _(sp):
                for k in range(S):
                    sp.dma_start(a[:, :, k, :], sums[k][0:NP, :].rearrange("(t p) c -> p t c", p=P)
                                 ).then_inc(loaded, 16)

            @block.scalar
            def _(act):
                act.wait_ge(ready, 1)
                nc.scalar.activation(ex[:], ex[:], ACT.Exp).then_inc(exp_ready, 1)

            @block.vector
            def _(dve):
                ch = Chain(dve, chain_s)
                dve.wait_ge(loaded, 16 * S)
                mk = [a[:, :, k, D + HEADS:ROW] for k in range(S)]
                ch.link(nc.vector.tensor_tensor(m[:], mk[0], mk[1], ALU.max))
                for k in range(2, S):
                    ch.link(nc.vector.tensor_tensor(m[:], m[:], mk[k], ALU.max))
                for k in range(S):
                    ins = nc.vector.tensor_tensor(ex[:, :, k], mk[k], m[:], ALU.subtract)
                ins.then_inc(ready, 1)
                dve.wait_ge(exp_ready, 1)
                for k in range(S):
                    acc = a[:, :, k, 0:D].rearrange("p t (h f) -> p t h f", h=HEADS)
                    nc.vector.tensor_tensor(acc, acc, ex[:, :, k].unsqueeze(3).to_broadcast([P, T, HEADS, DK]),
                                            ALU.mult)
                    ins = nc.vector.tensor_tensor(a[:, :, k, D:D + HEADS], a[:, :, k, D:D + HEADS], ex[:, :, k],
                                                  ALU.mult)
                ch.link(ins)
                for k in range(1, S):
                    ch.link(nc.vector.tensor_tensor(a[:, :, 0, 0:D + HEADS], a[:, :, 0, 0:D + HEADS],
                                                    a[:, :, k, 0:D + HEADS], ALU.add))
                ch.link(nc.vector.tensor_scalar(m[:], a[:, :, 0, D:D + HEADS], 1e-30, None, ALU.max))
                ch.link(nc.vector.reciprocal(m[:], m[:]))
                ch.link(nc.vector.tensor_tensor(R.xn[:].rearrange("p t (h f) -> p t h f", h=HEADS),
                                                a[:, :, 0, 0:D].rearrange("p t (h f) -> p t h f", h=HEADS),
                                                m[:, :, :].unsqueeze(3).to_broadcast([P, T, HEADS, DK]), ALU.mult))


def l0_gnn(nc, R, A):
    class S:
        pass
    qtab = nc.dram_tensor("hgt_q", [NP * RELS, D], F32).ap()
    vktab = nc.dram_tensor("hgt_vk", [NP * RELS, 2 * D], F32).ap()
    sums = [nc.dram_tensor(f"hgt_sums{k}", [NP + P, ROW], F32).ap() for k in range(STREAMS)]
    with ExitStack() as ctx:
        S.oh = ctx.enter_context(nc.sbuf_tensor("l0g_types", [P, T, NT], F32))
        S.ohg = ctx.enter_context(nc.sbuf_tensor("l0g_types_gated", [P, T, NT], F32))
        node_types(nc, R, "l0g_nt", A["node_type_4"], A["L0_gnn_skip"], S)
        layernorm_T(nc, R, "l0g_ln", R.x)
        with nc.sbuf_tensor("l0g_k", [P, T, D], F32) as kn, nc.sbuf_tensor("l0g_v", [P, T, D], F32) as vn:
            typed_project(nc, R, "l0g_kp", A["L0_gnn_k_linears"], S.oh, kn, False)
            typed_project(nc, R, "l0g_vp", A["L0_gnn_v_linears"], S.oh, vn, False)
            typed_project(nc, R, "l0g_qp", A["L0_gnn_q_linears"], S.oh, R.xn, False)
            layernorm_T(nc, R, "l0g_qT", R.xn, norm=False)
            relation_table(nc, R, "l0g_qr", A["L0_gnn_relation_att"], A["L0_gnn_relation_pri"], None, qtab)
            layernorm_T(nc, R, "l0g_vT", vn, norm=False)
            relation_table(nc, R, "l0g_vr", A["L0_gnn_relation_msg"], A["L0_gnn_relation_pri"], kn, vktab)
        clear_sums(nc, R, "l0g_clear", sums)
        edge_sums(nc, R, "l0g_edges", A["src"], A["dst"], A["edge_type_8"], A["src"].shape[0], qtab, vktab, sums)
        merge_sums(nc, R, "l0g_merge", sums)
        layernorm_T(nc, R, "l0g_aT", R.xn, norm=False)
        typed_project(nc, R, "l0g_ap", A["L0_gnn_a_linears"], S.ohg, R.x, True)


def build(nc, A, out):
    class R:
        pass
    ctx = ExitStack()
    with ctx:
        def sb(name, shape, dt=F32):
            return ctx.enter_context(nc.sbuf_tensor(name, shape, dt))
        R.x = sb("x_all", [P, T, D])
        R.xn = sb("xn_all", [P, T, D])
        R.xt = sb("xt_all", [P, NC, NP])
        R.ident = sb("ident", [P, P])
        R.ones = sb("ones", [P, P])
        R.lower = sb("lower", [P, P])
        R.valid = sb("valid", [P, T])
        R.scores = sb("scores", [P, T, 16])
        R.gates = sb("gates", [P, T, 8])
        R.dis = sb("dis", [P, T])
        R.ad = sb("a_dst_all", [P, T, HEADS])
        R.we = sb("gat_W", [P, NC, D + HEADS])
        R.was = sb("gat_W_src", [P, NC, HEADS, P])
        setup(nc, R, A["x"])
        edges = nc.dram_tensor("edge_counts", [NP * NP + 512, 1], F32).ap()
        count_edges(nc, R, "cnt1", A["src"], A["dst"], A["src"].shape[0], edges)
        l0_gnn(nc, R, A)
        l0_ffn(nc, R, A)
        l1_gnn(nc, R, A, edges)
        l1_ffn(nc, R, A)
        l2_gnn(nc, R, A, edges)
        l2_ffn(nc, R, A, nc.dram_tensor("route_counts", [NP * NP + 512, 1], F32).ap())
        l3_gnn(nc, R, A, edges)
        l3_ffn(nc, R, A)
        store(nc, R, out)


_OUT = (N, D)


def kernel(**inputs):
    import numpy as _np
    import concourse.bacc as _bacc
    from concourse import mybir as _mybir
    from concourse.bass_utils import run_bass_kernel_spmd as _run

    nc = _bacc.Bacc("TRN2", target_bir_lowering=False, num_devices=1)
    arrays, args = {}, {}
    for name in inputs:
        a = _np.ascontiguousarray(inputs[name])
        arrays[f"in_{name}_dram"] = a
        args[name] = nc.dram_tensor(f"in_{name}_dram", a.shape, _mybir.dt.from_np(a.dtype), kind="ExternalInput").ap()
    out = nc.dram_tensor("out_0_dram", _OUT, F32, kind="ExternalOutput").ap()
    build(nc, args, out)
    r = _run(nc, [arrays], core_ids=[0])
    return r.results[0]["out_0_dram"]
```

```python
from contextlib import ExitStack

import concourse.bass as bass
from concourse import mybir

ALU = mybir.AluOpType
ACT = mybir.ActivationFunctionType
F32 = mybir.dt.float32
I32 = mybir.dt.int32
U32 = mybir.dt.uint32
U16 = mybir.dt.uint16
AX_X = mybir.AxisListType.X

P = 128
D = 256
N = 3125
T = (N + P - 1) // P
NP = T * P
NC = D // P
LAST = N - (T - 1) * P
U = 5
G = T // U
EPS = 1e-5
BIG = 1e30

ds = bass.ds


class Stage:

    def __init__(self, nc, name):
        self.nc, self.name = nc, name

    def __enter__(self):
        self.ctx = ExitStack()
        self.sems = []
        self.n = 0
        return self

    def sb(self, name, shape, dt=F32):
        return self.ctx.enter_context(self.nc.sbuf_tensor(f"{self.name}_{name}", shape, dt))

    def ps(self, name, shape, dt=F32):
        return self.ctx.enter_context(self.nc.psum_tensor(f"{self.name}_{name}", shape, dt))

    def sem(self, name):
        s = self.nc.alloc_semaphore(name=f"{self.name}_{name}")
        self.sems.append(s)
        return s

    def block(self):
        return self.nc.Block()

    def __exit__(self, *exc):
        self.ctx.close()
        self.nc.all_engine_barrier()
        self.nc.clear_and_free_semaphores(self.sems)
        self.nc.all_engine_barrier()
        return False


class Chain:

    def __init__(self, eng, sem):
        self.eng, self.sem, self.n, self.base = eng, sem, 0, 0

    def link(self, ins):
        self.n += 1
        ins.then_inc(self.sem, 1)
        self.eng.wait_ge(self.sem, self.base + self.n)

    def loop(self, i, per):
        self.start, self.per = self.base + self.n, per
        self.base, self.n = self.start + i * per, 0

    def end(self, trips):
        assert self.n == self.per, (self.n, self.per)
        self.base, self.n = self.start + trips * self.per, 0


def col(ap):
    return ap.rearrange("(p a) -> p a", a=1)


def row(ap):
    return ap.rearrange("(a n) -> a n", a=1)


def setup(nc, R, x):
    with Stage(nc, "setup") as st:
        loaded = st.sem("x_loaded")
        zeroed = st.sem("tail_zeroed")
        made = st.sem("constants_made")
        with st.block() as block:
            @block.sync
            def _(sp):
                sp.dma_start(R.x[:, 0:T - 1, :], x[0:(T - 1) * P, :].rearrange("(t p) d -> p t d", p=P)
                             ).then_inc(loaded, 16)
                sp.wait_ge(zeroed, 1)
                sp.dma_start(R.x[0:LAST, T - 1, :], x[(T - 1) * P:N, :]).then_inc(loaded, 16)
                sp.wait_ge(loaded, 32)

            @block.gpsimd
            def _(pool):
                nc.gpsimd.memset(R.x[:, T - 1, :], 0.0).then_inc(zeroed, 1)
                nc.gpsimd.memset(R.ident[:], 0.0).then_inc(made, 1)
                nc.gpsimd.memset(R.ones[:], 1.0).then_inc(made, 1)
                nc.gpsimd.memset(R.lower[:], 1.0).then_inc(made, 1)
                nc.gpsimd.memset(R.valid[:], 1.0).then_inc(made, 1)
                nc.gpsimd.memset(R.ad[:, T, :], 0.0).then_inc(made, 1)
                pool.wait_ge(made, 5)
                nc.gpsimd.affine_select(out=R.ident[:], in_=R.ident[:], compare_op=ALU.not_equal, fill=1.0,
                                        base=0, pattern=[[-1, P]], channel_multiplier=1).then_inc(made, 1)
                nc.gpsimd.affine_select(out=R.lower[:], in_=R.lower[:], compare_op=ALU.is_gt, fill=0.0,
                                        base=0, pattern=[[-1, P]], channel_multiplier=1).then_inc(made, 1)
                nc.gpsimd.affine_select(out=R.valid[:], in_=R.valid[:], compare_op=ALU.is_gt, fill=0.0,
                                        base=N, pattern=[[-P, T]], channel_multiplier=-1).then_inc(made, 1)
                pool.wait_ge(made, 8)


def store(nc, R, out):
    with Stage(nc, "store") as st:
        stored = st.sem("out_stored")
        with st.block() as block:
            @block.sync
            def _(sp):
                sp.dma_start(out[0:(T - 1) * P, :].rearrange("(t p) d -> p t d", p=P), R.x[:, 0:T - 1, :]
                             ).then_inc(stored, 16)
                sp.dma_start(out[(T - 1) * P:N, :], R.x[0:LAST, T - 1, :]).then_inc(stored, 16)
                sp.wait_ge(stored, 32)


def layernorm_T(nc, R, name, src, gamma=None, beta=None, norm=True):
    with Stage(nc, name) as st:
        mean = st.sb("mean", [P, T])
        root = st.sb("root", [P, T])
        rstd = st.sb("rstd", [P, T])
        sq = st.sb("sq", [P, T, D]) if norm else None
        xs = st.sb("xs", [P, U, D])
        gb = st.sb("gb", [P, 2, D])
        pt = st.ps("pt", [P, U, 512])
        chain_s = st.sem("dve_chain")
        gb_loaded = st.sem("gb_loaded")
        centred = st.sem("centred")
        squared = st.sem("squared")
        var_ready = st.sem("var_ready")
        root_ready = st.sem("root_ready")
        xn_ready = st.sem("xn_ready")
        staged = st.sem("tile_staged")
        turned = st.sem("tile_transposed")
        copied = st.sem("tile_copied")
        rounds = norm + (gamma is not None)
        with st.block() as block:
            if gamma is not None:
                @block.sync
                def _(sp):
                    sp.dma_start(gb[:, 0, :], row(gamma).to_broadcast([P, D])).then_inc(gb_loaded, 16)
                    sp.dma_start(gb[:, 1, :], row(beta).to_broadcast([P, D])).then_inc(gb_loaded, 16)

            @block.vector
            def _(dve):
                ch = Chain(dve, chain_s)
                if norm:
                    for k in range(rounds):
                        a = src if k == 0 else R.xn
                        ch.link(nc.vector.tensor_reduce(mean[:], a[:], AX_X, ALU.add))
                        ch.link(nc.vector.tensor_scalar(mean[:], mean[:], 1.0 / D, None, ALU.mult))
                        nc.vector.tensor_tensor(R.xn[:], a[:], mean[:, :].unsqueeze(2).to_broadcast([P, T, D]),
                                                ALU.subtract).then_inc(centred, 1)
                        dve.wait_ge(squared, k + 1)
                        ch.link(nc.vector.tensor_reduce(root[:], sq[:], AX_X, ALU.add))
                        nc.vector.tensor_scalar(root[:], root[:], 1.0 / D, EPS, ALU.mult, ALU.add
                                                ).then_inc(var_ready, 1)
                        dve.wait_ge(root_ready, k + 1)
                        ch.link(nc.vector.reciprocal(rstd[:], root[:]))
                        ins = nc.vector.tensor_tensor(R.xn[:], R.xn[:],
                                                      rstd[:, :].unsqueeze(2).to_broadcast([P, T, D]), ALU.mult)
                        if k < rounds - 1:
                            ch.link(ins)
                    if gamma is not None:
                        dve.wait_ge(gb_loaded, 32)
                        ch.link(ins)
                        ch.link(nc.vector.tensor_tensor(R.xn[:], R.xn[:],
                                                        gb[:, 0:1, :].to_broadcast([P, T, D]), ALU.mult))
                        ins = nc.vector.tensor_tensor(R.xn[:], R.xn[:], gb[:, 1:2, :].to_broadcast([P, T, D]),
                                                      ALU.add)
                    ins.then_inc(xn_ready, 1)
                    dve.wait_ge(xn_ready, 1)
                a = R.xn if norm else src
                with dve.Fori(0, G) as g:
                    for u in range(U):
                        dve.wait_ge(turned, g * U + u + 1)
                        nc.vector.tensor_copy(xs[:, u, :], a[:, ds(g * U + u, 1), :].rearrange("p a d -> p (a d)")
                                              ).then_inc(staged, 1)

            @block.tensor
            def _(pe):
                pe.sem_inc(turned, U)
                with pe.Fori(0, G) as g:
                    for u in range(U):
                        pe.wait_ge(staged, g * U + u + 1)
                        pe.wait_ge(copied, g * U + u + 1)
                        for c in range(NC):
                            ins = nc.tensor.transpose(pt[:, u, c * P:(c + 1) * P], xs[:, u, c * P:(c + 1) * P],
                                                      R.ident[:])
                        ins.then_inc(turned, 1)

            @block.scalar
            def _(act):
                for k in range(rounds):
                    act.wait_ge(centred, k + 1)
                    nc.scalar.activation(sq[:], R.xn[:], ACT.Square).then_inc(squared, 1)
                    act.wait_ge(var_ready, k + 1)
                    nc.scalar.activation(root[:], root[:], ACT.Sqrt).then_inc(root_ready, 1)
                act.sem_inc(copied, U)
                with act.Fori(0, G) as g:
                    for u in range(U):
                        act.wait_ge(turned, g * U + u + 1 + U)
                        nc.scalar.activation(R.xt[:, :, ds((g * U + u) * P, P)],
                                             pt[:, u, 0:NC * P].rearrange("p (c n) -> p c n", c=NC),
                                             ACT.Copy).then_inc(copied, 1)


def project(nc, R, name, C, load, dst, bias=False, W=None):
    with Stage(nc, name) as st:
        if W is None:
            W = st.sb("W", [P, NC, C])
        b = st.sb("b", [1, C])
        xs = st.sb("xs", [P, U, NC, P])
        pt = st.ps("pt", [P, U, 512])
        loaded = st.sem("weights_loaded")
        staged = st.sem("tile_staged")
        multiplied = st.sem("tile_multiplied")
        copied = st.sem("tile_copied")
        n = []
        with st.block() as block:
            if load is None:
                n.append(0)
            else:
                @block.sync
                def _(sp):
                    n.append(load(sp, W, b, loaded))

            @block.gpsimd
            def _(pool):
                with pool.Fori(0, G) as g:
                    for u in range(U):
                        pool.wait_ge(multiplied, g * U + u + 1)
                        nc.gpsimd.tensor_copy(xs[:, u], R.xt[:, :, ds((g * U + u) * P, P)]).then_inc(staged, 1)

            @block.tensor
            def _(pe):
                pe.sem_inc(multiplied, U)
                if n[0]:
                    pe.wait_ge(loaded, n[0])
                with pe.Fori(0, G) as g:
                    for u in range(U):
                        pe.wait_ge(staged, g * U + u + 1)
                        pe.wait_ge(copied, g * U + u + 1)
                        for c in range(NC):
                            ins = nc.tensor.matmul(pt[:, u, 0:C], xs[:, u, c], W[:, c, :], start=(c == 0),
                                                   stop=(c == NC - 1 and not bias))
                        if bias:
                            ins = nc.tensor.matmul(pt[:, u, 0:C], R.ones[0:1, :], b[:, :], start=False, stop=True)
                        ins.then_inc(multiplied, 1)

            @block.scalar
            def _(act):
                act.sem_inc(copied, U)
                with act.Fori(0, G) as g:
                    for u in range(U):
                        act.wait_ge(multiplied, g * U + u + 1 + U)
                        for buf, lo, hi in dst:
                            ins = nc.scalar.activation(buf[:, ds(g * U + u, 1), 0:hi - lo]
                                                       .rearrange("p a c -> p (a c)"), pt[:, u, lo:hi], ACT.Copy)
                        ins.then_inc(copied, 1)


def top2_gates(nc, R, name, E, softmax_first):
    with Stage(nc, name) as st:
        m = st.sb("max", [P, T])
        e = st.sb("exp", [P, T, E])
        v = st.sb("values", [P, T, E])
        total = st.sb("total", [P, T])
        rank = st.sb("rank", [P, T, E])
        gt = st.sb("greater", [P, T, E, E])
        eq = st.sb("equal", [P, T, E, E])
        before = st.sb("before", [P, E, E])
        chain_s = st.sem("dve_chain")
        shifted = st.sem("scores_shifted")
        exp_ready = st.sem("exp_ready")
        ones_set = st.sem("before_set")
        before_ready = st.sem("before_ready")
        scores = R.scores[:, :, 0:E]
        gates = R.gates[:, :, 0:E]

        def wide(ap):
            return ap.unsqueeze(2).to_broadcast([P, T, E])
        with st.block() as block:
            @block.gpsimd
            def _(pool):
                nc.gpsimd.memset(before[:], 1.0).then_inc(ones_set, 1)
                pool.wait_ge(ones_set, 1)
                nc.gpsimd.affine_select(out=before[:], in_=before[:], compare_op=ALU.is_gt, fill=0.0, base=0,
                                        pattern=[[1, E], [-1, E]], channel_multiplier=0).then_inc(before_ready, 1)

            @block.vector
            def _(dve):
                ch = Chain(dve, chain_s)
                ch.link(nc.vector.tensor_reduce(m[:], scores, AX_X, ALU.max))
                nc.vector.tensor_tensor(e[:], scores, wide(m[:, :]), ALU.subtract).then_inc(shifted, 1)
                dve.wait_ge(exp_ready, 1)
                if softmax_first:
                    ch.link(nc.vector.tensor_reduce(total[:], e[:], AX_X, ALU.add))
                    ch.link(nc.vector.reciprocal(total[:], total[:]))
                    ch.link(nc.vector.tensor_tensor(e[:], e[:], wide(total[:, :]), ALU.mult))
                    ch.link(nc.vector.tensor_copy(v[:], e[:]))
                else:
                    ch.link(nc.vector.tensor_copy(v[:], scores))
                for k in range(E):
                    mine = v[:, :, k:k + 1].to_broadcast([P, T, E])
                    nc.vector.tensor_tensor(gt[:, :, k, :], v[:], mine, ALU.is_gt)
                    ins = nc.vector.tensor_tensor(eq[:, :, k, :], v[:], mine, ALU.is_equal)
                ch.link(ins)
                dve.wait_ge(before_ready, 1)
                for k in range(E):
                    ins = nc.vector.tensor_tensor(eq[:, :, k, :], eq[:, :, k, :],
                                                  before[:, k:k + 1, :].to_broadcast([P, T, E]), ALU.mult)
                ch.link(ins)
                ch.link(nc.vector.tensor_tensor(gt[:], gt[:], eq[:], ALU.add))
                ch.link(nc.vector.tensor_reduce(rank[:], gt[:], AX_X, ALU.add))
                ch.link(nc.vector.tensor_scalar(rank[:], rank[:], 2.0, None, ALU.is_lt))
                ch.link(nc.vector.tensor_tensor(e[:], e[:], rank[:], ALU.mult))
                ch.link(nc.vector.tensor_reduce(total[:], e[:], AX_X, ALU.add))
                if softmax_first:
                    ch.link(nc.vector.tensor_scalar(total[:], total[:], 1e-12, None, ALU.max))
                ch.link(nc.vector.reciprocal(total[:], total[:]))
                ch.link(nc.vector.tensor_tensor(gates, e[:], wide(total[:, :]), ALU.mult))

            @block.scalar
            def _(act):
                act.wait_ge(shifted, 1)
                nc.scalar.activation(e[:], e[:], ACT.Exp).then_inc(exp_ready, 1)


class EdgeCounter:
    W = 4

    def __init__(self, nc, st, R, src, dst, E, table, least=0):
        W = self.W
        self.nc, self.R, self.ends_of, self.E, self.table = nc, R, (src, dst), E, table
        self.EC = -(-E // P)
        self.EC += -self.EC % (2 * W)
        self.EC = max(self.EC, least * W)
        self.full, self.rest = E // self.EC, E % self.EC
        self.groups = self.EC // W
        self.ends = st.sb("ends", [P, 2, self.EC], I32)
        self.key = st.sb("key", [P, self.EC + W])
        self.earlier = st.sb("earlier", [P, W, W * P])
        self.spare_i = st.sb("spare_i", [P, W], I32)
        self.spare = st.sb("spare", [P, W])
        self.kb = st.sb("key_wide", [P, 2, W, P])
        self.same = st.sb("same", [P, 2 * W, W * P])
        self.ones = st.sb("pair_ones", [P, W * P])
        self.total = st.sb("total", [P, 2, W])
        self.before = st.sb("before", [P, 2, W])
        self.where = st.sb("where", [P, 2, W])
        self.idx = st.sb("idx", [P, 2, W], I32)
        self.pk = st.ps("pk", [P, 2, W * P])
        self.padded = st.sem("padding_set")
        self.ends_loaded = st.sem("edges_loaded")
        self.const = st.sem("masks_made")
        self.widened = st.sem("key_widened")
        self.turned = st.sem("key_rows_ready")
        self.idx_ready = st.sem("idx_ready")
        self.admitted = st.sem("pool_admitted")
        self.written = st.sem("group_written")
        self.scattered = st.sem("count_scattered")
        self.loads = 4 if self.rest else 2

    def load(self, sp):
        sp.wait_ge(self.padded, 1)
        EC, full, rest = self.EC, self.full, self.rest
        for k, ap in enumerate(self.ends_of):
            sp.dma_start(self.ends[0:full, k, :], ap[0:full * EC].rearrange("(p k) -> p k", k=EC)
                         ).then_inc(self.ends_loaded, 16)
            if rest:
                sp.dma_start(self.ends[full:full + 1, k, 0:rest], row(ap[full * EC:self.E])
                             ).then_inc(self.ends_loaded, 16)

    def masks(self, pool):
        nc, W = self.nc, self.W
        nc.gpsimd.memset(self.ends[:], NP - 1).then_inc(self.padded, 1)
        nc.gpsimd.memset(self.earlier[:], 1.0).then_inc(self.const, 1)
        nc.gpsimd.memset(self.ones[:], 1.0).then_inc(self.const, 1)
        nc.gpsimd.iota(self.spare_i[:], pattern=[[P, W]], base=NP * NP, channel_multiplier=1
                       ).then_inc(self.const, 1)
        pool.wait_ge(self.const, 3)
        nc.gpsimd.affine_select(out=self.earlier[:], in_=self.earlier[:], compare_op=ALU.is_gt, fill=0.0, base=0,
                                pattern=[[P, W], [-1, W * P]], channel_multiplier=1).then_inc(self.const, 1)

    def add(self, pool, n, b):
        pool.wait_ge(self.idx_ready, n + 1)
        pool.sem_inc(self.admitted, 1)
        for a in range(self.W):
            self.nc.gpsimd.indirect_dma_start(
                out=self.table[:, :], in_=self.total[:, b, a:a + 1], in_offset=None, compute_op=ALU.add,
                out_offset=bass.IndirectOffsetOnAxis(ap=self.idx[:, b, a:a + 1], axis=0)
            ).then_inc(self.scattered, 16)
        pool.wait_ge(self.scattered, (n + 1) * 16 * self.W)
        pool.sem_inc(self.written, 1)

    def turn(self, pe, n, b):
        pe.wait_ge(self.widened, n + 1)
        for a in range(self.W):
            ins = self.nc.tensor.transpose(self.pk[:, b, a * P:(a + 1) * P], self.kb[:, b, a, :], self.R.ident[:])
        ins.then_inc(self.turned, 1)

    def keys(self, dve, ch):
        nc, key, ends = self.nc, self.key, self.ends
        dve.wait_ge(self.const, 4)
        dve.sem_inc(self.written, 2)
        ch.link(nc.vector.tensor_copy(self.spare[:], self.spare_i[:]))
        nc.vector.memset(key[:, self.EC:], 0.0)
        dve.wait_ge(self.ends_loaded, 16 * self.loads)
        k = key[:, 0:self.EC]
        ch.link(nc.vector.tensor_copy(k, ends[:, 1, :]))
        ch.link(nc.vector.tensor_scalar(k, k, float(NP), None, ALU.mult))
        ch.link(nc.vector.tensor_tensor(k, k, ends[:, 0, :], ALU.add))

    def widen(self, n, b):
        kg = self.key[:, ds(n * self.W, self.W)]
        self.nc.vector.tensor_copy(self.kb[:, b], kg.unsqueeze(2).to_broadcast([P, self.W, P])
                                   ).then_inc(self.widened, 1)

    def compare(self, dve, n, b, half):
        nc, W = self.nc, self.W
        if half == 0:
            dve.wait_ge(self.turned, n + 1)
            dve.wait_ge(self.written, n + 1)
        for a in (2 * half, 2 * half + 1):
            ka = self.key[:, ds(n * W + a, 1)]
            nc.vector.scalar_tensor_tensor(out=self.same[:, a], in0=self.pk[:, b, :], scalar=ka,
                                           in1=self.earlier[:, a, :], op0=ALU.is_equal, op1=ALU.mult,
                                           accum_out=self.before[:, b, a:a + 1])
            ins = nc.vector.scalar_tensor_tensor(out=self.same[:, W + a], in0=self.pk[:, b, :], scalar=ka,
                                                 in1=self.ones[:], op0=ALU.is_equal, op1=ALU.mult,
                                                 accum_out=self.total[:, b, a:a + 1])
        return ins

    LINKS = 5

    def place(self, ch, n, b, ins):
        nc, where, before, spare = self.nc, self.where, self.before, self.spare
        ch.link(ins)
        ch.link(nc.vector.tensor_scalar(before[:, b], before[:, b], 0.5, None, ALU.is_lt))
        ch.link(nc.vector.tensor_tensor(where[:, b], self.key[:, ds(n * self.W, self.W)], spare[:], ALU.subtract))
        ch.link(nc.vector.tensor_tensor(where[:, b], where[:, b], before[:, b], ALU.mult))
        ch.link(nc.vector.tensor_tensor(where[:, b], where[:, b], spare[:], ALU.add))
        nc.vector.tensor_copy(self.idx[:, b], where[:, b]).then_inc(self.idx_ready, 1)


def experts(nc, R, name, E, H, w1, b1, w2, b2, add_xn, count=None):
    HC = H // P
    with Stage(nc, name) as st:
        w1s = st.sb("w1", [P, E, NC, H])
        w2s = st.sb("w2", [P, E, HC, D])
        b1s = st.sb("b1", [P, E, HC])
        b2s = st.sb("b2", [E, D])
        gs = st.sb("gates_tile", [P, E])
        gT = st.sb("gates_T", [E, P])
        hT = st.sb("hT", [P, 2, HC, P])
        ph = st.ps("ph", [P, 2, 512])
        py = st.ps("py", [P, 2, 512])
        pg = st.ps("pg", [E, P])
        pb = st.ps("pb", [P, D])
        loaded = st.sem("weights_loaded")
        h_ready = st.sem("hidden_ready")
        gelu_ready = st.sem("gelu_ready")
        y_ready = st.sem("y_ready")
        y_added = st.sem("y_added")
        gates_staged = st.sem("gates_staged")
        gates_turned = st.sem("gates_turned")
        gT_ready = st.sem("gates_T_ready")
        bias_ready = st.sem("bias_ready")
        bias_added = st.sem("bias_added")
        chain_s = st.sem("dve_chain")
        ec = EdgeCounter(nc, st, R, *count) if count else None
        GT = E // 2
        left = (ec.groups - T * GT) // 2 if ec else 0
        assert left >= 0 and GT % 2 == 0
        with st.block() as block:
            @block.sync
            def _(sp):
                for e in range(E):
                    sp.dma_start(w1s[:, e], w1[e].rearrange("(c p) h -> p c h", p=P)).then_inc(loaded, 16)
                    sp.dma_start(w2s[:, e], w2[e].rearrange("(c p) d -> p c d", p=P)).then_inc(loaded, 16)
                sp.dma_start(b1s[:].rearrange("p e c -> p (e c)"), b1.rearrange("e (c p) -> p (e c)", p=P),
                             allow_slow_non_contiguous=True).then_inc(loaded, 16)
                sp.dma_start(b2s[:], b2).then_inc(loaded, 16)
                if ec:
                    ec.load(sp)
                    sp.wait_ge(ec.ends_loaded, 16 * ec.loads)

            if ec:
                @block.gpsimd
                def _(pool):
                    ec.masks(pool)
                    with pool.Fori(0, T * GT // 2 + left) as g:
                        for b in range(2):
                            ec.add(pool, g * 2 + b, b)

            @block.tensor
            def _(pe):
                pe.wait_ge(loaded, 16 * (2 * E + 2))
                pe.sem_inc(y_ready, 2)
                pe.sem_inc(gates_turned, 1)
                pe.sem_inc(bias_ready, 1)

                def hidden(i, e):
                    pe.wait_ge(gelu_ready, i * E + e + 1)
                    for h in range(HC):
                        for c in range(NC):
                            ins = nc.tensor.matmul(ph[:, e % 2, h * P:(h + 1) * P],
                                                   w1s[:, e, c, h * P:(h + 1) * P],
                                                   R.xt[:, c, ds(i * P, P)], start=(c == 0),
                                                   stop=(c == NC - 1))
                    ins.then_inc(h_ready, 1)

                def tile(i, last):
                    for e in range(E):
                        if e + 1 < E:
                            hidden(i, e + 1)
                        elif not last:
                            hidden(i + 1, 0)
                        pe.wait_ge(gelu_ready, i * E + e + 3)
                        pe.wait_ge(y_added, i * E + e + 1)
                        for h in range(HC):
                            ins = nc.tensor.matmul(py[:, e % 2, 0:D], hT[:, e % 2, h, :], w2s[:, e, h, :],
                                                   start=(h == 0), stop=(h == HC - 1))
                        ins.then_inc(y_ready, 1)
                        if ec and e % 2 == 0:
                            ec.turn(pe, i * GT + e // 2 + 1, (e // 2 + 1) % 2)
                        if e == 1:
                            pe.wait_ge(gates_staged, i + 1)
                            pe.wait_ge(gT_ready, i + 1)
                            nc.tensor.transpose(pg[:], gs[:], R.ident[:]).then_inc(gates_turned, 1)
                    pe.wait_ge(gT_ready, i + 2)
                    pe.wait_ge(bias_added, i + 1)
                    nc.tensor.matmul(pb[:], gT[:], b2s[:], start=True, stop=True).then_inc(bias_ready, 1)

                if ec:
                    ec.turn(pe, 0, 0)
                hidden(0, 0)
                with pe.Fori(0, T - 1) as i:
                    tile(i, False)
                tile(T - 1, True)
                if left:
                    with pe.Fori(T * GT // 2, T * GT // 2 + left) as g:
                        for b in range(2):
                            ec.turn(pe, g * 2 + b + 1, (b + 1) % 2)

            @block.scalar
            def _(act):
                act.wait_ge(loaded, 16 * (2 * E + 2))
                act.sem_inc(gelu_ready, 2)
                with act.Fori(0, T) as i:
                    for e in range(E):
                        act.wait_ge(h_ready, i * E + e + 1)
                        act.wait_ge(y_ready, i * E + e + 1)
                        for h in range(HC):
                            ins = nc.scalar.activation(hT[:, e % 2, h, :], ph[:, e % 2, h * P:(h + 1) * P],
                                                       ACT.Gelu, bias=b1s[:, e, h:h + 1])
                        ins.then_inc(gelu_ready, 1)

            @block.vector
            def _(dve):
                ch = Chain(dve, chain_s)
                if add_xn:
                    ch.link(nc.vector.tensor_tensor(R.x[:], R.x[:], R.xn[:], ALU.add))
                dve.sem_inc(y_added, 2)
                dve.sem_inc(gT_ready, 1)
                dve.sem_inc(bias_added, 1)
                if ec:
                    ec.keys(dve, ch)
                    ec.widen(0, 0)
                with dve.Fori(0, T) as i:
                    if ec:
                        ch.loop(i, GT * ec.LINKS)
                    xi = R.x[:, ds(i, 1), :].rearrange("p a d -> p (a d)")
                    dve.wait_ge(gates_turned, i + 1)
                    nc.vector.tensor_copy(gs[:], R.gates[:, ds(i, 1), 0:E].rearrange("p a e -> p (a e)")
                                          ).then_inc(gates_staged, 1)
                    for e in range(E):
                        n, b = i * GT + e // 2, e // 2 % 2
                        if ec and e % 2 == 0:
                            ec.widen(n + 1, 1 - b)
                        dve.wait_ge(y_ready, i * E + e + 3)
                        if e:
                            dve.wait_ge(y_added, i * E + e + 2)
                        nc.vector.scalar_tensor_tensor(out=xi, in0=py[:, e % 2, 0:D],
                                                       scalar=R.gates[:, ds(i, 1), e], in1=xi,
                                                       op0=ALU.mult, op1=ALU.add).then_inc(y_added, 1)
                        if ec:
                            ins = ec.compare(dve, n, b, e % 2)
                            if e % 2:
                                ec.place(ch, n, b, ins)
                        if e == 1:
                            dve.wait_ge(gates_turned, i + 2)
                            dve.wait_ge(bias_ready, i + 1)
                            nc.vector.tensor_copy(gT[:], pg[:]).then_inc(gT_ready, 1)
                    dve.wait_ge(bias_ready, i + 2)
                    dve.wait_ge(y_added, i * E + E + 2)
                    nc.vector.tensor_tensor(xi, xi, pb[:], ALU.add).then_inc(bias_added, 1)
                if ec:
                    ch.end(T)
                if left:
                    with dve.Fori(T * GT // 2, T * GT // 2 + left) as g:
                        ch.loop(g - T * GT // 2, 2 * ec.LINKS)
                        for b in range(2):
                            n = g * 2 + b
                            ec.widen(n + 1, 1 - b)
                            ec.compare(dve, n, b, 0)
                            ec.place(ch, n, b, ec.compare(dve, n, b, 1))
                    ch.end(left)


def load_plain(w, bias=None):
    def load(sp, W, b, sem):
        sp.dma_start(W[:], w.rearrange("(c p) n -> p c n", p=P)).then_inc(sem, 16)
        if bias is None:
            return 16
        sp.dma_start(b[:], row(bias)).then_inc(sem, 16)
        return 32
    return load


def l0_ffn(nc, R, A, edges):
    layernorm_T(nc, R, "l0f_ln", R.x)

    def load(sp, W, b, sem):
        for c in range(NC):
            sp.dma_start(W[:, c, :], A["L0_ffn_router_w"].rearrange("e (c p) -> p c e", p=P)[:, c, :],
                         allow_slow_non_contiguous=True).then_inc(sem, 16)
        return 16 * NC
    project(nc, R, "l0f_router", 8, load, [(R.scores, 0, 8)])
    top2_gates(nc, R, "l0f_gates", 8, True)
    experts(nc, R, "l0f_experts", 8, D, A["L0_ffn_w1"], A["L0_ffn_b1"], A["L0_ffn_w2"], A["L0_ffn_b2"], True,
            count=(A["src"], A["dst"], A["src"].shape[0], edges))


def l3_ffn(nc, R, A):
    layernorm_T(nc, R, "l3f_ln", R.x, gamma=A["L3_ffn_gamma"], beta=A["L3_ffn_beta"])
    project(nc, R, "l3f_router", 8, load_plain(A["L3_ffn_Wr"], A["L3_ffn_br"]), [(R.scores, 0, 8)], bias=True)
    top2_gates(nc, R, "l3f_gates", 8, False)
    experts(nc, R, "l3f_experts", 8, 2 * D, A["L3_ffn_W1"], A["L3_ffn_b1"], A["L3_ffn_W2"], A["L3_ffn_b2"], False)


JG = [(j, min(j + 4, T)) for j in range(0, T, 4)]
NJ = len(JG)


def turn_group(nc, pe, R, src, q, bank):
    lo, hi = JG[q]
    for j in range(lo, hi):
        ins = nc.tensor.transpose(bank[:, (j - lo) * P:(j - lo + 1) * P], src[:, j * P:(j + 1) * P], R.ident[:])
    return ins


def multiply_group(nc, pe, turned, V, lo_c, hi_c, q, out):
    lo, hi = JG[q]
    for j in range(lo, hi):
        ins = nc.tensor.matmul(out, turned[:, (j - lo) * P:(j - lo + 1) * P], V[:, j, lo_c:hi_c],
                               start=(j == 0), stop=(j == T - 1))
    return ins


def table_rows(table):
    return table[0:NP * NP, :].rearrange("(t p n) a -> t p (n a)", p=P, n=NP)


def load_table(sp, rows, cnt, loaded, freed):
    def one(it, slot, first=False):
        if not first:
            sp.wait_ge(freed, it + 1)
        src = rows[0] if first else rows[ds(it, 1)].rearrange("a p n -> p (a n)")
        sp.dma_start(cnt[:, slot], src).then_inc(loaded[slot], 16)
    one(0, 0, True)
    with sp.Fori(0, T // 2) as g:
        one(g * 2 + 1, 1)
        one(g * 2 + 2, 0)


def gcn(nc, R, name, table, count):
    rows = table_rows(table)
    with Stage(nc, name + "_deg") as st:
        cnt = st.sb("cnt", [P, 2, NP])
        deg = st.sb("deg", [P, T])
        root = st.sb("root", [P, T])
        loaded = [st.sem("rows_loaded0"), st.sem("rows_loaded1")]
        freed = st.sem("rows_used")
        root_ready = st.sem("root_ready")
        deg_ready = st.sem("deg_ready")
        chain_s = st.sem("dve_chain")
        with st.block() as block:
            @block.sync
            def _(sp):
                load_table(sp, rows, cnt, loaded, freed)

            @block.vector
            def _(dve):
                ch = Chain(dve, chain_s)

                def degree(it, k, slot):
                    dve.wait_ge(loaded[slot], k * 16 + 16)
                    nc.vector.tensor_reduce(deg[:, ds(it, 1)], cnt[:, slot], AX_X, ALU.add).then_inc(freed, 1)

                dve.sem_inc(freed, 2)
                degree(0, 0, 0)
                with dve.Fori(0, T // 2) as g:
                    degree(g * 2 + 1, g, 1)
                    degree(g * 2 + 2, g + 1, 0)
                dve.wait_ge(freed, T + 2)
                nc.vector.tensor_scalar(root[:], deg[:], 1.0, None, ALU.max).then_inc(deg_ready, 1)
                dve.wait_ge(root_ready, 1)
                ch.link(nc.vector.reciprocal(root[:], root[:]))
                ch.link(nc.vector.tensor_scalar(deg[:], deg[:], 0.0, None, ALU.is_gt))
                ch.link(nc.vector.tensor_tensor(R.dis[:], root[:], deg[:], ALU.mult))
                ch.link(nc.vector.tensor_tensor(R.xn[:], R.xn[:], R.dis[:, :].unsqueeze(2).to_broadcast([P, T, D]),
                                                ALU.mult))

            @block.scalar
            def _(act):
                act.wait_ge(deg_ready, 1)
                nc.scalar.activation(root[:], root[:], ACT.Sqrt).then_inc(root_ready, 1)

    with Stage(nc, name) as st:
        cnt = st.sb("cnt", [P, 2, NP])
        turned = st.sb("turned", [P, 2, 512])
        pt = st.ps("pt", [P, 2, 512])
        po = st.ps("po", [P, 2, 512])
        loaded = [st.sem("rows_loaded0"), st.sem("rows_loaded1")]
        freed = st.sem("rows_turned")
        bank_ready = st.sem("bank_ready")
        copied = st.sem("bank_copied")
        used = st.sem("turned_used")
        out_ready = st.sem("out_ready")
        out_used = st.sem("out_used")
        chain_s = st.sem("dve_chain")
        GT = 4
        ec = EdgeCounter(nc, st, R, *count, least=GT * T)
        assert ec.groups == GT * T
        with st.block() as block:
            @block.sync
            def _(sp):
                ec.load(sp)
                load_table(sp, rows, cnt, loaded, freed)
                sp.wait_ge(ec.ends_loaded, 16 * ec.loads)

            @block.gpsimd
            def _(pool):
                ec.masks(pool)
                with pool.Fori(0, ec.groups // 2) as g:
                    for b in range(2):
                        ec.add(pool, g * 2 + b, b)

            @block.tensor
            def _(pe):
                pe.sem_inc(freed, 2)
                pe.sem_inc(used, 2)

                def turn(it, b, q):
                    n = it * NJ + q
                    pe.wait_ge(copied, n + 1)
                    turn_group(nc, pe, R, cnt[:, b], q, pt[:, (b + q) % 2]).then_inc(bank_ready, 1)

                def tile(it, k, b):
                    pe.wait_ge(loaded[b], k * 16 + 16)
                    pe.wait_ge(out_used, it + 1)
                    turn(it, b, 0)
                    for q in range(NJ):
                        if q + 1 < NJ:
                            turn(it, b, q + 1)
                        if q + 1 == NJ:
                            pe.wait_ge(bank_ready, it * NJ + NJ)
                            pe.sem_inc(freed, 1)
                        pe.wait_ge(copied, it * NJ + q + 3)
                        ins = multiply_group(nc, pe, turned[:, (b + q) % 2], R.xn, 0, D, q, po[:, b, 0:D])
                        ins.then_inc(used, 1)
                        if q in (0, 2, 4, NJ - 1):
                            ec.turn(pe, it * GT + q // 2 + 1, (q // 2 + 1) % 2)
                    pe.wait_ge(used, it * NJ + NJ + 2)
                    pe.sem_inc(out_ready, 1)

                ec.turn(pe, 0, 0)
                tile(0, 0, 0)
                with pe.Fori(0, T // 2) as g:
                    tile(g * 2 + 1, g, 1)
                    tile(g * 2 + 2, g + 1, 0)

            @block.scalar
            def _(act):
                act.sem_inc(copied, 2)

                def tile(it, b):
                    for q in range(NJ):
                        w = (JG[q][1] - JG[q][0]) * P
                        act.wait_ge(bank_ready, it * NJ + q + 1)
                        act.wait_ge(used, it * NJ + q + 1)
                        nc.scalar.activation(turned[:, (b + q) % 2, 0:w], pt[:, (b + q) % 2, 0:w], ACT.Copy
                                             ).then_inc(copied, 1)
                tile(0, 0)
                with act.Fori(0, T // 2) as g:
                    tile(g * 2 + 1, 1)
                    tile(g * 2 + 2, 0)

            @block.vector
            def _(dve):
                dve.sem_inc(out_used, 2)

                ch = Chain(dve, chain_s)
                ec.keys(dve, ch)
                ec.widen(0, 0)

                def tile(it, b):
                    for k in range(GT):
                        n, slot = it * GT + k, k % 2
                        ec.widen(n + 1, 1 - slot)
                        ec.compare(dve, n, slot, 0)
                        ec.place(ch, n, slot, ec.compare(dve, n, slot, 1))
                    xi = R.x[:, ds(it, 1), :].rearrange("p a d -> p (a d)")
                    dve.wait_ge(out_ready, it + 1)
                    nc.vector.scalar_tensor_tensor(out=xi, in0=po[:, b, 0:D], scalar=R.dis[:, ds(it, 1)], in1=xi,
                                                   op0=ALU.mult, op1=ALU.add).then_inc(out_used, 1)
                tile(0, 0)
                with dve.Fori(0, T // 2) as g:
                    ch.loop(g, 2 * GT * ec.LINKS)
                    tile(g * 2 + 1, 1)
                    tile(g * 2 + 2, 0)
                ch.end(T // 2)


HEADS = 4
SLOPE = 0.2


def gat_weights(nc, R, name, W, att_src, att_dst, F):
    HF = HEADS * F
    with Stage(nc, name) as st:
        a = st.sb("a", [P, 2, HF])
        prod = st.sb("prod", [P, 2, NC, HEADS, F])
        wa = st.sb("wa", [P, 2, NC, HEADS])
        loaded = st.sem("weights_loaded")
        chain_s = st.sem("dve_chain")
        with st.block() as block:
            @block.sync
            def _(sp):
                sp.dma_start(R.we[:, :, 0:HF], W.rearrange("(c p) n -> p c n", p=P)).then_inc(loaded, 16)
                for k, v in enumerate((att_src, att_dst)):
                    sp.dma_start(a[:, k, :], row(v.rearrange("h f -> (h f)")).to_broadcast([P, HF])
                                 ).then_inc(loaded, 16)

            @block.vector
            def _(dve):
                ch = Chain(dve, chain_s)
                dve.wait_ge(loaded, 48)
                for k in range(2):
                    for c in range(NC):
                        ins = nc.vector.tensor_tensor(prod[:, k, c].rearrange("p h f -> p (h f)"),
                                                      R.we[:, c, 0:HF], a[:, k, :], ALU.mult)
                ch.link(ins)
                for k in range(2):
                    ins = nc.vector.tensor_reduce(wa[:, k], prod[:, k], AX_X, ALU.add)
                ch.link(ins)
                nc.vector.tensor_copy(R.we[:, :, HF:HF + HEADS], wa[:, 1])
                for c in range(NC):
                    ins = nc.vector.tensor_copy(R.was[:, c], wa[:, 0, c, :].unsqueeze(2).to_broadcast([P, HEADS, P]))
                ch.link(ins)


def source_rows(nc, R, name, as_row):
    with Stage(nc, name) as st:
        pt = st.ps("pt", [P, U, 512])
        multiplied = st.sem("tile_multiplied")
        copied = st.sem("tile_copied")
        with st.block() as block:
            @block.tensor
            def _(pe):
                with pe.Fori(0, G) as g:
                    for u in range(U):
                        pe.wait_ge(copied, g * U + u + 1)
                        for h in range(HEADS):
                            for c in range(NC):
                                ins = nc.tensor.matmul(pt[:, u, h * P:(h + 1) * P], R.was[:, c, h, :],
                                                       R.xt[:, c, ds((g * U + u) * P, P)], start=(c == 0),
                                                       stop=(c == NC - 1))
                        ins.then_inc(multiplied, 1)

            @block.scalar
            def _(act):
                act.sem_inc(copied, U)
                with act.Fori(0, G) as g:
                    for u in range(U):
                        act.wait_ge(multiplied, g * U + u + 1)
                        nc.scalar.activation(as_row[:, :, ds((g * U + u) * P, P)],
                                             pt[:, u, :].rearrange("p (h n) -> p h n", h=HEADS),
                                             ACT.Copy).then_inc(copied, 1)


def gat_attend(nc, R, name, table, as_row, bias, F, finish, self_loops, dram=None):
    rows = table_rows(table)
    HF = HEADS * F
    AHEAD = 2
    BANKS = 4

    def slot(h, q):
        return (h * NJ + q) % BANKS

    with Stage(nc, name) as st:
        cnt = st.sb("cnt", [P, 2, NP])
        neg = st.sb("neg", [P, NP])
        more = st.sb("more", [P, HEADS - NC, NP])
        Y = [R.xt[:, h] for h in range(NC)] + [more[:, h] for h in range(HEADS - NC)]
        top = st.sb("top", [P, 2, HEADS])
        negm = st.sb("negm", [P, 2, HEADS])
        den = st.sb("den", [P, 2, HEADS])
        bb = st.sb("bias", [P, HF])
        ot = st.sb("out", [P, 2, HEADS, F])
        turned = st.sb("turned", [P, BANKS, 512])
        pt = st.ps("pt", [P, BANKS, 512])
        po = st.ps("po", [P, 2, 512])
        loaded = [st.sem("rows_loaded0"), st.sem("rows_loaded1")]
        stored = [st.sem("out_stored0"), st.sem("out_stored1")]
        bias_loaded = st.sem("bias_loaded")
        freed = st.sem("rows_used")
        shifted = st.sem("scores_shifted")
        masked = st.sem("masked_ready")
        exp_ready = st.sem("exp_ready")
        p_ready = st.sem("p_ready")
        p_turned = st.sem("p_turned")
        bank_ready = st.sem("bank_ready")
        copied = st.sem("bank_copied")
        used = st.sem("turned_used")
        out_ready = st.sem("out_ready")
        out_used = st.sem("out_used")
        out_done = st.sem("out_done")
        po_read = st.sem("output_bank_read")
        admitted = st.sem("dve_admitted")
        chain_s = st.sem("dve_chain")
        with st.block() as block:
            @block.sync
            def _(sp):
                sp.dma_start(bb[:], row(bias).to_broadcast([P, HF])).then_inc(bias_loaded, 16)

                def one(it, slot, first=False):
                    if not first:
                        sp.wait_ge(freed, it + 1)
                    src = rows[0] if first else rows[ds(it, 1)].rearrange("a p n -> p (a n)")
                    sp.dma_start(cnt[:, slot], src).then_inc(loaded[slot], 16)

                one(0, 0, True)
                with sp.Fori(0, T // 2) as g:
                    one(g * 2 + 1, 1)
                    one(g * 2 + 2, 0)

            if dram is not None:
                @block.gpsimd
                def _(pool):
                    with pool.Fori(0, T // 2) as g:
                        for b in range(2):
                            it = g * 2 + b
                            pool.wait_ge(out_done, it + 1)
                            pool.dma_start(dram[ds(it * P, P), :], ot[:, b].rearrange("p h f -> p (h f)")
                                           ).then_inc(stored[b], 16)
                            pool.wait_ge(stored[b], g * 16 + 16)
                            pool.sem_inc(out_used, 1)
                    pool.wait_ge(out_done, T)
                    pool.dma_start(dram[(T - 1) * P:T * P, :], ot[:, 0].rearrange("p h f -> p (h f)")
                                   ).then_inc(stored[0], 16)
                    pool.wait_ge(stored[0], (T // 2 + 1) * 16)

            @block.vector
            def _(dve):
                ch = Chain(dve, chain_s)
                dve.sem_inc(freed, 2)
                dve.sem_inc(p_turned, HEADS)

                def begin(it, k, b):
                    dve.wait_ge(loaded[b], k * 16 + 16)
                    if self_loops:
                        dgl = cnt[:, b, ds(it * P, P)]
                        ch.link(nc.vector.tensor_tensor(dgl, dgl, R.ident[:], ALU.add))
                    ch.link(nc.vector.tensor_scalar(neg[:], cnt[:, b], 0.5, -BIG, ALU.is_lt, ALU.mult))

                def mask(it, b, h):
                    u = it * HEADS + h
                    dve.wait_ge(shifted, u + 1)
                    dve.sem_inc(admitted, 1)
                    ch.link(nc.vector.tensor_tensor_reduce(Y[h], Y[h], neg[:], 1.0, -3e38,
                                                           ALU.add, ALU.max, top[:, b, h:h + 1]))
                    t = top[:, b, h:h + 1]
                    ch.link(nc.vector.scalar_tensor_tensor(out=t, in0=t, scalar=SLOPE, in1=t, op0=ALU.mult,
                                                           op1=ALU.max))
                    ch.link(nc.vector.tensor_scalar(negm[:, b, h:h + 1], t, -1.0, None, ALU.mult))
                    nc.vector.scalar_tensor_tensor(out=Y[h], in0=Y[h], scalar=SLOPE, in1=Y[h], op0=ALU.mult,
                                                   op1=ALU.max).then_inc(masked, 1)

                def weigh(it, b, h):
                    u = it * HEADS + h
                    dve.wait_ge(exp_ready, u + 1)
                    ins = nc.vector.tensor_tensor_reduce(Y[h], Y[h], cnt[:, b], 1.0, 0.0, ALU.mult,
                                                         ALU.add, den[:, b, h:h + 1])
                    ins.then_inc(p_ready, 1)
                    if h == HEADS - 1:
                        dve.wait_ge(p_ready, u + 1)
                        dve.sem_inc(freed, 1)

                def end(it, b):
                    dve.wait_ge(p_ready, it * HEADS + HEADS)
                    ch.link(nc.vector.tensor_scalar(den[:, b], den[:, b], 1e-16, None, ALU.add))
                    ch.link(nc.vector.reciprocal(den[:, b], den[:, b]))
                    dve.wait_ge(out_ready, it + 1)
                    dve.wait_ge(out_used, it + 1)
                    ch.link(nc.vector.tensor_tensor(ot[:, b], po[:, b, 0:HF].rearrange("p (h f) -> p h f", h=HEADS),
                                                    den[:, b].unsqueeze(2).to_broadcast([P, HEADS, F]), ALU.mult))
                    dve.sem_inc(po_read, 1)
                    of = ot[:, b].rearrange("p h f -> p (h f)")
                    ch.link(nc.vector.tensor_tensor(of, of, bb[:], ALU.add))
                    if finish == "x":
                        xi = R.x[:, ds(it, 1), :].rearrange("p a d -> p (a d)")
                        ch.link(nc.vector.tensor_tensor(xi, xi, of, ALU.add))
                    elif finish == "scores":
                        ch.link(nc.vector.tensor_copy(R.scores[:, ds(it, 1), 0:HF].rearrange("p a c -> p (a c)"),
                                                      of))
                    dve.sem_inc(out_done, 1)
                    if dram is None:
                        dve.sem_inc(out_used, 1)

                def tile(it, k, b, last=None):
                    begin(it, k, b)
                    for h in range(HEADS):
                        mask(it, b, h)
                        if h:
                            weigh(it, b, h - 1)
                        elif last is not None:
                            weigh(last, 1 - b, HEADS - 1)
                        if h == 2 and last is not None:
                            end(last, 1 - b)

                dve.sem_inc(out_used, 2)
                dve.sem_inc(po_read, 2)
                dve.wait_ge(bias_loaded, 16)
                per = self_loops + 1 + 3 * HEADS + 4 + (finish in ("x", "scores"))
                tile(0, 0, 0)
                with dve.Fori(0, T // 2) as g:
                    ch.loop(g, 2 * per)
                    tile(g * 2 + 1, g, 1, g * 2)
                    tile(g * 2 + 2, g + 1, 0, g * 2 + 1)
                ch.end(T // 2)
                weigh(T - 1, 0, HEADS - 1)
                end(T - 1, 0)

            @block.scalar
            def _(act):
                act.sem_inc(copied, BANKS)

                half = NP // 2

                def shift(it, b, h, part):
                    cut = slice(part * half, (part + 1) * half)
                    if part == 0:
                        act.wait_ge(p_turned, it * HEADS + h + 1)
                    ins = nc.scalar.activation(Y[h][:, cut], as_row[:, h, cut], ACT.Identity,
                                               bias=R.ad[:, ds(it, 1), h])
                    if part == 1:
                        ins.then_inc(shifted, 1)

                def exp(it, b, h, part):
                    cut = slice(part * half, (part + 1) * half)
                    if part == 0:
                        act.wait_ge(masked, it * HEADS + h + 1)
                    ins = nc.scalar.activation(Y[h][:, cut], Y[h][:, cut], ACT.Exp, bias=negm[:, b, h:h + 1])
                    if part == 1:
                        ins.then_inc(exp_ready, 1)

                def copies(unit, groups):
                    if unit is None:
                        return
                    it, h = unit
                    for q in groups:
                        n = (it * HEADS + h) * NJ + q
                        w = (JG[q][1] - JG[q][0]) * P
                        act.wait_ge(bank_ready, n + 1)
                        act.wait_ge(used, n + 1)
                        nc.scalar.activation(turned[:, slot(h, q), 0:w], pt[:, slot(h, q), 0:w], ACT.Copy
                                             ).then_inc(copied, 1)

                def tile(it, b, last=None):
                    for h in range(HEADS):
                        if h >= 2:
                            old = (it, h - 2)
                        else:
                            old = None if last is None else (last, h + 2)
                        ahead = (it, b, h + 1) if h + 1 < HEADS else (it + 1, 1 - b, 0)
                        copies(old, (0, 1))
                        shift(*ahead, 0)
                        copies(old, (2, 3))
                        shift(*ahead, 1)
                        copies(old, (4, 5))
                        exp(it, b, h, 0)
                        copies(old, (6,))
                        exp(it, b, h, 1)

                shift(0, 0, 0, 0)
                shift(0, 0, 0, 1)
                tile(0, 0)
                with act.Fori(0, T // 2) as g:
                    tile(g * 2 + 1, 1, g * 2)
                    tile(g * 2 + 2, 0, g * 2 + 1)
                copies((T - 1, 2), range(NJ))
                copies((T - 1, 3), range(NJ))

            @block.tensor
            def _(pe):
                pe.sem_inc(used, BANKS)

                def turn(it, h, q):
                    n = (it * HEADS + h) * NJ + q
                    pe.wait_ge(copied, n + 1)
                    turn_group(nc, pe, R, Y[h], q, pt[:, slot(h, q)]).then_inc(bank_ready, 1)

                def tile(it, b):
                    pe.wait_ge(po_read, it + 1)
                    for h in range(HEADS):
                        pe.wait_ge(p_ready, it * HEADS + h + 1)
                        for q in range(AHEAD):
                            turn(it, h, q)
                        for q in range(NJ):
                            if q + AHEAD < NJ:
                                turn(it, h, q + AHEAD)
                            if q == NJ - 1:
                                pe.wait_ge(bank_ready, (it * HEADS + h + 1) * NJ)
                                pe.sem_inc(p_turned, 1)
                            pe.wait_ge(copied, (it * HEADS + h) * NJ + q + 1 + BANKS)
                            multiply_group(nc, pe, turned[:, slot(h, q)], R.xn, h * F, (h + 1) * F, q,
                                           po[:, b, h * F:(h + 1) * F]).then_inc(used, 1)
                    pe.wait_ge(used, (it + 1) * HEADS * NJ + BANKS)
                    pe.sem_inc(out_ready, 1)

                tile(0, 0)
                with pe.Fori(0, T // 2) as g:
                    tile(g * 2 + 1, 1)
                    tile(g * 2 + 2, 0)


def gat(nc, R, name, table, W, att_src, att_dst, bias, F, finish, self_loops=False, dram=None):
    HF = HEADS * F
    with nc.sbuf_tensor(name + "_as_row", [P, HEADS, NP], F32) as as_row:
        with nc.sbuf_tensor(name + "_W_src", [P, NC, HEADS, P], F32) as R.was:
            gat_weights(nc, R, name + "_w", W, att_src, att_dst, F)
            project(nc, R, name + "_h", HF + HEADS, None, [(R.xn, 0, HF), (R.ad, HF, HF + HEADS)],
                    W=R.we[:, :, 0:HF + HEADS])
            source_rows(nc, R, name + "_src", as_row)
        gat_attend(nc, R, name, table, as_row, bias, F, finish, self_loops, dram)


def l1_gnn(nc, R, A, edges, routes):
    layernorm_T(nc, R, "l1g_ln", R.x)
    project(nc, R, "l1g_h", D, load_plain(A["L1_gnn_W"]), [(R.xn, 0, D)])
    ends = A["L2_ffn_edge_index"]
    gcn(nc, R, "l1g", edges, (ends[0], ends[1], ends.shape[1], routes))


def reload(nc, R, name, dram):
    with Stage(nc, name) as st:
        loaded = st.sem("rows_loaded")
        with st.block() as block:
            @block.sync
            def _(sp):
                sp.dma_start(R.xn[:], dram[:, :].rearrange("(t p) d -> p t d", p=P)).then_inc(loaded, 16)
                sp.wait_ge(loaded, 16)
    layernorm_T(nc, R, name + "_T", R.xn, norm=False)


def l3_gnn(nc, R, A, edges):
    hidden = nc.dram_tensor("gat_hidden", [2, NP, D], F32).ap()
    layernorm_T(nc, R, "l3g_ln", R.x)
    for k in range(3):
        gat(nc, R, f"l3g{k}", edges, A[f"L3_gnn_W{k}"], A[f"L3_gnn_as{k}"], A[f"L3_gnn_ad{k}"], A[f"L3_gnn_b{k}"],
            D // HEADS, "x" if k == 2 else "dram", self_loops=True, dram=None if k == 2 else hidden[k])
        if k < 2:
            reload(nc, R, f"l3g{k}_next", hidden[k])


def transpose_weight(nc, R, name, W):
    with Stage(nc, name) as st:
        ws = st.sb("ws", [P, NC, D])
        pt = st.ps("pt", [P, NC, 512])
        loaded = st.sem("weight_loaded")
        turned = st.sem("weight_turned")
        copied = st.sem("weight_copied")
        with st.block() as block:
            @block.sync
            def _(sp):
                sp.dma_start(ws[:], W.rearrange("(c p) n -> p c n", p=P)).then_inc(loaded, 16)

            @block.tensor
            def _(pe):
                pe.wait_ge(loaded, 16)
                for c in range(NC):
                    for o in range(NC):
                        ins = nc.tensor.transpose(pt[:, c, o * P:(o + 1) * P], ws[:, o, c * P:(c + 1) * P],
                                                  R.ident[:])
                ins.then_inc(turned, 1)

            @block.vector
            def _(dve):
                dve.wait_ge(turned, 1)
                nc.vector.tensor_copy(R.we[:, :, 0:D], pt[:, :, 0:D]).then_inc(copied, 1)
                dve.wait_ge(copied, 1)


def similarity_gnn(nc, R, name, table):
    cols = table[0:NP * NP, :].rearrange("(t p n) a -> p t (n a)", p=P, n=NP)
    with Stage(nc, name) as st:
        cnt = st.sb("cnt", [P, 2, T, P])
        th = st.sb("tanh", [P, 2, 512])
        mw = st.sb("weights", [P, 2, 512])
        deg = st.sb("deg", [P, 2, 1])
        ot = st.sb("out", [P, 2, D])
        pt = st.ps("ps", [P, 2, 512])
        po = st.ps("po", [P, 2, 512])
        loaded = [st.sem("cols_loaded0"), st.sem("cols_loaded1")]
        freed = st.sem("cols_used")
        dots = st.sem("dots_ready")
        tanhed = st.sem("tanh_ready")
        weighed = st.sem("weights_ready")
        th_free = st.sem("tanh_slot_free")
        used = st.sem("weights_used")
        out_ready = st.sem("out_ready")
        out_used = st.sem("out_used")
        chain_s = st.sem("dve_chain")
        with st.block() as block:
            @block.sync
            def _(sp):
                def one(jt, slot, first=False):
                    if not first:
                        sp.wait_ge(freed, jt + 1)
                    sp.dma_start(cnt[:, slot], cols[:, :, 0:P] if first else cols[:, :, ds(jt * P, P)]
                                 ).then_inc(loaded[slot], 16)
                one(0, 0, True)
                with sp.Fori(0, T // 2) as g:
                    one(g * 2 + 1, 1)
                    one(g * 2 + 2, 0)

            @block.tensor
            def _(pe):
                pe.sem_inc(freed, 2)
                pe.sem_inc(used, 2)

                def dot(jt, b, q):
                    n = jt * NJ + q
                    pe.wait_ge(tanhed, n + 1)
                    lo, hi = JG[q]
                    for i in range(lo, hi):
                        for c in range(NC):
                            ins = nc.tensor.matmul(pt[:, (b + q) % 2, (i - lo) * P:(i - lo + 1) * P],
                                                   R.xt[:, c, i * P:(i + 1) * P], R.xt[:, c, ds(jt * P, P)],
                                                   start=(c == 0), stop=(c == NC - 1))
                    ins.then_inc(dots, 1)

                def tile(jt, k, b):
                    dot(jt, b, 0)
                    pe.wait_ge(out_used, jt + 1)
                    for q in range(NJ):
                        if q + 1 < NJ:
                            dot(jt, b, q + 1)
                        pe.wait_ge(weighed, jt * NJ + q + 1)
                        multiply_group(nc, pe, mw[:, (b + q) % 2], R.xn, 0, D, q, po[:, b, 0:D]).then_inc(used, 1)
                    for i in range(T):
                        ins = nc.tensor.matmul(po[:, b, D:D + 1], cnt[:, b, i, :], R.ones[:, 0:1], start=(i == 0),
                                               stop=(i == T - 1))
                    ins.then_inc(out_ready, 1)
                    pe.wait_ge(out_ready, jt + 1)
                    pe.sem_inc(freed, 1)

                tile(0, 0, 0)
                with pe.Fori(0, T // 2) as g:
                    tile(g * 2 + 1, g, 1)
                    tile(g * 2 + 2, g + 1, 0)

            @block.scalar
            def _(act):
                act.sem_inc(tanhed, 2)

                def tile(jt, b):
                    for q in range(NJ):
                        w = (JG[q][1] - JG[q][0]) * P
                        n = jt * NJ + q
                        act.wait_ge(dots, n + 1)
                        act.wait_ge(th_free, n + 1)
                        nc.scalar.activation(th[:, (b + q) % 2, 0:w], pt[:, (b + q) % 2, 0:w], ACT.Tanh
                                             ).then_inc(tanhed, 1)
                tile(0, 0)
                with act.Fori(0, T // 2) as g:
                    tile(g * 2 + 1, 1)
                    tile(g * 2 + 2, 0)

            @block.vector
            def _(dve):
                ch = Chain(dve, chain_s)
                dve.sem_inc(out_used, 2)
                dve.sem_inc(th_free, 2)

                def tile(jt, k, b):
                    dve.wait_ge(loaded[b], k * 16 + 16)
                    for q in range(NJ):
                        lo, hi = JG[q]
                        n = jt * NJ + q
                        w = (hi - lo) * P
                        dve.wait_ge(tanhed, n + 3)
                        dve.wait_ge(used, n + 1)
                        nc.vector.tensor_tensor(mw[:, (b + q) % 2, 0:w], th[:, (b + q) % 2, 0:w],
                                                cnt[:, b, lo:hi, :].rearrange("p t n -> p (t n)"), ALU.mult
                                                ).then_inc(weighed, 1)
                        dve.wait_ge(weighed, n + 1)
                        dve.sem_inc(th_free, 1)
                    xi = R.x[:, ds(jt, 1), :].rearrange("p a d -> p (a d)")
                    hi_ = R.xn[:, ds(jt, 1), :].rearrange("p a d -> p (a d)")
                    dve.wait_ge(out_ready, jt + 1)
                    ch.link(nc.vector.tensor_scalar(deg[:, b], po[:, b, D:D + 1], 1.0, None, ALU.max))
                    ch.link(nc.vector.reciprocal(deg[:, b], deg[:, b]))
                    ch.link(nc.vector.tensor_scalar(ot[:, b], po[:, b, 0:D], deg[:, b], 0.9, ALU.mult, ALU.mult))
                    dve.sem_inc(out_used, 1)
                    ch.link(nc.vector.scalar_tensor_tensor(out=ot[:, b], in0=hi_, scalar=0.1, in1=ot[:, b],
                                                           op0=ALU.mult, op1=ALU.add))
                    ch.link(nc.vector.tensor_tensor(xi, xi, ot[:, b], ALU.add))

                tile(0, 0, 0)
                with dve.Fori(0, T // 2) as g:
                    ch.loop(g, 10)
                    tile(g * 2 + 1, g, 1)
                    tile(g * 2 + 2, g + 1, 0)
                ch.end(T // 2)


def l2_gnn(nc, R, A, edges):
    layernorm_T(nc, R, "l2g_ln", R.x)
    transpose_weight(nc, R, "l2g_w", A["L2_gnn_W"])

    def load(sp, W, b, sem):
        sp.dma_start(b[:], row(A["L2_gnn_b"])).then_inc(sem, 16)
        return 16
    project(nc, R, "l2g_h", D, load, [(R.xn, 0, D)], bias=True, W=R.we[:, :, 0:D])
    layernorm_T(nc, R, "l2g_hT", R.xn, norm=False)
    similarity_gnn(nc, R, "l2g", edges)


def router_scores(nc, R, name, gamma, beta, E):
    C = HEADS * E
    with Stage(nc, name) as st:
        c = st.sb("centred", [P, T, C])
        sq = st.sb("squared", [P, T, C])
        mean = st.sb("mean", [P, T])
        gb = st.sb("gb", [P, 2, C])
        loaded = st.sem("gb_loaded")
        var_ready = st.sem("var_ready")
        root_ready = st.sem("root_ready")
        chain_s = st.sem("dve_chain")
        with st.block() as block:
            @block.sync
            def _(sp):
                sp.dma_start(gb[:, 0, :], row(gamma).to_broadcast([P, C])).then_inc(loaded, 16)
                sp.dma_start(gb[:, 1, :], row(beta).to_broadcast([P, C])).then_inc(loaded, 16)

            @block.scalar
            def _(act):
                act.wait_ge(var_ready, 1)
                nc.scalar.activation(mean[:], mean[:], ACT.Sqrt).then_inc(root_ready, 1)

            @block.vector
            def _(dve):
                ch = Chain(dve, chain_s)
                a = R.scores[:, :, 0:C]

                def wide(ap):
                    return ap.unsqueeze(2).to_broadcast([P, T, C])
                ch.link(nc.vector.tensor_reduce(mean[:], a, AX_X, ALU.add))
                ch.link(nc.vector.tensor_scalar(mean[:], mean[:], 1.0 / C, None, ALU.mult))
                ch.link(nc.vector.tensor_tensor(c[:], a, wide(mean[:, :]), ALU.subtract))
                ch.link(nc.vector.tensor_tensor(sq[:], c[:], c[:], ALU.mult))
                ch.link(nc.vector.tensor_reduce(mean[:], sq[:], AX_X, ALU.add))
                nc.vector.tensor_scalar(mean[:], mean[:], 1.0 / C, EPS, ALU.mult, ALU.add).then_inc(var_ready, 1)
                dve.wait_ge(root_ready, 1)
                dve.wait_ge(loaded, 32)
                ch.link(nc.vector.reciprocal(mean[:], mean[:]))
                ch.link(nc.vector.tensor_tensor(c[:], c[:], wide(mean[:, :]), ALU.mult))
                ch.link(nc.vector.tensor_tensor(c[:], c[:], gb[:, 0:1, :].to_broadcast([P, T, C]), ALU.mult))
                ch.link(nc.vector.tensor_tensor(c[:], c[:], gb[:, 1:2, :].to_broadcast([P, T, C]), ALU.add))
                s0 = R.scores[:, :, 0:E]
                ch.link(nc.vector.tensor_tensor(s0, c[:, :, 0:E], c[:, :, E:2 * E], ALU.add))
                for h in range(2, HEADS):
                    ch.link(nc.vector.tensor_tensor(s0, s0, c[:, :, h * E:(h + 1) * E], ALU.add))
                ch.link(nc.vector.tensor_scalar(s0, s0, 1.0 / HEADS, None, ALU.mult))


def l2_ffn(nc, R, A, routes):
    E = 4
    layernorm_T(nc, R, "l2f_ln", R.x)
    gat(nc, R, "l2f", routes, A["L2_ffn_W_gat"], A["L2_ffn_att_src"], A["L2_ffn_att_dst"], A["L2_ffn_b_gat"], E,
        "scores", self_loops=True)
    router_scores(nc, R, "l2f_scores", A["L2_ffn_ln_gamma"], A["L2_ffn_ln_beta"], E)
    top2_gates(nc, R, "l2f_gates", E, False)
    layernorm_T(nc, R, "l2f_ln2", R.x)
    experts(nc, R, "l2f_experts", E, 2 * D, A["L2_ffn_W1"], A["L2_ffn_b1"], A["L2_ffn_W2"], A["L2_ffn_b2"], False)


SH = 8
SG = 64
SD = 64
INNER = SH * SD
PAIRS = SH // 2


def slice_weights(nc, R, name, A, S):
    with Stage(nc, name) as st:
        wx = st.sb("wx", [P, NC, INNER])
        wxT = st.sb("wxT", [P, PAIRS, D])
        bd = st.sb("bd_slice", [P, P])
        bx = st.sb("bx", [P, PAIRS])
        bs = st.sb("b_slice", [1, SG])
        rt = st.sb("temp", [P, SH])
        pt = st.ps("pt", [P, PAIRS, 512])
        pw = st.ps("pw", [P, NC, 512])
        pb = st.ps("pb", [P, 512])
        zeroed = st.sem("bd_zeroed")
        loaded = st.sem("weights_loaded")
        turned = st.sem("wx_turned")
        copied = st.sem("wx_copied")
        multiplied = st.sem("multiplied")
        chain_s = st.sem("dve_chain")
        with st.block() as block:
            @block.gpsimd
            def _(pool):
                nc.gpsimd.memset(bd[:], 0.0).then_inc(zeroed, 1)

            @block.sync
            def _(sp):
                sp.dma_start(wx[:], A["L1_ffn_W_x"].rearrange("(c p) n -> p c n", p=P)).then_inc(loaded, 16)
                sp.dma_start(bx[:], A["L1_ffn_b_x"].rearrange("(k p) -> p k", p=P), allow_slow_non_contiguous=True
                             ).then_inc(loaded, 16)
                sp.dma_start(bs[:], row(A["L1_ffn_b_slice"])).then_inc(loaded, 16)
                sp.dma_start(rt[:], A["L1_ffn_temperature"].rearrange("a h b c -> a (h b c)").to_broadcast([P, SH])
                             ).then_inc(loaded, 16)
                sp.wait_ge(zeroed, 1)
                for k in range(2):
                    sp.dma_start(bd[k * SD:(k + 1) * SD, k * SG:(k + 1) * SG], A["L1_ffn_W_slice"]
                                 ).then_inc(loaded, 16)

            @block.tensor
            def _(pe):
                pe.wait_ge(loaded, 96)
                for k in range(PAIRS):
                    for c in range(NC):
                        ins = nc.tensor.transpose(pt[:, k, c * P:(c + 1) * P], wx[:, c, k * P:(k + 1) * P],
                                                  R.ident[:])
                ins.then_inc(turned, 1)
                pe.wait_ge(copied, 1)
                for k in range(PAIRS):
                    for c in range(NC):
                        nc.tensor.matmul(pw[:, c, k * P:(k + 1) * P], wxT[:, k, c * P:(c + 1) * P], bd[:],
                                         start=True, stop=True)
                    ins = nc.tensor.matmul(pb[0:1, k * P:(k + 1) * P], bx[:, k:k + 1], bd[:], start=True, stop=True)
                ins.then_inc(multiplied, 1)

            @block.vector
            def _(dve):
                ch = Chain(dve, chain_s)
                dve.wait_ge(turned, 1)
                nc.vector.tensor_copy(wxT[:], pt[:, :, 0:D]).then_inc(copied, 1)
                dve.wait_ge(loaded, 96)
                ch.link(nc.vector.tensor_scalar(rt[:], rt[:], 0.1, 5.0, ALU.max, ALU.min))
                ch.link(nc.vector.reciprocal(rt[:], rt[:]))
                dve.wait_ge(multiplied, 1)
                for c in range(NC):
                    ins = nc.vector.tensor_tensor(S.wc[:, c, :].rearrange("p (h g) -> p h g", h=SH),
                                                  pw[:, c, :].rearrange("p (h g) -> p h g", h=SH),
                                                  rt[:, :].unsqueeze(2).to_broadcast([P, SH, SG]), ALU.mult)
                cb = S.cb[:, :].rearrange("p (h g) -> p h g", h=SH)
                ch.link(nc.vector.tensor_tensor(cb, pb[0:1, :].rearrange("p (h g) -> p h g", h=SH),
                                                bs[:, :].unsqueeze(1).to_broadcast([1, SH, SG]), ALU.add))
                ch.link(nc.vector.tensor_tensor(cb, cb, rt[0:1, :].unsqueeze(2).to_broadcast([1, SH, SG]), ALU.mult))


def slice_tokens(nc, R, name, A, S):
    with Stage(nc, name) as st:
        wf = st.sb("wf", [P, NC, INNER])
        bf = st.sb("bf", [1, INNER])
        xs = st.sb("xs", [P, 2, NC, P])
        zero = st.sb("zero", [P, P])
        top = st.sb("top", [P, 2, SH])
        total = st.sb("total", [P, 2, SH])
        sw = st.sb("sw", [P, 2, SH, SG])
        fx = st.sb("fx", [P, 2, PAIRS, P + 1])
        pl = st.ps("pl", [P, 512])
        pf = st.ps("pf", [P, 2, 512])
        pt = st.ps("pt", [P, 2, 512])
        pa = st.ps("pa", [P, 2, 512])
        loaded = st.sem("weights_loaded")
        const = st.sem("constants_set")
        staged = st.sem("tile_staged")
        logits = st.sem("logits_ready")
        logits_read = st.sem("logits_read")
        fx_ready = st.sem("fx_ready")
        fx_copied = st.sem("fx_copied")
        shifted = st.sem("shifted")
        exp_ready = st.sem("exp_ready")
        sw_ready = st.sem("slice_weights_ready")
        sw_turned = st.sem("slice_weights_turned")
        swT_copied = st.sem("turned_copied")
        summed = st.sem("tile_summed")
        done = st.sem("sums_done")
        chain_s = st.sem("dve_chain")
        with st.block() as block:
            @block.sync
            def _(sp):
                sp.dma_start(wf[:], A["L1_ffn_W_fx"].rearrange("(c p) n -> p c n", p=P)).then_inc(loaded, 16)
                sp.dma_start(bf[:], row(A["L1_ffn_b_fx"])).then_inc(loaded, 16)

            @block.gpsimd
            def _(pool):
                nc.gpsimd.memset(zero[:], 0.0).then_inc(const, 1)
                nc.gpsimd.memset(fx[:], 1.0).then_inc(const, 1)

                def tile(it, b):
                    pool.wait_ge(fx_ready, it + 1)
                    nc.gpsimd.tensor_copy(xs[:, b], R.xt[:, :, ds(it * P, P)]).then_inc(staged, 1)
                tile(0, 0)
                with pool.Fori(0, T // 2) as g:
                    tile(g * 2 + 1, 1)
                    tile(g * 2 + 2, 0)

            @block.tensor
            def _(pe):
                pe.sem_inc(fx_ready, 2)
                pe.sem_inc(summed, 2)
                pe.wait_ge(loaded, 32)
                pe.wait_ge(const, 2)
                for k in range(2):
                    nc.tensor.matmul(pa[:, k, 0:2 * (P + 1)], zero[:],
                                     fx[:, 0, 0:2, :].rearrange("p k c -> p (k c)"), start=True, stop=False,
                                     skip_group_check=True)

                def project_tile(it, b):
                    pe.wait_ge(staged, it + 1)
                    pe.wait_ge(logits_read, it + 1)
                    for c in range(NC):
                        nc.tensor.matmul(pl[:], xs[:, b, c], S.wc[:, c, :], start=(c == 0), stop=False)
                    nc.tensor.matmul(pl[:], R.ones[0:1, :], S.cb[:], start=False, stop=True).then_inc(logits, 1)
                    pe.wait_ge(fx_copied, it + 1)
                    for c in range(NC):
                        nc.tensor.matmul(pf[:, b], xs[:, b, c], wf[:, c, :], start=(c == 0), stop=False)
                    nc.tensor.matmul(pf[:, b], R.ones[0:1, :], bf[:], start=False, stop=True).then_inc(fx_ready, 1)

                def sum_tile(it, b):
                    pe.wait_ge(sw_ready, it + 1)
                    pe.wait_ge(swT_copied, it + 1)
                    for k in range(PAIRS):
                        ins = nc.tensor.transpose(pt[:, b, k * P:(k + 1) * P],
                                                  sw[:, b, 2 * k:2 * k + 2, :].rearrange("p h g -> p (h g)"),
                                                  R.ident[:])
                    ins.then_inc(sw_turned, 1)
                    pe.wait_ge(fx_copied, it + 3)
                    for k in range(PAIRS):
                        o = (k % 2) * (P + 1)
                        ins = nc.tensor.matmul(pa[:, k // 2, o:o + P + 1],
                                               sw[:, b, 2 * k:2 * k + 2, :].rearrange("p h g -> p (h g)"),
                                               fx[:, b, k, :], start=False, stop=False, skip_group_check=True)
                    ins.then_inc(summed, 1)

                def tile(it, b):
                    project_tile(it, b)
                    sum_tile(it, b)

                tile(0, 0)
                with pe.Fori(0, T // 2) as g:
                    tile(g * 2 + 1, 1)
                    tile(g * 2 + 2, 0)
                for k in range(2):
                    ins = nc.tensor.matmul(pa[:, k, 0:2 * (P + 1)], zero[:],
                                           fx[:, 0, 0:2, :].rearrange("p k c -> p (k c)"), start=False, stop=True,
                                           skip_group_check=True)
                ins.then_inc(done, 1)

            @block.scalar
            def _(act):
                act.sem_inc(fx_copied, 2)
                act.sem_inc(swT_copied, 2)
                act.wait_ge(const, 2)

                def tile(it, b):
                    act.wait_ge(fx_ready, it + 3)
                    act.wait_ge(summed, it + 1)
                    nc.scalar.activation(fx[:, b, :, 0:P], pf[:, b].rearrange("p (k c) -> p k c", k=PAIRS), ACT.Copy
                                         ).then_inc(fx_copied, 1)
                    act.wait_ge(shifted, it + 1)
                    nc.scalar.activation(sw[:, b], sw[:, b], ACT.Exp).then_inc(exp_ready, 1)
                    act.wait_ge(sw_turned, it + 1)
                    nc.scalar.activation(S.swT[:, :, ds(it * P, P)], pt[:, b].rearrange("p (k n) -> p k n", k=PAIRS),
                                         ACT.Copy).then_inc(swT_copied, 1)
                tile(0, 0)
                with act.Fori(0, T // 2) as g:
                    tile(g * 2 + 1, 1)
                    tile(g * 2 + 2, 0)

            @block.vector
            def _(dve):
                ch = Chain(dve, chain_s)
                dve.sem_inc(logits_read, 1)

                def tile(it, b):
                    lg = pl[:].rearrange("p (h g) -> p h g", h=SH)
                    dve.wait_ge(logits, it + 1)
                    ch.link(nc.vector.tensor_reduce(top[:, b], lg, AX_X, ALU.max))
                    dve.wait_ge(summed, it + 1)
                    nc.vector.tensor_tensor(sw[:, b], lg, top[:, b].unsqueeze(2).to_broadcast([P, SH, SG]),
                                            ALU.subtract).then_inc(shifted, 1)
                    dve.wait_ge(shifted, it + 1)
                    dve.sem_inc(logits_read, 1)
                    dve.wait_ge(exp_ready, it + 1)
                    ch.link(nc.vector.tensor_reduce(total[:, b], sw[:, b], AX_X, ALU.add))
                    ch.link(nc.vector.reciprocal(total[:, b], total[:, b]))
                    ch.link(nc.vector.tensor_scalar(total[:, b], total[:, b], R.valid[:, ds(it, 1)], None, ALU.mult))
                    nc.vector.tensor_tensor(sw[:, b], sw[:, b], total[:, b].unsqueeze(2).to_broadcast([P, SH, SG]),
                                            ALU.mult).then_inc(sw_ready, 1)
                tile(0, 0)
                with dve.Fori(0, T // 2) as g:
                    ch.loop(g, 8)
                    tile(g * 2 + 1, 1)
                    tile(g * 2 + 2, 0)
                ch.end(T // 2)
                dve.wait_ge(done, 1)
                for k in range(PAIRS):
                    o = (k % 2) * (P + 1)
                    ins = nc.vector.tensor_copy(S.tok[:, k, :], pa[:, k // 2, o:o + P + 1])
                ch.link(ins)


def slice_attention(nc, R, name, A, S):
    SCALE = float(SD) ** -0.5
    with Stage(nc, name) as st:
        bd = st.sb("bd", [P, P])
        off = st.sb("off", [P, P])
        w3 = st.sb("w_qkv", [P, 3, P])
        wo = st.sb("wo", [P, PAIRS, D])
        nrm = st.sb("norm", [P, PAIRS])
        tb = st.sb("tokens", [P, PAIRS, P])
        tT = st.sb("tokens_T", [P, PAIRS, P])
        qT = st.sb("qT", [P, PAIRS, P])
        kT = st.sb("kT", [P, PAIRS, P])
        v = st.sb("v", [P, PAIRS, P])
        at = st.sb("attn", [P, PAIRS, P])
        top = st.sb("top", [P, PAIRS])
        aT = st.sb("attn_T", [P, PAIRS, P])
        oT = st.sb("out_T", [P, PAIRS, P])
        ps = st.ps("ps", [P, 6, 512])
        pz = st.ps("pz", [P, 2, 512])
        zeroed = st.sem("zeroed")
        loaded = st.sem("weights_loaded")
        made = st.sem("mask_made")
        pe_done = st.sem("pe_step_done")
        dve_done = st.sem("dve_step_done")
        exp_ready = st.sem("exp_ready")
        chain_s = st.sem("dve_chain")

        def four(bank):
            return ps[:, bank, :].rearrange("p (k c) -> p k c", k=PAIRS)

        with st.block() as block:
            @block.gpsimd
            def _(pool):
                nc.gpsimd.memset(w3[:], 0.0).then_inc(zeroed, 1)
                nc.gpsimd.memset(bd[:], 1.0).then_inc(made, 1)
                pool.wait_ge(made, 1)
                nc.gpsimd.affine_select(out=bd[:, SG:P], in_=bd[:, SG:P], compare_op=ALU.is_ge, fill=0.0, base=-SG,
                                        pattern=[[0, SG]], channel_multiplier=1).then_inc(made, 1)
                nc.gpsimd.affine_select(out=bd[:, 0:SG], in_=bd[:, 0:SG], compare_op=ALU.is_gt, fill=0.0, base=SG,
                                        pattern=[[0, SG]], channel_multiplier=-1).then_inc(made, 1)

            @block.sync
            def _(sp):
                sp.dma_start(wo[:], A["L1_ffn_W_out"].rearrange("(k p) d -> p k d", p=P)).then_inc(loaded, 16)
                sp.wait_ge(zeroed, 1)
                for i, w in enumerate(("L1_ffn_W_q", "L1_ffn_W_k", "L1_ffn_W_v")):
                    for h in range(2):
                        sp.dma_start(w3[h * SD:(h + 1) * SD, i, h * SD:(h + 1) * SD], A[w]).then_inc(loaded, 16)

            @block.tensor
            def _(pe):
                pe.wait_ge(dve_done, 1)
                for k in range(PAIRS):
                    ins = nc.tensor.transpose(ps[:, 0, k * P:(k + 1) * P], tb[:, k], R.ident[:])
                ins.then_inc(pe_done, 1)
                pe.wait_ge(loaded, 16 * 7)
                pe.wait_ge(dve_done, 2)
                for k in range(PAIRS):
                    nc.tensor.matmul(ps[:, 1, k * P:(k + 1) * P], w3[:, 0], tT[:, k], start=True, stop=True)
                    nc.tensor.matmul(ps[:, 2, k * P:(k + 1) * P], w3[:, 1], tT[:, k], start=True, stop=True)
                    ins = nc.tensor.matmul(ps[:, 3, k * P:(k + 1) * P], tT[:, k], w3[:, 2], start=True, stop=True)
                ins.then_inc(pe_done, 1)
                pe.wait_ge(dve_done, 3)
                for k in range(PAIRS):
                    ins = nc.tensor.matmul(ps[:, 4, k * P:(k + 1) * P], qT[:, k], kT[:, k], start=True, stop=True)
                ins.then_inc(pe_done, 1)
                pe.wait_ge(dve_done, 4)
                for k in range(PAIRS):
                    ins = nc.tensor.transpose(ps[:, 5, k * P:(k + 1) * P], at[:, k], R.ident[:])
                ins.then_inc(pe_done, 1)
                pe.wait_ge(dve_done, 5)
                for k in range(PAIRS):
                    ins = nc.tensor.matmul(ps[:, 0, k * P:(k + 1) * P], v[:, k], aT[:, k], start=True, stop=True)
                ins.then_inc(pe_done, 1)
                pe.wait_ge(dve_done, 6)
                for k in range(PAIRS):
                    ins = nc.tensor.matmul(pz[:, k // 2, (k % 2) * D:(k % 2 + 1) * D], oT[:, k], wo[:, k], start=True,
                                           stop=True)
                ins.then_inc(pe_done, 1)

            @block.scalar
            def _(act):
                act.wait_ge(made, 4)
                nc.scalar.activation(at[:], at[:], ACT.Exp).then_inc(exp_ready, 1)

            @block.vector
            def _(dve):
                ch = Chain(dve, chain_s)
                dve.wait_ge(made, 3)
                ch.link(nc.vector.tensor_scalar(off[:], bd[:], -1.0, BIG, ALU.add, ALU.mult))
                ch.link(nc.vector.tensor_scalar(nrm[:], S.tok[:, :, P], 1e-5, None, ALU.add))
                ch.link(nc.vector.reciprocal(nrm[:], nrm[:]))
                ch.link(nc.vector.tensor_tensor(tb[:], S.tok[:, :, 0:P], nrm[:, :].unsqueeze(2).to_broadcast([P, PAIRS, P]),
                                                ALU.mult))
                nc.vector.tensor_tensor(tb[:], tb[:], bd[:, :].unsqueeze(1).to_broadcast([P, PAIRS, P]), ALU.mult
                                        ).then_inc(dve_done, 1)
                dve.wait_ge(pe_done, 1)
                nc.vector.tensor_copy(tT[:], four(0)).then_inc(dve_done, 1)
                dve.wait_ge(pe_done, 2)
                nc.vector.tensor_copy(qT[:], four(1))
                nc.vector.tensor_copy(kT[:], four(2))
                nc.vector.tensor_copy(v[:], four(3)).then_inc(dve_done, 1)
                dve.wait_ge(pe_done, 3)
                ch.link(nc.vector.tensor_scalar(at[:], four(4), SCALE, None, ALU.mult))
                ch.link(nc.vector.tensor_tensor(at[:], at[:], off[:, :].unsqueeze(1).to_broadcast([P, PAIRS, P]),
                                                ALU.add))
                ch.link(nc.vector.tensor_reduce(top[:], at[:], AX_X, ALU.max))
                nc.vector.tensor_tensor(at[:], at[:], top[:, :].unsqueeze(2).to_broadcast([P, PAIRS, P]), ALU.subtract
                                        ).then_inc(made, 1)
                dve.wait_ge(exp_ready, 1)
                ch.link(nc.vector.tensor_reduce(top[:], at[:], AX_X, ALU.add))
                ch.link(nc.vector.reciprocal(top[:], top[:]))
                nc.vector.tensor_tensor(at[:], at[:], top[:, :].unsqueeze(2).to_broadcast([P, PAIRS, P]), ALU.mult
                                        ).then_inc(dve_done, 1)
                dve.wait_ge(pe_done, 4)
                nc.vector.tensor_copy(aT[:], four(5)).then_inc(dve_done, 1)
                dve.wait_ge(pe_done, 5)
                nc.vector.tensor_copy(oT[:], four(0)).then_inc(dve_done, 1)
                dve.wait_ge(pe_done, 6)
                nc.vector.tensor_copy(S.z[:].rearrange("p (a k) d -> p a k d", a=2),
                                      pz[:, :, :].rearrange("p a (k d) -> p a k d", k=2)).then_inc(dve_done, 1)
                dve.wait_ge(dve_done, 7)


def slice_spread(nc, R, name, A, S):
    with Stage(nc, name) as st:
        bo = st.sb("bo", [1, D])
        ss = st.sb("sw_staged", [P, U, PAIRS, P])
        po = st.ps("po", [P, U, 512])
        loaded = st.sem("bias_loaded")
        staged = st.sem("tile_staged")
        out_ready = st.sem("out_ready")
        added = st.sem("tile_added")
        with st.block() as block:
            @block.sync
            def _(sp):
                sp.dma_start(bo[:], row(A["L1_ffn_b_out"])).then_inc(loaded, 16)

            @block.scalar
            def _(act):
                with act.Fori(0, G) as g:
                    for u in range(U):
                        act.wait_ge(out_ready, g * U + u + 1)
                        nc.scalar.activation(ss[:, u], S.swT[:, :, ds((g * U + u) * P, P)], ACT.Copy
                                             ).then_inc(staged, 1)

            @block.tensor
            def _(pe):
                pe.sem_inc(out_ready, U)
                pe.wait_ge(loaded, 16)
                with pe.Fori(0, G) as g:
                    for u in range(U):
                        pe.wait_ge(staged, g * U + u + 1)
                        pe.wait_ge(added, g * U + u + 1)
                        for k in range(PAIRS):
                            nc.tensor.matmul(po[:, u, 0:D], ss[:, u, k], S.z[:, k], start=(k == 0), stop=False)
                        nc.tensor.matmul(po[:, u, 0:D], R.ones[0:1, :], bo[:], start=False, stop=True
                                         ).then_inc(out_ready, 1)

            @block.vector
            def _(dve):
                dve.sem_inc(added, U)
                with dve.Fori(0, G) as g:
                    for u in range(U):
                        xi = R.x[:, ds(g * U + u, 1), :].rearrange("p a d -> p (a d)")
                        dve.wait_ge(out_ready, g * U + u + 1 + U)
                        nc.vector.tensor_tensor(xi, xi, po[:, u, 0:D], ALU.add).then_inc(added, 1)


def l1_ffn(nc, R, A):
    class S:
        pass
    layernorm_T(nc, R, "l1f_ln", R.x)
    with ExitStack() as ctx:
        def sb(name, shape):
            return ctx.enter_context(nc.sbuf_tensor("l1f_" + name, shape, F32))
        S.wc = sb("wc", [P, NC, INNER])
        S.cb = sb("cb", [1, INNER])
        S.swT = sb("swT", [P, PAIRS, NP])
        S.tok = sb("tok", [P, PAIRS, P + 1])
        S.z = sb("z", [P, PAIRS, D])
        slice_weights(nc, R, "l1f_w", A, S)
        slice_tokens(nc, R, "l1f_tok", A, S)
        slice_attention(nc, R, "l1f_att", A, S)
        slice_spread(nc, R, "l1f_out", A, S)


NT = 4
RELS = 8
DK = D // HEADS
STREAMS = 4
ROW = D + 2 * HEADS


def node_types(nc, R, name, node_type, skip, S):
    with Stage(nc, name) as st:
        nt = st.sb("nt", [P, T], I32)
        sk = st.sb("skip", [P, NT])
        zeroed = st.sem("nt_zeroed")
        loaded = st.sem("loaded")
        sig_ready = st.sem("sigmoid_ready")
        chain_s = st.sem("dve_chain")
        with st.block() as block:
            @block.gpsimd
            def _(pool):
                nc.gpsimd.memset(nt[:], 0).then_inc(zeroed, 1)

            @block.sync
            def _(sp):
                sp.dma_start(sk[:], row(skip).to_broadcast([P, NT])).then_inc(loaded, 16)
                sp.wait_ge(zeroed, 1)
                sp.dma_start(nt[:, 0:T - 1], node_type[0:(T - 1) * P].rearrange("(t p) -> p t", p=P),
                             allow_slow_non_contiguous=True).then_inc(loaded, 16)
                sp.dma_start(nt[0:LAST, T - 1:T], col(node_type[(T - 1) * P:N])).then_inc(loaded, 16)

            @block.scalar
            def _(act):
                act.wait_ge(loaded, 48)
                nc.scalar.activation(sk[:], sk[:], ACT.Sigmoid).then_inc(sig_ready, 1)

            @block.vector
            def _(dve):
                ch = Chain(dve, chain_s)
                dve.wait_ge(loaded, 48)
                for k in range(NT):
                    ins = nc.vector.tensor_scalar(S.oh[:, :, k], nt[:], float(k), None, ALU.is_equal)
                ch.link(ins)
                dve.wait_ge(sig_ready, 1)
                ch.link(nc.vector.tensor_tensor(S.ohg[:], S.oh[:], sk[:, :].unsqueeze(1).to_broadcast([P, T, NT]),
                                                ALU.mult))


def typed_project(nc, R, name, W, oh, dst, add, clear=None):
    with Stage(nc, name) as st:
        ws = st.sb("W", [P, NC, NT, D])
        xs = st.sb("xs", [P, 2, NC, P])
        pt = st.ps("pt", [P, 2, NT // 2, 512])
        loaded = st.sem("weights_loaded")
        staged = st.sem("tile_staged")
        multiplied = st.sem("tile_multiplied")
        chosen = st.sem("tile_chosen")
        chain_s = st.sem("dve_chain")
        if clear is not None:
            zeros = st.sb("zeros", [P, NP])
            zeroed = st.sem("zeros_set")
            cleared = st.sem("table_cleared")
        with st.block() as block:
            @block.sync
            def _(sp):
                for c in range(NC):
                    sp.dma_start(ws[:, c], W[:, c * P:(c + 1) * P, :].rearrange("t p n -> p t n")
                                 ).then_inc(loaded, 16)
                if clear is not None:
                    rows = table_rows(clear)
                    sp.wait_ge(zeroed, 1)
                    with sp.Fori(0, T) as t:
                        sp.dma_start(rows[ds(t, 1)].rearrange("a p n -> p (a n)"), zeros[:]).then_inc(cleared, 16)
                    sp.dma_start(clear[NP * NP:, :].rearrange("(p k) a -> p (k a)", p=P),
                                 zeros[:, 0:EdgeCounter.W]).then_inc(cleared, 16)
                    sp.wait_ge(cleared, 16 * (T + 1))

            if clear is not None:
                @block.gpsimd
                def _(pool):
                    nc.gpsimd.memset(zeros[:], 0.0).then_inc(zeroed, 1)

            @block.scalar
            def _(act):
                def tile(it, b):
                    act.wait_ge(multiplied, it + 1)
                    nc.scalar.activation(xs[:, b], R.xt[:, :, ds(it * P, P)], ACT.Copy).then_inc(staged, 1)
                tile(0, 0)
                with act.Fori(0, T // 2) as g:
                    tile(g * 2 + 1, 1)
                    tile(g * 2 + 2, 0)

            @block.tensor
            def _(pe):
                pe.sem_inc(multiplied, 2)
                pe.wait_ge(loaded, 16 * NC)

                def tile(it, b):
                    pe.wait_ge(staged, it + 1)
                    pe.wait_ge(chosen, it + 1)
                    for k in range(NT // 2):
                        for c in range(NC):
                            ins = nc.tensor.matmul(pt[:, b, k], xs[:, b, c],
                                                   ws[:, c, 2 * k:2 * k + 2, :].rearrange("p t n -> p (t n)"),
                                                   start=(c == 0), stop=(c == NC - 1))
                    ins.then_inc(multiplied, 1)
                tile(0, 0)
                with pe.Fori(0, T // 2) as g:
                    tile(g * 2 + 1, 1)
                    tile(g * 2 + 2, 0)

            @block.vector
            def _(dve):
                ch = Chain(dve, chain_s)
                dve.sem_inc(chosen, 2)

                def tile(it, b):
                    o = dst[:, ds(it, 1), :].rearrange("p a d -> p (a d)")
                    dve.wait_ge(multiplied, it + 3)
                    for k in range(NT):
                        y = pt[:, b, k // 2, (k % 2) * D:(k % 2 + 1) * D]
                        f = oh[:, ds(it, 1), k]
                        if k == 0 and not add:
                            ch.link(nc.vector.tensor_scalar(o, y, f, None, ALU.mult))
                        else:
                            ch.link(nc.vector.scalar_tensor_tensor(out=o, in0=y, scalar=f, in1=o, op0=ALU.mult,
                                                                   op1=ALU.add))
                    dve.sem_inc(chosen, 1)
                tile(0, 0)
                with dve.Fori(0, T // 2) as g:
                    ch.loop(g, 2 * NT)
                    tile(g * 2 + 1, 1)
                    tile(g * 2 + 2, 0)
                ch.end(T // 2)


def relation_table(nc, R, name, rel, pri, extra, dram):
    C = D + (D if extra is not None else 0)
    with Stage(nc, name) as st:
        bd = st.sb("bd", [P, NC, RELS, P])
        pr = st.sb("pri", [P, RELS * HEADS])
        xs = st.sb("xs", [P, 2, NC, P])
        ot = st.sb("rows", [P, 2, RELS, C])
        pt = st.ps("pt", [P, 2 * NC * 2, 512])
        zeroed = st.sem("bd_zeroed")
        loaded = st.sem("weights_loaded")
        scaled = st.sem("weights_scaled")
        staged = st.sem("tile_staged")
        multiplied = st.sem("tile_multiplied")
        copied = st.sem("tile_copied")
        extra_copied = st.sem("extra_copied")
        slot_free = st.sem("rows_slot_free")
        admitted = st.sem("store_admitted")
        stored = [st.sem("rows_stored0"), st.sem("rows_stored1")]
        chain_s = st.sem("dve_chain")
        rows = dram[:, :].rearrange("(n r) c -> n (r c)", r=RELS)
        with st.block() as block:
            @block.gpsimd
            def _(pool):
                nc.gpsimd.memset(bd[:], 0.0).then_inc(zeroed, 1)

                def tile(it, b):
                    pool.wait_ge(multiplied, it + 1)
                    nc.gpsimd.tensor_copy(xs[:, b], R.xt[:, :, ds(it * P, P)]).then_inc(staged, 1)
                tile(0, 0)
                with pool.Fori(0, T // 2) as g:
                    tile(g * 2 + 1, 1)
                    tile(g * 2 + 2, 0)

            @block.sync
            def _(sp):
                sp.dma_start(pr[:], row(pri.rearrange("r h -> (r h)")).to_broadcast([P, RELS * HEADS])
                             ).then_inc(loaded, 16)
                sp.wait_ge(zeroed, 1)
                for h in range(HEADS):
                    lo = (h % 2) * DK
                    sp.dma_start(bd[lo:lo + DK, h // 2, :, lo:lo + DK], rel[:, h].rearrange("r d e -> d r e")
                                 ).then_inc(loaded, 16)

                def tile(it, k, b):
                    sp.wait_ge(copied, it + 3)
                    if extra is not None:
                        sp.sem_inc(admitted, 1)
                        sp.wait_ge(extra_copied, it + 1)
                    sp.sem_inc(admitted, 1)
                    sp.dma_start(rows[ds(it * P, P), :], ot[:, b].rearrange("p r c -> p (r c)")
                                 ).then_inc(stored[b], 16)
                    sp.wait_ge(stored[b], k * 16 + 16)
                    sp.sem_inc(slot_free, 1)
                tile(0, 0, 0)
                with sp.Fori(0, T // 2) as g:
                    tile(g * 2 + 1, g, 1)
                    tile(g * 2 + 2, g + 1, 0)

            @block.tensor
            def _(pe):
                pe.sem_inc(multiplied, 2)
                pe.wait_ge(scaled, 1)

                def tile(it, b):
                    pe.wait_ge(staged, it + 1)
                    pe.wait_ge(copied, it + 1)
                    for c in range(NC):
                        for k in range(2):
                            ins = nc.tensor.matmul(pt[:, b * 4 + c * 2 + k, :], xs[:, b, c],
                                                   bd[:, c, 4 * k:4 * k + 4, :].rearrange("p r n -> p (r n)"),
                                                   start=True, stop=True)
                    ins.then_inc(multiplied, 1)
                tile(0, 0)
                with pe.Fori(0, T // 2) as g:
                    tile(g * 2 + 1, 1)
                    tile(g * 2 + 2, 0)

            @block.scalar
            def _(act):
                act.sem_inc(copied, 2)
                act.sem_inc(slot_free, 2)

                def tile(it, b):
                    act.wait_ge(multiplied, it + 3)
                    act.wait_ge(slot_free, it + 1)
                    for c in range(NC):
                        for k in range(2):
                            ins = nc.scalar.activation(ot[:, b, 4 * k:4 * k + 4, c * P:(c + 1) * P],
                                                       pt[:, b * 4 + c * 2 + k, :].rearrange("p (r n) -> p r n", r=4),
                                                       ACT.Copy)
                    ins.then_inc(copied, 1)
                tile(0, 0)
                with act.Fori(0, T // 2) as g:
                    tile(g * 2 + 1, 1)
                    tile(g * 2 + 2, 0)

            @block.vector
            def _(dve):
                ch = Chain(dve, chain_s)
                dve.wait_ge(loaded, 16 * (1 + HEADS))
                if extra is None:
                    ch.link(nc.vector.tensor_scalar(pr[:], pr[:], float(DK) ** -0.5, None, ALU.mult))
                    prv = pr[:, :].rearrange("p (r h) -> p r h", h=HEADS)
                    for h in range(HEADS):
                        lo = (h % 2) * DK
                        blk = bd[lo:lo + DK, h // 2, :, lo:lo + DK]
                        ins = nc.vector.tensor_tensor(blk, blk, prv[lo:lo + DK, :, h].unsqueeze(2)
                                                      .to_broadcast([DK, RELS, DK]), ALU.mult)
                    ch.link(ins)
                dve.sem_inc(scaled, 1)
                if extra is not None:
                    def tile(it, b):
                        dve.wait_ge(slot_free, it + 1)
                        nc.vector.tensor_copy(ot[:, b, :, D:C], extra[:, ds(it, 1), :].to_broadcast([P, RELS, D])
                                              ).then_inc(extra_copied, 1)
                    tile(0, 0)
                    with dve.Fori(0, T // 2) as g:
                        tile(g * 2 + 1, 1)
                        tile(g * 2 + 2, 0)


def clear_sums(nc, R, name, sums):
    with Stage(nc, name) as st:
        init = st.sb("init", [P, ROW])
        made = st.sem("init_made")
        stored = st.sem("init_stored")
        with st.block() as block:
            @block.gpsimd
            def _(pool):
                nc.gpsimd.memset(init[:, 0:D + HEADS], 0.0).then_inc(made, 1)
                nc.gpsimd.memset(init[:, D + HEADS:ROW], -BIG).then_inc(made, 1)

            @block.sync
            def _(sp):
                sp.wait_ge(made, 2)
                with sp.Fori(0, T + 1) as t:
                    for k in range(STREAMS):
                        sp.dma_start(sums[k][ds(t * P, P), :], init[:]).then_inc(stored, 16)
                sp.wait_ge(stored, 16 * STREAMS * (T + 1))


def edge_sums(nc, R, name, src, dst, etype, E, qtab, vktab, sums):
    EC = -(-E // P)
    EC += -EC % (2 * STREAMS)
    full, rest = E // EC, E % EC
    S = STREAMS
    GR = EC // S
    XC = EC + 2 * S
    with Stage(nc, name) as st:
        ends = st.sb("ends", [P, 3, XC], I32)
        key = st.sb("key", [P, XC])
        tmp = st.sb("tmp", [P, XC])
        idx_all = st.sb("idx_all", [P, XC, 3], I32)
        spare_i = st.sb("spare_i", [P, 1], I32)
        spare = st.sb("spare", [P, 1])
        idx = st.sb("idx", [P, 2, S, 3], I32)
        widx = st.sb("write_idx", [P, S], I32)
        kb = st.sb("key_wide", [P, 2, S, P])
        eq = st.sb("same", [P, S, P])
        neg = st.sb("neg", [P, S, P])
        low = st.sb("same_earlier", [P, S, P])
        before = st.sb("before", [P, S])
        q = st.sb("q", [P, 2, S, D])
        vk = st.sb("vk", [P, 2, S, 2 * D])
        old = st.sb("old", [P, S, ROW])
        new = st.sb("new", [P, S, ROW])
        prod = st.sb("prod", [P, S, D])
        score = st.sb("score", [P, S, HEADS])
        sw = st.sb("score_wide", [P, S, HEADS, P])
        msk = st.sb("masked", [P, S, HEADS, P])
        top = st.sb("top", [P, S, HEADS])
        ex = st.sb("exponents", [P, S, 2 * HEADS])
        w = st.sb("weighted", [P, S, ROW])
        pk = st.ps("pk", [P, S, 512])
        pr = st.ps("pr", [P, S, 512])
        padded = st.sem("padding_set")
        loaded = st.sem("edges_loaded")
        const = st.sem("spare_made")
        chain_s = st.sem("dve_chain")
        kb_ready = st.sem("key_wide_ready")
        keys_ready = st.sem("keys_ready")
        idx_ready = st.sem("idx_ready")
        key_rows = st.sem("key_rows_ready")
        sw_ready = st.sem("score_wide_ready")
        score_rows = st.sem("score_rows_ready")
        ex_ready = st.sem("exponents_ready")
        w_ready = st.sem("weights_ready")
        weighted = st.sem("weighted_ready")
        summed = st.sem("column_summed")
        new_ready = st.sem("new_ready")
        written = st.sem("sum_written")
        admitted = st.sem("pool_admitted")
        score_ready = st.sem("score_ready")
        eq_ready = st.sem("same_ready")
        neg_ready = st.sem("neg_ready")
        old_scaled = st.sem("old_scaled")
        rows_gathered = [[st.sem(f"rows_gathered{b}{k}") for k in range(S)] for b in range(2)]
        old_gathered = [st.sem(f"old_gathered{k}") for k in range(S)]
        scattered = [st.sem(f"sum_scattered{k}") for k in range(S)]
        with st.block() as block:
            @block.sync
            def _(sp):
                sp.wait_ge(padded, 3)
                for k, ap in enumerate((src, dst, etype)):
                    sp.dma_start(ends[0:full, k, 0:EC], ap[0:full * EC].rearrange("(p k) -> p k", k=EC)
                                 ).then_inc(loaded, 16)
                    sp.dma_start(ends[full:full + 1, k, 0:rest], row(ap[full * EC:E])).then_inc(loaded, 16)

            @block.gpsimd
            def _(pool):
                nc.gpsimd.memset(ends[:, 0], NP - 1).then_inc(padded, 1)
                nc.gpsimd.memset(ends[:, 1], NP - 1).then_inc(padded, 1)
                nc.gpsimd.memset(ends[:, 2], 0).then_inc(padded, 1)
                nc.gpsimd.iota(spare_i[:], pattern=[[0, 1]], base=NP, channel_multiplier=1).then_inc(const, 1)

                def gather_rows(b, n, k):
                    pool.wait_ge(idx_ready, n * S + k + 1)
                    pool.sem_inc(admitted, 1)
                    for slot, (buf, tab) in enumerate(((q, qtab), (vk, vktab))):
                        nc.gpsimd.indirect_dma_start(
                            out=buf[:, b, k], out_offset=None, in_=tab[:, :],
                            in_offset=bass.IndirectOffsetOnAxis(ap=idx[:, b, k, slot:slot + 1], axis=0)
                        ).then_inc(rows_gathered[b][k], 16)

                for b in range(2):
                    for k in range(S):
                        gather_rows(b, b, k)
                with pool.Fori(0, GR // 2) as g:
                    for b in range(2):
                        n = g * 2 + b
                        for k in range(S):
                            nc.gpsimd.indirect_dma_start(
                                out=old[:, k], out_offset=None, in_=sums[k][:, :],
                                in_offset=bass.IndirectOffsetOnAxis(ap=idx[:, b, k, 2:3], axis=0)
                            ).then_inc(old_gathered[k], 16)
                        for k in range(S):
                            pool.wait_ge(new_ready, n * S + k + 1)
                            pool.sem_inc(admitted, 1)
                            nc.gpsimd.indirect_dma_start(
                                out=sums[k][:, :], in_=new[:, k], in_offset=None,
                                out_offset=bass.IndirectOffsetOnAxis(ap=widx[:, k:k + 1], axis=0)
                            ).then_inc(scattered[k], 16)
                        for k in range(S):
                            gather_rows(b, n + 2, k)
                        for k in range(S):
                            pool.wait_ge(scattered[k], n * 16 + 16)
                            pool.sem_inc(written, 1)
                for b in range(2):
                    for k in range(S):
                        pool.wait_ge(rows_gathered[b][k], (GR // 2 + 1) * 32)

            @block.tensor
            def _(pe):
                def key_row(b, n, k):
                    pe.wait_ge(kb_ready, n * S + k + 1)
                    pe.wait_ge(eq_ready, n * S + k + 1)
                    nc.tensor.transpose(pk[:, k, 0:P], kb[:, b, k], R.ident[:]).then_inc(key_rows, 1)

                pe.sem_inc(eq_ready, S)
                for k in range(S):
                    key_row(0, 0, k)
                with pe.Fori(0, GR // 2) as g:
                    for b in range(2):
                        n = g * 2 + b
                        for k in range(S):
                            pe.wait_ge(sw_ready, n * S + k + 1)
                            for h in range(HEADS):
                                ins = nc.tensor.transpose(pr[:, k, h * P:(h + 1) * P], sw[:, k, h], R.ident[:])
                            ins.then_inc(score_rows, 1)
                        for k in range(S):
                            key_row(1 - b, n + 1, k)
                        for k in range(S):
                            pe.wait_ge(weighted, n * S + k + 1)
                            nc.tensor.matmul(pk[:, k, P:P + D + HEADS], eq[:, k], w[:, k, 0:D + HEADS], start=True,
                                             stop=True).then_inc(summed, 1)

            @block.scalar
            def _(act):
                act.wait_ge(keys_ready, 1)
                for k in range(S):
                    nc.scalar.activation(kb[:, 0, k], key[:, k:k + 1].to_broadcast([P, P]), ACT.Copy
                                         ).then_inc(kb_ready, 1)
                with act.Fori(0, GR // 2) as g:
                    for b in range(2):
                        n = g * 2 + b
                        for k in range(S):
                            act.wait_ge(key_rows, n * S + k + 1)
                            nc.scalar.activation(kb[:, 1 - b, k],
                                                 key[:, ds((n + 1) * S + k, 1)].to_broadcast([P, P]), ACT.Copy
                                                 ).then_inc(kb_ready, 1)
                        for k in range(S):
                            act.wait_ge(eq_ready, n * S + k + 1 + S)
                            nc.scalar.activation(neg[:, k], eq[:, k], ACT.Copy, scale=BIG, bias=-BIG
                                                 ).then_inc(neg_ready, 1)
                            act.wait_ge(score_ready, n * S + k + 1)
                            nc.scalar.activation(sw[:, k], score[:, k].unsqueeze(2).to_broadcast([P, HEADS, P]),
                                                 ACT.Copy).then_inc(sw_ready, 1)
                        for k in range(S):
                            act.wait_ge(ex_ready, n * S + k + 1)
                            nc.scalar.activation(w[:, k, D:ROW], ex[:, k], ACT.Exp).then_inc(w_ready, 1)
                        for k in range(S):
                            act.wait_ge(w_ready, n * S + k + 1)
                            for h in range(HEADS):
                                cut = slice(h * DK, (h + 1) * DK)
                                ins = nc.scalar.activation(old[:, k, cut], old[:, k, cut], ACT.Copy,
                                                           scale=w[:, k, D + HEADS + h:D + HEADS + h + 1])
                            ins.then_inc(old_scaled, 1)

            @block.vector
            def _(dve):
                ch = Chain(dve, chain_s)
                dve.sem_inc(written, S)
                dve.wait_ge(loaded, 96)
                dve.wait_ge(const, 1)
                ch.link(nc.vector.tensor_copy(spare[:], spare_i[:]))
                ch.link(nc.vector.tensor_copy(key[:], ends[:, 1]))
                for slot, e in ((0, 1), (1, 0)):
                    ch.link(nc.vector.tensor_scalar(tmp[:], ends[:, e], float(RELS), None, ALU.mult))
                    ch.link(nc.vector.tensor_tensor(tmp[:], tmp[:], ends[:, 2], ALU.add))
                    ch.link(nc.vector.tensor_copy(idx_all[:, :, slot], tmp[:]))
                ch.link(nc.vector.tensor_copy(idx_all[:, :, 2], ends[:, 1]))

                def heads(ap):
                    return ap.rearrange("p (h f) -> p h f", h=HEADS)

                dve.sem_inc(keys_ready, 1)

                def indices(b, n, k):
                    c = n * S + k
                    nc.vector.tensor_copy(idx[:, b, k], idx_all[:, ds(c, 1), :].rearrange("p a c -> p (a c)")
                                          ).then_inc(idx_ready, 1)

                for b in range(2):
                    for k in range(S):
                        indices(b, b, k)

                with dve.Fori(0, GR // 2) as g:
                    ch.loop(g, 2 * 9 * S)
                    for b in range(2):
                        n = g * 2 + b
                        for k in range(S):
                            c = n * S + k
                            kn = key[:, ds(c, 1)]
                            dve.wait_ge(key_rows, c + 1)
                            nc.vector.scalar_tensor_tensor(out=low[:, k], in0=pk[:, k, 0:P], scalar=kn, in1=R.lower[:],
                                                           op0=ALU.is_equal, op1=ALU.mult,
                                                           accum_out=before[:, k:k + 1])
                            ch.link(nc.vector.tensor_scalar(eq[:, k], pk[:, k, 0:P], kn, None, ALU.is_equal))
                            dve.sem_inc(eq_ready, 1)
                            ch.link(nc.vector.tensor_scalar(before[:, k:k + 1], before[:, k:k + 1], 0.5, None,
                                                            ALU.is_lt))
                            ch.link(nc.vector.scalar_tensor_tensor(out=before[:, k:k + 1], in0=kn, scalar=spare[:],
                                                                   in1=before[:, k:k + 1], op0=ALU.subtract,
                                                                   op1=ALU.mult))
                            dve.wait_ge(rows_gathered[b][k], g * 32 + 32)
                            ch.link(nc.vector.tensor_tensor(prod[:, k], q[:, b, k], vk[:, b, k, D:2 * D], ALU.mult))
                            nc.vector.tensor_reduce(score[:, k], heads(prod[:, k]), AX_X, ALU.add
                                                    ).then_inc(score_ready, 1)
                        for k in range(S):
                            c = n * S + k
                            dve.wait_ge(neg_ready, c + 1)
                            dve.wait_ge(score_rows, c + 1)
                            ch.link(nc.vector.tensor_tensor(msk[:, k], pr[:, k].rearrange("p (h n) -> p h n", h=HEADS),
                                                            neg[:, k:k + 1, :].to_broadcast([P, HEADS, P]), ALU.add))
                            ch.link(nc.vector.tensor_reduce(top[:, k], msk[:, k], AX_X, ALU.max))
                        for k in range(S):
                            c = n * S + k
                            dve.wait_ge(written, c + 1)
                            nc.vector.tensor_scalar(widx[:, k:k + 1], before[:, k:k + 1], spare[:], None, ALU.add)
                            dve.wait_ge(old_gathered[k], n * 16 + 16)
                            mo, mn = old[:, k, D + HEADS:ROW], new[:, k, D + HEADS:ROW]
                            ch.link(nc.vector.tensor_tensor(mn, top[:, k], mo, ALU.max))
                            nc.vector.tensor_tensor(ex[:, k, 0:HEADS], score[:, k], mn, ALU.subtract)
                            nc.vector.tensor_tensor(ex[:, k, HEADS:2 * HEADS], mo, mn, ALU.subtract
                                                    ).then_inc(ex_ready, 1)
                            indices(b, n + 2, k)
                        for k in range(S):
                            c = n * S + k
                            dve.wait_ge(w_ready, c + 1)
                            nc.vector.tensor_tensor(heads(w[:, k, 0:D]), heads(vk[:, b, k, 0:D]),
                                                    w[:, k, D:D + HEADS].unsqueeze(2).to_broadcast([P, HEADS, DK]),
                                                    ALU.mult).then_inc(weighted, 1)
                            fac = w[:, k, D + HEADS:ROW]
                            ch.link(nc.vector.tensor_tensor(old[:, k, D:D + HEADS], old[:, k, D:D + HEADS], fac,
                                                            ALU.mult))
                        for k in range(S):
                            c = n * S + k
                            dve.wait_ge(old_scaled, c + 1)
                            dve.wait_ge(summed, c + 1)
                            ch.link(nc.vector.tensor_tensor(new[:, k, 0:D + HEADS], old[:, k, 0:D + HEADS],
                                                            pk[:, k, P:P + D + HEADS], ALU.add))
                            dve.sem_inc(new_ready, 1)
                ch.end(GR // 2)


def merge_sums(nc, R, name, sums):
    S = STREAMS
    with Stage(nc, name) as st:
        a = st.sb("sums", [P, T, S, ROW])
        m = st.sb("max", [P, T, HEADS])
        ex = st.sb("factor", [P, T, S, HEADS])
        loaded = st.sem("sums_loaded")
        chain_s = st.sem("dve_chain")
        ready = st.sem("exponents_ready")
        exp_ready = st.sem("factors_ready")
        with st.block() as block:
            @block.sync
            def _(sp):
                for k in range(S):
                    sp.dma_start(a[:, :, k, :], sums[k][0:NP, :].rearrange("(t p) c -> p t c", p=P)
                                 ).then_inc(loaded, 16)

            @block.scalar
            def _(act):
                act.wait_ge(ready, 1)
                nc.scalar.activation(ex[:], ex[:], ACT.Exp).then_inc(exp_ready, 1)

            @block.vector
            def _(dve):
                ch = Chain(dve, chain_s)
                dve.wait_ge(loaded, 16 * S)
                mk = [a[:, :, k, D + HEADS:ROW] for k in range(S)]
                ch.link(nc.vector.tensor_tensor(m[:], mk[0], mk[1], ALU.max))
                for k in range(2, S):
                    ch.link(nc.vector.tensor_tensor(m[:], m[:], mk[k], ALU.max))
                for k in range(S):
                    ins = nc.vector.tensor_tensor(ex[:, :, k], mk[k], m[:], ALU.subtract)
                ins.then_inc(ready, 1)
                dve.wait_ge(exp_ready, 1)
                for k in range(S):
                    acc = a[:, :, k, 0:D].rearrange("p t (h f) -> p t h f", h=HEADS)
                    nc.vector.tensor_tensor(acc, acc, ex[:, :, k].unsqueeze(3).to_broadcast([P, T, HEADS, DK]),
                                            ALU.mult)
                    ins = nc.vector.tensor_tensor(a[:, :, k, D:D + HEADS], a[:, :, k, D:D + HEADS], ex[:, :, k],
                                                  ALU.mult)
                ch.link(ins)
                for k in range(1, S):
                    ch.link(nc.vector.tensor_tensor(a[:, :, 0, 0:D + HEADS], a[:, :, 0, 0:D + HEADS],
                                                    a[:, :, k, 0:D + HEADS], ALU.add))
                ch.link(nc.vector.tensor_scalar(m[:], a[:, :, 0, D:D + HEADS], 1e-30, None, ALU.max))
                ch.link(nc.vector.reciprocal(m[:], m[:]))
                ch.link(nc.vector.tensor_tensor(R.xn[:].rearrange("p t (h f) -> p t h f", h=HEADS),
                                                a[:, :, 0, 0:D].rearrange("p t (h f) -> p t h f", h=HEADS),
                                                m[:, :, :].unsqueeze(3).to_broadcast([P, T, HEADS, DK]), ALU.mult))


def l0_gnn(nc, R, A, edges, routes):
    class S:
        pass
    qtab = nc.dram_tensor("hgt_q", [NP * RELS, D], F32).ap()
    vktab = nc.dram_tensor("hgt_vk", [NP * RELS, 2 * D], F32).ap()
    sums = [nc.dram_tensor(f"hgt_sums{k}", [NP + P, ROW], F32).ap() for k in range(STREAMS)]
    with ExitStack() as ctx:
        S.oh = ctx.enter_context(nc.sbuf_tensor("l0g_types", [P, T, NT], F32))
        S.ohg = ctx.enter_context(nc.sbuf_tensor("l0g_types_gated", [P, T, NT], F32))
        node_types(nc, R, "l0g_nt", A["node_type_4"], A["L0_gnn_skip"], S)
        layernorm_T(nc, R, "l0g_ln", R.x)
        with nc.sbuf_tensor("l0g_k", [P, T, D], F32) as kn, nc.sbuf_tensor("l0g_v", [P, T, D], F32) as vn:
            typed_project(nc, R, "l0g_kp", A["L0_gnn_k_linears"], S.oh, kn, False)
            typed_project(nc, R, "l0g_vp", A["L0_gnn_v_linears"], S.oh, vn, False)
            typed_project(nc, R, "l0g_qp", A["L0_gnn_q_linears"], S.oh, R.xn, False, clear=routes)
            layernorm_T(nc, R, "l0g_qT", R.xn, norm=False)
            relation_table(nc, R, "l0g_qr", A["L0_gnn_relation_att"], A["L0_gnn_relation_pri"], None, qtab)
            layernorm_T(nc, R, "l0g_vT", vn, norm=False)
            relation_table(nc, R, "l0g_vr", A["L0_gnn_relation_msg"], A["L0_gnn_relation_pri"], kn, vktab)
        clear_sums(nc, R, "l0g_clear", sums)
        edge_sums(nc, R, "l0g_edges", A["src"], A["dst"], A["edge_type_8"], A["src"].shape[0], qtab, vktab, sums)
        merge_sums(nc, R, "l0g_merge", sums)
        layernorm_T(nc, R, "l0g_aT", R.xn, norm=False)
        typed_project(nc, R, "l0g_ap", A["L0_gnn_a_linears"], S.ohg, R.x, True, clear=edges)


def build(nc, A, out):
    class R:
        pass
    ctx = ExitStack()
    with ctx:
        def sb(name, shape, dt=F32):
            return ctx.enter_context(nc.sbuf_tensor(name, shape, dt))
        R.x = sb("x_all", [P, T, D])
        R.xn = sb("xn_all", [P, T, D])
        R.xt = sb("xt_all", [P, NC, NP])
        R.ident = sb("ident", [P, P])
        R.ones = sb("ones", [P, P])
        R.lower = sb("lower", [P, P])
        R.valid = sb("valid", [P, T])
        R.scores = sb("scores", [P, T, 16])
        R.gates = sb("gates", [P, T, 8])
        R.dis = sb("dis", [P, T])
        R.ad = sb("a_dst_all", [P, T + 1, HEADS])
        R.we = sb("gat_W", [P, NC, D + HEADS])
        setup(nc, R, A["x"])
        edges = nc.dram_tensor("edge_counts", [NP * NP + EdgeCounter.W * P, 1], F32).ap()
        routes = nc.dram_tensor("route_counts", [NP * NP + EdgeCounter.W * P, 1], F32).ap()
        l0_gnn(nc, R, A, edges, routes)
        l0_ffn(nc, R, A, edges)
        l1_gnn(nc, R, A, edges, routes)
        l1_ffn(nc, R, A)
        l2_gnn(nc, R, A, edges)
        l2_ffn(nc, R, A, routes)
        l3_gnn(nc, R, A, edges)
        l3_ffn(nc, R, A)
        store(nc, R, out)


_OUT = (N, D)


def kernel(**inputs):
    import numpy as _np
    import concourse.bacc as _bacc
    from concourse import mybir as _mybir
    from concourse.bass_utils import run_bass_kernel_spmd as _run

    nc = _bacc.Bacc("TRN2", target_bir_lowering=False, num_devices=1)
    arrays, args = {}, {}
    for name in inputs:
        a = _np.ascontiguousarray(inputs[name])
        arrays[f"in_{name}_dram"] = a
        args[name] = nc.dram_tensor(f"in_{name}_dram", a.shape, _mybir.dt.from_np(a.dtype), kind="ExternalInput").ap()
    out = nc.dram_tensor("out_0_dram", _OUT, F32, kind="ExternalOutput").ap()
    build(nc, args, out)
    r = _run(nc, [arrays], core_ids=[0])
    return r.results[0]["out_0_dram"]
```
